# Optimizing a Trainium2 kernel written in Bass

```python
import numpy as np
import jax
import jax.numpy as jnp

def _softmax(x, axis=-1):
    return jax.nn.softmax(x, axis=axis)

def _gelu(x):
    return jax.nn.gelu(x, approximate=True)

def _silu(x):
    return jax.nn.silu(x)

def _sigmoid(x):
    return jax.nn.sigmoid(x)

def _layernorm(x, axis=-1, eps=1e-05):
    m = jnp.mean(x, axis=axis, keepdims=True)
    v = jnp.var(x, axis=axis, keepdims=True)
    return (x - m) / jnp.sqrt(v + eps)

def _scatter_add(tgt, idx, src, axis=0):
    return tgt.at[idx].add(src)

def _segment_sum(src, seg, n):
    return jax.ops.segment_sum(src, seg, n)
kernel_name = 'mk_xattn_ffn_d2_seqx_r4_389cae'

def setup_inputs(seed: int=0):
    np.random.seed(seed)
    _w = jnp.asarray

    def _rec_inputs():
        import jax
        import jax.numpy as jnp
        _rk = jax.random.key(seed)
        x = -0.0002928 + 1 * jax.random.normal(jax.random.fold_in(_rk, 1), (4, 512, 256), jnp.float32)
        _lenS = 512 - jax.random.randint(jax.random.fold_in(_rk, 7), (4,), 0, max(1, 512 // 4) + 1, jnp.int32)
        _lenS2 = 512 - jax.random.randint(jax.random.fold_in(_rk, 8), (4,), 0, max(1, 512 // 4) + 1, jnp.int32)
        _ctx_1024P = jax.random.normal(jax.random.fold_in(_rk, 11), (4, 16, 256), jnp.float32)
        _ctx_1024c = jax.random.dirichlet(jax.random.fold_in(_rk, 511), 0.3 * jnp.ones((16,), jnp.float32), (4, 512))
        _ctx_1024t = jnp.einsum('bsk,bkd->bsd', _ctx_1024c, _ctx_1024P)
        _ctx_1024t = _ctx_1024t * jax.lax.rsqrt(jnp.mean(jnp.square(_ctx_1024t)) + 1e-12) * 0.953939
        ctx_1024 = -1.39393e-06 + 0.999914 * (_ctx_1024t + 0.3 * jax.random.normal(jax.random.fold_in(_rk, 611), (4, 512, 256), jnp.float32))
        return (x, ctx_1024)
    x, ctx_1024 = _rec_inputs()

    def _L0_xattn_setup():
        import jax, jax.numpy as jnp
        import numpy as np
        B, S, D, H, DH = (2, 512, 256, 16, 64)
        ATTN_SCALE = float(np.sqrt(DH))
        IGNORE = -100000.0
        key = jax.random.key(seed)
        ks = jax.random.split(key, 8)
        std = 0.02
        return {'query_input': jax.random.normal(ks[0], (B, S, D), jnp.float32), 'key_input': jax.random.normal(ks[1], (B, S, D), jnp.float32), 'value_input': jax.random.normal(ks[2], (B, S, D), jnp.float32), 'W_Q': jax.random.normal(ks[3], (H, D, DH), jnp.float32) * std, 'W_K': jax.random.normal(ks[4], (H, D, DH), jnp.float32) * std, 'W_V': jax.random.normal(ks[5], (H, D, DH), jnp.float32) * std, 'W_O': jax.random.normal(ks[6], (H, DH, D), jnp.float32) * std, 'b_Q': jnp.zeros((H, DH), jnp.float32), 'b_K': jnp.zeros((H, DH), jnp.float32), 'b_V': jnp.zeros((H, DH), jnp.float32), 'b_O': jnp.zeros((D,), jnp.float32)}
    _L0_xattn_all = _L0_xattn_setup()
    _L0_xattn_in = {k: v for k, v in _L0_xattn_all.items() if k in ('W_Q', 'W_K', 'W_V', 'W_O', 'b_Q', 'b_K', 'b_V', 'b_O')}
    del _L0_xattn_all

    def _L0_ffn_setup():
        import jax, jax.numpy as jnp
        import numpy as np
        TOP_K = 2
        LN_EPS = 1e-05
        B, S, H, E, F = (2, 512, 256, 8, 1024)

        def _layernorm(x, w, b):
            mu = jnp.mean(x, axis=-1, keepdims=True)
            var = jnp.mean(jnp.square(x - mu), axis=-1, keepdims=True)
            return (x - mu) * jax.lax.rsqrt(var + LN_EPS) * w + b
        key = jax.random.key(seed)
        ks = jax.random.split(key, 6)
        x = jax.random.normal(ks[0], (B, S, H), dtype=jnp.float32)
        Wg = jax.random.normal(ks[1], (H, E), dtype=jnp.float32) * 0.02
        alpha = jax.random.normal(ks[2], (E,), dtype=jnp.float32)
        ln_w = jnp.ones((E, H), dtype=jnp.float32)
        ln_b = jnp.zeros((E, H), dtype=jnp.float32)
        fc1_w = jax.random.normal(ks[3], (E, H, F), dtype=jnp.float32) * 0.02
        fc1_b = jnp.zeros((E, F), dtype=jnp.float32)
        fc2_w = jax.random.normal(ks[4], (E, F, H), dtype=jnp.float32) * 0.02
        fc2_b = jnp.zeros((E, H), dtype=jnp.float32)
        return {'x': x, 'Wg': Wg, 'alpha': alpha, 'ln_w': ln_w, 'ln_b': ln_b, 'fc1_w': fc1_w, 'fc1_b': fc1_b, 'fc2_w': fc2_w, 'fc2_b': fc2_b}
    _L0_ffn_all = _L0_ffn_setup()
    _L0_ffn_in = {k: v for k, v in _L0_ffn_all.items() if k in ('Wg', 'alpha', 'ln_w', 'ln_b', 'fc1_w', 'fc1_b', 'fc2_w', 'fc2_b')}
    del _L0_ffn_all

    def _L1_xattn_setup():
        import jax, jax.numpy as jnp
        import numpy as np
        B, S, D = (1, 1024, 256)
        NUM_HEADS, HEAD_DIM = (16, 64)
        WINDOW = 128
        EMBED = NUM_HEADS * HEAD_DIM
        key = jax.random.key(seed)
        ks = jax.random.split(key, 7)
        scale_in = 1.0 / np.sqrt(D)
        scale_e = 1.0 / np.sqrt(EMBED)
        return {'query': jax.random.normal(ks[0], (B, S, D), dtype=jnp.float32), 'key': jax.random.normal(ks[1], (B, S, D), dtype=jnp.float32), 'value': jax.random.normal(ks[2], (B, S, D), dtype=jnp.float32), 'Wq': jax.random.normal(ks[3], (D, EMBED), dtype=jnp.float32) * scale_in, 'Wk': jax.random.normal(ks[4], (D, EMBED), dtype=jnp.float32) * scale_in, 'Wv': jax.random.normal(ks[5], (D, EMBED), dtype=jnp.float32) * scale_in, 'Wo': jax.random.normal(ks[6], (EMBED, D), dtype=jnp.float32) * scale_e}
    _L1_xattn_all = _L1_xattn_setup()
    _L1_xattn_in = {k: v for k, v in _L1_xattn_all.items() if k in ('Wq', 'Wk', 'Wv', 'Wo')}
    del _L1_xattn_all

    def _L1_ffn_setup():
        import jax, jax.numpy as jnp
        import numpy as np
        B, T, D, H, R, N = (16, 256, 256, 64, 64, 8)
        key = jax.random.key(seed)
        ks = jax.random.split(key, 8)
        s = lambda k, shape, fan: jax.random.normal(k, shape, jnp.float32) / np.sqrt(fan)
        return {'x': jax.random.normal(ks[0], (B, T, D), jnp.float32), 'W_base': s(ks[1], (D, D), D), 'b_base': jnp.zeros((D,), jnp.float32), 'W_enc': s(ks[2], (N, D, H), D), 'b_enc': jnp.zeros((N, H), jnp.float32), 'W_dec': s(ks[3], (N, H, D), H), 'b_dec': jnp.zeros((N, D), jnp.float32), 'W_down': s(ks[4], (N, D, R), D), 'b_down': jnp.zeros((N, R), jnp.float32), 'W_up': s(ks[5], (N, R, D), R), 'b_up': jnp.zeros((N, D), jnp.float32), 'connected_idx': jnp.arange(N, dtype=jnp.int32)}
    _L1_ffn_all = _L1_ffn_setup()
    _L1_ffn_in = {k: v for k, v in _L1_ffn_all.items() if k in ('W_base', 'b_base', 'W_enc', 'b_enc', 'W_dec', 'b_dec', 'W_down', 'b_down', 'W_up', 'b_up', 'connected_idx')}
    del _L1_ffn_all
    return {'x': x, 'ctx_1024': ctx_1024, 'L0_xattn_W_Q': _L0_xattn_in['W_Q'], 'L0_xattn_W_K': _L0_xattn_in['W_K'], 'L0_xattn_W_V': _L0_xattn_in['W_V'], 'L0_xattn_W_O': _L0_xattn_in['W_O'], 'L0_xattn_b_Q': _L0_xattn_in['b_Q'], 'L0_xattn_b_K': _L0_xattn_in['b_K'], 'L0_xattn_b_V': _L0_xattn_in['b_V'], 'L0_xattn_b_O': _L0_xattn_in['b_O'], 'L0_ffn_Wg': _L0_ffn_in['Wg'], 'L0_ffn_alpha': _L0_ffn_in['alpha'], 'L0_ffn_ln_w': _L0_ffn_in['ln_w'], 'L0_ffn_ln_b': _L0_ffn_in['ln_b'], 'L0_ffn_fc1_w': _L0_ffn_in['fc1_w'], 'L0_ffn_fc1_b': _L0_ffn_in['fc1_b'], 'L0_ffn_fc2_w': _L0_ffn_in['fc2_w'], 'L0_ffn_fc2_b': _L0_ffn_in['fc2_b'], 'L1_xattn_Wq': _L1_xattn_in['Wq'], 'L1_xattn_Wk': _L1_xattn_in['Wk'], 'L1_xattn_Wv': _L1_xattn_in['Wv'], 'L1_xattn_Wo': _L1_xattn_in['Wo'], 'L1_ffn_W_base': _L1_ffn_in['W_base'], 'L1_ffn_b_base': _L1_ffn_in['b_base'], 'L1_ffn_W_enc': _L1_ffn_in['W_enc'], 'L1_ffn_b_enc': _L1_ffn_in['b_enc'], 'L1_ffn_W_dec': _L1_ffn_in['W_dec'], 'L1_ffn_b_dec': _L1_ffn_in['b_dec'], 'L1_ffn_W_down': _L1_ffn_in['W_down'], 'L1_ffn_b_down': _L1_ffn_in['b_down'], 'L1_ffn_W_up': _L1_ffn_in['W_up'], 'L1_ffn_b_up': _L1_ffn_in['b_up'], 'L1_ffn_connected_idx': _L1_ffn_in['connected_idx']}

def reference(x, ctx_1024, L0_xattn_W_Q, L0_xattn_W_K, L0_xattn_W_V, L0_xattn_W_O, L0_xattn_b_Q, L0_xattn_b_K, L0_xattn_b_V, L0_xattn_b_O, L0_ffn_Wg, L0_ffn_alpha, L0_ffn_ln_w, L0_ffn_ln_b, L0_ffn_fc1_w, L0_ffn_fc1_b, L0_ffn_fc2_w, L0_ffn_fc2_b, L1_xattn_Wq, L1_xattn_Wk, L1_xattn_Wv, L1_xattn_Wo, L1_ffn_W_base, L1_ffn_b_base, L1_ffn_W_enc, L1_ffn_b_enc, L1_ffn_W_dec, L1_ffn_b_dec, L1_ffn_W_down, L1_ffn_b_down, L1_ffn_W_up, L1_ffn_b_up, L1_ffn_connected_idx):
    import jax
    import jax.numpy as jnp

    def _L0_xattn_ref(query_input, key_input, value_input, W_Q, W_K, W_V, W_O, b_Q, b_K, b_V, b_O):
        import jax, jax.numpy as jnp
        import numpy as np
        B, S, D, H, DH = (2, 512, 256, 16, 64)
        ATTN_SCALE = float(np.sqrt(DH))
        IGNORE = -100000.0
        q = jnp.einsum('bpd,hde->bphe', query_input, W_Q) + b_Q
        k = jnp.einsum('bpd,hde->bphe', key_input, W_K) + b_K
        v = jnp.einsum('bpd,hde->bphe', value_input, W_V) + b_V
        attn_scores = jnp.einsum('bqhe,bkhe->bhqk', q, k) / ATTN_SCALE
        causal_mask = jnp.tril(jnp.ones((S, S), dtype=bool))
        attn_scores = jnp.where(causal_mask, attn_scores, IGNORE)
        pattern = jax.nn.softmax(attn_scores, axis=-1)
        z = jnp.einsum('bkhe,bhqk->bqhe', v, pattern)
        out = jnp.einsum('bphe,hed->bpd', z, W_O) + b_O
        return out

    def _L0_ffn_ref(x, Wg, alpha, ln_w, ln_b, fc1_w, fc1_b, fc2_w, fc2_b):
        import jax, jax.numpy as jnp
        import numpy as np
        TOP_K = 2
        LN_EPS = 1e-05
        B, S, H, E, F = (2, 512, 256, 8, 1024)

        def _layernorm(x, w, b):
            mu = jnp.mean(x, axis=-1, keepdims=True)
            var = jnp.mean(jnp.square(x - mu), axis=-1, keepdims=True)
            return (x - mu) * jax.lax.rsqrt(var + LN_EPS) * w + b
        b, s, h = x.shape
        xf = x.reshape(-1, h)
        logits = xf @ Wg
        top_vals, top_idx = jax.lax.top_k(logits, TOP_K)
        gate_score = jax.nn.softmax(top_vals, axis=-1)
        one_hot = jax.nn.one_hot(top_idx, Wg.shape[1], dtype=xf.dtype)
        comb = jnp.einsum('tke,tk->te', one_hot, gate_score) * alpha
        out = jnp.zeros_like(xf)
        for e in range(Wg.shape[1]):
            hdn = _layernorm(xf, ln_w[e], ln_b[e])
            a = jax.nn.gelu(hdn @ fc1_w[e] + fc1_b[e], approximate=True)
            y = a @ fc2_w[e] + fc2_b[e]
            out = out + y * comb[:, e:e + 1]
        return out.reshape(b, s, h)

    def _L1_xattn_ref(query, key, value, Wq, Wk, Wv, Wo):
        import jax, jax.numpy as jnp
        import numpy as np
        B, S, D = (1, 1024, 256)
        NUM_HEADS, HEAD_DIM = (16, 64)
        WINDOW = 128
        EMBED = NUM_HEADS * HEAD_DIM
        Bq, Sq, _ = query.shape
        q = (query @ Wq).reshape(Bq, Sq, NUM_HEADS, HEAD_DIM).transpose(0, 2, 1, 3)
        k = (key @ Wk).reshape(Bq, Sq, NUM_HEADS, HEAD_DIM).transpose(0, 2, 1, 3)
        v = (value @ Wv).reshape(Bq, Sq, NUM_HEADS, HEAD_DIM).transpose(0, 2, 1, 3)
        idx = jnp.arange(Sq)
        local_mask = jnp.abs(idx[:, None] - idx[None, :]) > WINDOW
        scores = jnp.einsum('bhqd,bhkd->bhqk', q, k) / jnp.sqrt(jnp.float32(HEAD_DIM))
        scores = jnp.where(local_mask, -jnp.inf, scores)
        attn = jax.nn.softmax(scores, axis=-1)
        out = jnp.einsum('bhqk,bhkd->bhqd', attn, v)
        out = out.transpose(0, 2, 1, 3).reshape(Bq, Sq, EMBED)
        return out @ Wo

    def _L1_ffn_ref(x, W_base, b_base, W_enc, b_enc, W_dec, b_dec, W_down, b_down, W_up, b_up, connected_idx):
        import jax, jax.numpy as jnp
        import numpy as np
        B, T, D, H, R, N = (16, 256, 256, 64, 64, 8)
        base = jnp.einsum('btd,de->bte', x, W_base) + b_base
        h = jax.nn.relu(jnp.einsum('btd,ndh->nbth', x, W_enc) + b_enc[:, None, None, :])
        recon = jnp.einsum('nbth,nhd->nbtd', h, W_dec) + b_dec[:, None, None, :]
        losses = jnp.mean((recon - x[None]) ** 2, axis=(2, 3))
        top1 = jnp.argmin(losses, axis=0)
        adp = connected_idx[top1]
        Wd, bd = (W_down[adp], b_down[adp])
        Wu, bu = (W_up[adp], b_up[adp])
        mid = jax.nn.relu(jnp.einsum('btd,bdr->btr', x, Wd) + bd[:, None, :])
        adapter_out = jnp.einsum('btr,brd->btd', mid, Wu) + bu[:, None, :]
        return base + adapter_out
    x = x + _L0_xattn_ref(_layernorm(x, axis=-1), ctx_1024, ctx_1024, L0_xattn_W_Q, L0_xattn_W_K, L0_xattn_W_V, L0_xattn_W_O, L0_xattn_b_Q, L0_xattn_b_K, L0_xattn_b_V, L0_xattn_b_O)
    x = x + _L0_ffn_ref(_layernorm(x, axis=-1), L0_ffn_Wg, L0_ffn_alpha, L0_ffn_ln_w, L0_ffn_ln_b, L0_ffn_fc1_w, L0_ffn_fc1_b, L0_ffn_fc2_w, L0_ffn_fc2_b)
    x = x + _L1_xattn_ref(_layernorm(x, axis=-1), ctx_1024, ctx_1024, L1_xattn_Wq, L1_xattn_Wk, L1_xattn_Wv, L1_xattn_Wo)
    x = x + _L1_ffn_ref(_layernorm(x, axis=-1), L1_ffn_W_base, L1_ffn_b_base, L1_ffn_W_enc, L1_ffn_b_enc, L1_ffn_W_dec, L1_ffn_b_dec, L1_ffn_W_down, L1_ffn_b_down, L1_ffn_W_up, L1_ffn_b_up, L1_ffn_connected_idx)
    return x

_drawn_inputs = setup_inputs


def setup_inputs(seed=0):
    import zlib

    import numpy as np

    out = dict(_drawn_inputs(seed))
    spreads = {'L0_xattn_b_Q': (0.0, 0.8),
     'L0_xattn_b_K': (0.0, 0.8),
     'L0_xattn_b_V': (0.0, 0.1),
     'L0_xattn_b_O': (0.0, 0.1),
     'L0_ffn_ln_w': (1.0, 0.6),
     'L0_ffn_ln_b': (0.0, 0.8),
     'L0_ffn_fc1_b': (0.0, 0.422),
     'L0_ffn_fc2_b': (0.0, 0.1),
     'L1_ffn_b_base': (0.0, 0.1),
     'L1_ffn_b_enc': (0.0, 0.1),
     'L1_ffn_b_dec': (0.0, 0.1),
     'L1_ffn_b_down': (0.0, 0.1),
     'L1_ffn_b_up': (0.0, 0.1)}
    factors = {'L0_xattn_W_Q': 8.0, 'L0_xattn_W_K': 8.0}
    for name, (base, spread) in spreads.items():
        noise = np.random.default_rng([zlib.crc32(name.encode()), seed]).standard_normal(out[name].shape)
        drawn = base * np.exp(spread * noise) if base else spread * noise
        out[name] = jnp.asarray(drawn.astype(out[name].dtype))
    for name, factor in factors.items():
        out[name] = (out[name] * factor).astype(out[name].dtype)
    return out
```

```python
from contextlib import ExitStack, contextmanager

import concourse.bass as bass
from concourse import mybir

F32 = mybir.dt.float32
F32R = mybir.dt.float32r
BF16 = mybir.dt.bfloat16
ALU = mybir.AluOpType
ACT = mybir.ActivationFunctionType
AX = mybir.AxisListType

P = 128
D = 256
KD = D // P
B = 4
S = 512
TOK = B * S
NT = TOK // P
TPB = S // P
H = 16
DH = 64
NP = H // 2
LN_EPS = 1e-5
Q_SCALE = DH ** -0.5
MASKED = -(2.0 ** 100)
LOW, UP = 0, 1
E = 8
F = 1024
NF = F // P
BANK = 512


def ge(eng, sem, count):
    if isinstance(count, int) and count <= 0:
        return
    eng.wait_ge(sem, count)


def as_f32(ap):
    return ap.bitcast(F32)


@contextmanager
def cleared_semaphores(nc):
    made = []

    def make(name):
        made.append(nc.alloc_semaphore(name))
        return made[-1]

    yield make
    nc.clear_and_free_semaphores(made)
    nc.all_engine_barrier()


class Shared:

    def __init__(self, sb):
        self.x = sb("x_sb", [P, NT, D], F32)
        self.uT_hi, self.uT_lo = sb("uT_hi", [P, KD, TOK], F32R), sb("uT_lo", [P, KD, TOK], F32R)
        self.cT_hi, self.cT_lo = sb("cT_hi", [P, KD, TOK], F32R), sb("cT_lo", [P, KD, TOK], F32R)
        self.ident, self.one = sb("ident", [P, P], F32), sb("one", [P, P], F32)
        self.masks = sb("masks", [P, 2, P], F32)
        self.consts = sb("consts", [P, 2], F32)


class Gates:

    def __init__(self, sb):
        self.columns = sb("g_columns", [P, E * NF + 2 * E * KD], F32)
        self.comb, self.comb_e = sb("g_comb", [P, NT, E], F32), sb("g_comb_e", [P, E, NT], F32)
        self.fc1b = self.columns[:, 0:E * NF]
        self.lnw = self.columns[:, E * NF:E * NF + E * KD]
        self.lnb = self.columns[:, E * NF + E * KD:E * NF + 2 * E * KD]


class Statistics:

    def __init__(self, sb, name):
        self.bn, self.mv = sb(name + "_bn", [P, NT, 6], F32), sb(name + "_mv", [P, NT, 2], F32)
        self.veps, self.sd, self.r0 = (sb(name + n, [P, NT], F32) for n in ("_veps", "_sd", "_r0"))
        self.t1, self.t2, self.t3 = (sb(name + n, [P, NT], F32) for n in ("_t1", "_t2", "_t3"))
        self.rstd = sb(name + "_rstd", [P, NT], F32)


class Chain:

    def __init__(self, eng, sem):
        self.eng, self.sem, self.count = eng, sem, 0

    def inc(self, instruction):
        self.count += 1
        instruction.then_inc(self.sem, 1)

    def wait(self):
        self.eng.wait_ge(self.sem, self.count)


def norm_rows(dve, chain, src, dst, st, stats_to_act, act_sqrt_done):
    for t in range(NT):
        chain.inc(dve.bn_stats(st.bn[:, t, :], src[:, t, :]))
    chain.wait()
    for t in range(NT):
        chain.inc(dve.bn_aggr(st.mv[:, t, :], st.bn[:, t, :]))
    chain.wait()
    dve.tensor_scalar(st.veps[:, :], st.mv[:, :, 1], LN_EPS, None, ALU.add).then_inc(stats_to_act, 1)
    dve.wait_ge(act_sqrt_done, 1)
    chain.inc(dve.reciprocal(st.r0[:, :], st.sd[:, :]))
    chain.wait()
    chain.inc(dve.tensor_tensor(st.t1[:, :], st.r0[:, :], st.r0[:, :], ALU.mult))
    chain.wait()
    chain.inc(dve.tensor_tensor(st.t2[:, :], st.t1[:, :], st.veps[:, :], ALU.mult))
    chain.wait()
    chain.inc(dve.tensor_scalar(st.t3[:, :], st.t2[:, :], -0.5, 1.5, ALU.mult, ALU.add))
    chain.wait()
    chain.inc(dve.tensor_tensor(st.rstd[:, :], st.r0[:, :], st.t3[:, :], ALU.mult))
    chain.wait()
    for t in range(NT):
        chain.inc(dve.tensor_scalar(dst[:, t, :], src[:, t, :], st.mv[:, t, 0:1], st.rstd[:, t:t + 1],
                                    ALU.subtract, ALU.mult))


def attention_inputs(nc, m, tag, x_dram, ctx_dram, bo_dram, uT32=None):
    with ExitStack() as ctx:
        sb = lambda n, s, d: ctx.enter_context(nc.sbuf_tensor(f"{tag}_{n}", s, d))
        make = ctx.enter_context(cleared_semaphores(nc))
        sem = lambda n: make(f"{tag}_{n}")
        first = x_dram is not None
        st = Statistics(sb, "st")
        u = sb("u", [P, NT, D], F32)
        c = sb("c", [P, NT, D], F32) if first else None
        bo = sb("bo", [P, D], F32) if first else None
        banks = [ctx.enter_context(nc.psum_tensor(f"{tag}_ps{i}", [P, BANK], F32)) for i in range(4)]
        x_loaded, bo_loaded = sem("x_loaded"), sem("bo_loaded")
        c_loaded = [sem(f"c_loaded{b}") for b in range(B)]
        const_step, const_ready = sem("const_step"), sem("const_ready")
        dve_step, var_ready, sqrt_ready = sem("dve_step"), sem("var_ready"), sem("sqrt_ready")
        u_ready, turned, hi_ready, lo_ready = sem("u_ready"), sem("turned"), sem("hi_ready"), sem("lo_ready")
        bo_added, f32_ready = sem("bo_added"), sem("f32_ready")

        jobs = ([(c, m.cT_hi, m.cT_lo, g) for g in range(NT // 2)] if first else []) + \
               [(u, m.uT_hi, m.uT_lo, g) for g in range(NT // 2)]
        n_c = len(jobs) - NT // 2

        with nc.Block() as block:
            @block.sync
            def _(sp):
                if first:
                    for b in range(B):
                        rows = slice(b * S, (b + 1) * S)
                        sp.dma_start(m.x[:, TPB * b:TPB * b + TPB, :],
                                     x_dram[rows, :].rearrange("(t p) d -> p t d", p=P)).then_inc(x_loaded, 16)
                    sp.dma_start(bo[:, :], bo_dram.rearrange("(a n) -> a n", a=1).to_broadcast([P, D])) \
                        .then_inc(bo_loaded, 16)

            @block.gpsimd
            def _(pool):
                if first:
                    make_constants(pool, m, const_step, const_ready)
                    pool.wait_ge(bo_loaded, 16)
                    pool.wait_ge(u_ready, 1)
                    for t in range(NT):
                        pool.tensor_tensor(m.x[:, t, :], m.x[:, t, :], bo[:, :], ALU.add).then_inc(bo_added, 1)

            @block.scalar
            def _(act):
                if first:
                    for b in range(B):
                        rows = slice(b * S, (b + 1) * S)
                        act.dma_start(c[:, TPB * b:TPB * b + TPB, :],
                                      ctx_dram[rows, :].rearrange("(t p) d -> p t d", p=P)).then_inc(c_loaded[b], 16)
                act.wait_ge(var_ready, 1)
                act.activation(st.sd[:, :], st.veps[:, :], ACT.Sqrt).then_inc(sqrt_ready, 1)
                for n, (_, hi, lo, g) in enumerate(jobs):
                    act.wait_ge(turned, n + 1)
                    act.activation(hi[:, :, 2 * P * g:2 * P * (g + 1)],
                                   banks[n % 4][:, :].rearrange("p (k t) -> p k t", k=KD), ACT.Copy) \
                        .then_inc(hi_ready, 1)
                    if uT32 is not None:
                        act.activation(uT32[:, :, 2 * P * g:2 * P * (g + 1)],
                                       banks[n % 4][:, :].rearrange("p (k t) -> p k t", k=KD), ACT.Copy) \
                            .then_inc(f32_ready, 1)

            @block.vector
            def _(dve):
                chain = Chain(dve, dve_step)
                if first:
                    dve.wait_ge(x_loaded, 16 * B)
                norm_rows(dve, chain, m.x, u, st, var_ready, sqrt_ready)
                chain.wait()
                dve.tensor_copy(st.t1[:, :], st.rstd[:, :]).then_inc(u_ready, 1)
                for n, (_, hi, lo, g) in enumerate(jobs):
                    dve.wait_ge(hi_ready, n + 1)
                    if uT32 is not None:
                        dve.wait_ge(f32_ready, n + 1)
                    cols = slice(2 * P * g, 2 * P * (g + 1))
                    dve.tensor_tensor(lo[:, :, cols], banks[n % 4][:, :].rearrange("p (k t) -> p k t", k=KD),
                                      as_f32(hi[:, :, cols]), ALU.subtract).then_inc(lo_ready, 1)

            @block.tensor
            def _(pe):
                if first:
                    pe.wait_ge(const_ready, 1)
                for n, (src, _, _, g) in enumerate(jobs):
                    if n < n_c:
                        pe.wait_ge(c_loaded[g // 2], 16)
                    else:
                        pe.wait_ge(u_ready, 1)
                    if n >= 4:
                        pe.wait_ge(lo_ready, n - 3)
                        if uT32 is not None:
                            pe.wait_ge(f32_ready, n - 3)
                    for k in range(KD):
                        for j in range(2):
                            last = pe.transpose(banks[n % 4][:, (2 * k + j) * P:(2 * k + j + 1) * P],
                                                src[:, 2 * g + j, k * P:(k + 1) * P], m.ident[:, :])
                    last.then_inc(turned, 1)


def make_constants(pool, m, step, ready):
    pool.memset(m.ident[:, :], 0.0).then_inc(step, 1)
    pool.memset(m.masks[:, :, :], 0.0).then_inc(step, 1)
    pool.memset(m.consts[:, 0:1], 1.0).then_inc(step, 1)
    pool.memset(m.consts[:, 1:2], Q_SCALE).then_inc(step, 1)
    n = 4
    for tile, q_step, k_step, compare, fill in (
            (m.ident[:, :], 1, -1, ALU.not_equal, 1.0),
            (m.masks[:, LOW, :], -1, 1, ALU.is_ge, MASKED),
            (m.masks[:, UP, :], 1, -1, ALU.is_ge, MASKED)):
        pool.wait_ge(step, n)
        pool.affine_select(out=tile, in_=tile, compare_op=compare, fill=fill, base=0, pattern=[[k_step, P]],
                           channel_multiplier=q_step).then_inc(step, 1)
        n += 1
    pool.wait_ge(step, n)
    pool.memset(m.one[:, :], 1.0).then_inc(ready, 1)


def attention(nc, m, tag, wq, wk, wv, wo, bq, bk, bv, blocks_of):
    biased = bq is not None
    seen = [blocks_of(j) for j in range(TPB)]
    first_key = [s[0][0] for s in seen]
    width = [P * len(s) for s in seen]
    place = list(range(TPB))[::-1]
    turns = []
    for i in range(TPB):
        turns += [(i, (0, 1))] if 2 * width[place[i]] <= BANK else [(i, (0,)), (i, (1,))]
    t_of = [[q for q, (ii, _) in enumerate(turns) if ii == i] for i in range(TPB)]
    NTURN = len(turns)
    narrow_first = len(t_of[0]) < len(t_of[1])
    order = [("S", 0), ("Q", 0), ("S", 1), ("K", 0), ("PVB", 0)] + [("T", q) for q in t_of[0]] + \
            [("S", 2), ("S", 3)] + [("T", q) for q in t_of[1]] + \
            [("VT", 0), ("O", 0), ("O", 1), ("VR", 0), ("PVA", 0)] + [("T", q) for q in t_of[2] + t_of[3]]
    ring_jobs = [o for o in order if o[0] in ("Q", "K", "VT", "VR", "T", "O")]
    RING = 3
    assert len(ring_jobs) % RING == 0
    next_item, ends_before = ("Q", "K", "VT", "VR"), ("PVB", "O")

    with ExitStack() as ctx:
        sb = lambda n, s, d: ctx.enter_context(nc.sbuf_tensor(f"{tag}_{n}", s, d))
        make = ctx.enter_context(cleared_semaphores(nc))
        sem = lambda n: make(f"{tag}_{n}")
        w_stage = sb("w_stage", [P, 3, KD, P], F32)
        wo_stage = sb("wo_stage", [P, D], F32)
        b_stage = sb("b_stage", [P, 3], F32)
        w_hi, w_lo = sb("w_hi", [P, 3, KD, P], F32R), sb("w_lo", [P, 3, KD, P], F32R)
        wo_hi, wo_lo = sb("wo_hi", [P, D], F32R), sb("wo_lo", [P, D], F32R)
        bqk, bvz = sb("bqk", [P, 2], F32), sb("bvz", [P, 1], F32)
        q_hi, q_lo = sb("q_hi", [P, 2, S], F32R), sb("q_lo", [P, 2, S], F32R)
        k_hi, k_lo = sb("k_hi", [P, 2, S], F32R), sb("k_lo", [P, 2, S], F32R)
        vT = sb("vT", [P, S], F32)
        v_hi, v_lo = sb("v_hi", [P, 2, TPB, 3, DH], F32R), sb("v_lo", [P, 2, TPB, 3, DH], F32R)
        probs = sb("probs", [P, TPB, 2, S], F32)
        negmax, sums, rsum = sb("negmax", [P, TPB, 2], F32), sb("sums", [P, TPB, 2], F32), sb("rsum", [P, TPB, 2], F32)
        pT_hi, pT_lo = (sb(n, [P, 2, 2, TPB, 2 * P], F32R) for n in ("pT_hi", "pT_lo"))
        z_hi, z_lo = sb("z_hi", [P, S], F32R), sb("z_lo", [P, S], F32R)
        o_sb = sb("o_sb", [P, 2, BANK], F32)
        s_ps = [ctx.enter_context(nc.psum_tensor(f"{tag}_s{i}", [P, 2, BANK], F32)) for i in range(2)]
        ring = [ctx.enter_context(nc.psum_tensor(f"{tag}_ring{i}", [P, BANK], F32)) for i in range(RING)]
        z_ps = ctx.enter_context(nc.psum_tensor(f"{tag}_z", [P, BANK], F32))

        w_loaded, wo_loaded, b_loaded = sem("w_loaded"), sem("wo_loaded"), sem("b_loaded")
        w_step, w_ready, wo_step, wo_ready = sem("w_step"), sem("w_ready"), sem("wo_step"), sem("wo_ready")
        bqk_ready, bvz_ready, zeroed, o_read = sem("bqk_ready"), sem("bvz_ready"), sem("zeroed"), sem("o_read")
        s_done, q_done, k_done, vt_done, vr_done = sem("s_done"), sem("q_done"), sem("k_done"), sem("vt_done"), sem("vr_done")
        t_done, pva_done, pvb_done, o_done = sem("t_done"), sem("pva_done"), sem("pvb_done"), sem("o_done")
        max_ready, exp_ready, rsum_ready, norm_ready = sem("max_ready"), sem("exp_ready"), sem("rsum_ready"), sem("norm_ready")
        masked, norm0_ready = sem("masked"), sem("norm0_ready")
        q_hi_ready, k_hi_ready, vT_ready, v_hi_ready = sem("q_hi_ready"), sem("k_hi_ready"), sem("vT_ready"), sem("v_hi_ready")
        q_ready, k_ready, v_ready = sem("q_ready"), sem("k_ready"), sem("v_ready")
        pT_hi_ready, pT_ready, z_hi_ready, z_ready, x_added = \
            sem("pT_hi_ready"), sem("pT_ready"), sem("z_hi_ready"), sem("z_ready"), sem("x_added")

        def per_item(p, b, n, c):
            return p * (B * n) + (b * n + c)

        def ran(kind, p, b):
            if isinstance(p, int):
                it = B * p + b
                if it < 0:
                    return kind in next_item
                if it == 0:
                    return kind not in ends_before
                if it == B * NP - 1:
                    return kind not in next_item
                if it == B * NP:
                    return kind in ends_before
            return True

        def bank_of(kind, q):
            return ring[ring_jobs.index((kind, q)) % RING]

        def wait_bank_free(pe, kind, q, p, b):
            k, bb = ring_jobs.index((kind, q)), b
            while True:
                k -= RING
                if k < 0:
                    k, bb = k + len(ring_jobs), bb - 1
                if isinstance(p, int) and B * p + bb < -1:
                    return
                kk, qq = ring_jobs[k]
                if ran(kk, p, bb):
                    break
            sem, n, c = {"Q": (q_ready, 1, 2), "K": (k_ready, 1, 2), "VT": (vT_ready, 1, 2), "VR": (v_ready, 1, 2),
                         "T": (pT_ready, NTURN, qq + 1), "O": (o_read, 2, qq - 1)}[kk]
            pe.wait_ge(sem, per_item(p, bb, n, c))

        def turned_from(q):
            i, hs = turns[q]
            j = place[i]
            return bank_of("T", q)[:, 0:width[j] * len(hs)].rearrange(
                "p (h t n) -> p h t n", h=len(hs), n=P)

        def turned_into(half, q):
            i, hs = turns[q]
            j = place[i]
            k0, n = first_key[j], width[j] // P
            return half[:, j // 2, hs[0]:hs[-1] + 1, k0:k0 + n, P * (j % 2):P * (j % 2) + P]

        nd = 2 if biased else 1

        with nc.Block() as block:
            @block.sync
            def _(sp):
                def load(p):
                    for i, w in enumerate((wq, wk, wv)):
                        for dst, src in w(w_stage[:, i, :, :], p):
                            sp.dma_start(dst, src).then_inc(w_loaded, 16)
                    sp.dma_start(wo_stage[:, :], wo(p)).then_inc(wo_loaded, 16)
                    if biased:
                        for i, bias in enumerate((bq, bk, bv)):
                            sp.dma_start(b_stage[:, i:i + 1], bias(p)).then_inc(b_loaded, 16)

                load(0)
                with sp.Fori(1, NP) as p:
                    sp.wait_ge(wo_ready, p * 1)
                    if biased:
                        sp.wait_ge(bvz_ready, p * 1)
                    load(p)

            @block.gpsimd
            def _(pool):
                for half in (v_hi, v_lo):
                    for i in range(2):
                        pool.memset(as_f32(half[:, i, :, 1, :]), 0.0).then_inc(zeroed, 1)

                one, scale = (m.consts[:, i:i + 1] for i in range(2))

                def split_w(i, p):
                    done = {0: q_done, 1: k_done, 2: vt_done}[i]
                    if i == 0:
                        pool.wait_ge(w_loaded, p * (16 * 3 * nd) + 16 * 3 * nd)
                    ge(pool, done, per_item(p, 0, 1, 0))
                    w = w_stage[:, i, :, :].rearrange("p k n -> p (k n)")
                    hi, lo = (half[:, i, :, :].rearrange("p k n -> p (k n)") for half in (w_hi, w_lo))
                    steps = p * 4 + (i + 1 if i else 0)
                    if i == 0:
                        pool.tensor_tensor(w, w, scale.to_broadcast([P, KD * P]), ALU.mult).then_inc(w_step, 1)
                        pool.wait_ge(w_step, steps + 1)
                        steps = steps + 1
                    pool.tensor_tensor(hi, w, one.to_broadcast([P, KD * P]), ALU.mult).then_inc(w_step, 1)
                    pool.wait_ge(w_step, steps + 1)
                    pool.tensor_tensor(lo, w, as_f32(hi), ALU.subtract).then_inc(w_ready, 1)

                def split_wo(p):
                    pool.wait_ge(wo_loaded, p * 16 + 16)
                    ge(pool, o_done, per_item(p, 0, 2, 0))
                    pool.tensor_tensor(wo_hi[:, :], wo_stage[:, :], one.to_broadcast([P, D]), ALU.mult).then_inc(wo_step, 1)
                    pool.wait_ge(wo_step, p * 1 + 1)
                    pool.tensor_tensor(wo_lo[:, :], wo_stage[:, :], as_f32(wo_hi[:, :]), ALU.subtract).then_inc(wo_ready, 1)

                def norm_of(i, p, b):
                    j = place[i]
                    pool.wait_ge(rsum_ready, per_item(p, b, TPB, i + 1))
                    for h in range(2):
                        tile = probs[:, j, h, 0:width[j]]
                        pool.tensor_tensor(tile, tile, rsum[:, j, h:h + 1].to_broadcast([P, width[j]]), ALU.mult) \
                            .then_inc(norm_ready, 1)

                def x_of(a, p, b):
                    pool.wait_ge(o_read, per_item(p, b, 2, a - 1))
                    ge(pool, x_added, per_item(p, b, 2, a - 3))
                    t0 = TPB * ((b - 1) % B) + 2 * a
                    rows = m.x[:, t0:t0 + 2, :].rearrange("p t d -> p (t d)")
                    pool.tensor_tensor(rows, rows, o_sb[:, a, :], ALU.add).then_inc(x_added, 1)

                def body(p):
                    for b in range(B):
                        if b == B - 2 and ran("Q", p, b + 1):
                            split_w(0, p + 1)
                            split_w(1, p + 1)
                        norm_of(1, p, b)
                        norm_of(2, p, b)
                        norm_of(3, p, b)
                        if b == B - 2 and ran("Q", p, b + 1):
                            split_w(2, p + 1)
                        if ran("O", p, b):
                            if b == 0:
                                split_wo(p)
                            x_of(0, p, b)
                            x_of(1, p, b)

                for i in range(3):
                    split_w(i, 0)
                split_wo(0)
                body(0)
                with pool.Fori(1, NP - 1) as p:
                    body(p)
                body(NP - 1)
                x_of(0, NP, 0)
                x_of(1, NP, 0)

            @block.scalar
            def _(act):
                def copy_hi(dst, src, bias, done):
                    if bias is None:
                        act.activation(dst, src, ACT.Copy).then_inc(done, 1)
                    else:
                        act.activation(dst, src, ACT.Identity, bias=bias).then_inc(done, 1)

                def q_of(p, b):
                    act.wait_ge(q_done, per_item(p, b, 1, 2))
                    if biased and (b == B - 1 or b == -1):
                        act.wait_ge(bqk_ready, (p + (1 if b == B - 1 else 0)) * 1 + 1)
                    copy_hi(q_hi[:, (b + 1) % 2, :], bank_of("Q", 0)[:, :], bqk[:, 0:1] if biased else None, q_hi_ready)

                def k_of(p, b):
                    act.wait_ge(k_done, per_item(p, b, 1, 2))
                    copy_hi(k_hi[:, (b + 1) % 2, :], bank_of("K", 0)[:, :], bqk[:, 1:2] if biased else None, k_hi_ready)

                def vt_of(p, b):
                    act.wait_ge(vt_done, per_item(p, b, 1, 2))
                    act.activation(vT[:, :], bank_of("VT", 0)[:, :], ACT.Copy).then_inc(vT_ready, 1)

                def vr_of(p, b):
                    act.wait_ge(vr_done, per_item(p, b, 1, 2))
                    act.activation(v_hi[:, (b + 1) % 2, :, 0:3:2, :],
                                   bank_of("VR", 0)[:, :].rearrange("p (t h e) -> p t h e", t=TPB, h=2),
                                   ACT.Copy).then_inc(v_hi_ready, 1)

                def exp_of(i, p, b):
                    j = place[i]
                    act.wait_ge(max_ready, per_item(p, b, TPB, i + 1))
                    ge(act, t_done, per_item(p, b, NTURN, t_of[i][-1] + 1 - NTURN))
                    for h in range(2):
                        act.activation(probs[:, j, h, 0:width[j]], s_ps[i % 2][:, h, 0:width[j]], ACT.Exp,
                                       bias=negmax[:, j, h:h + 1], accum_out=sums[:, j, h:h + 1]) \
                            .then_inc(exp_ready, 1)

                def z_of(p, b):
                    act.wait_ge(pvb_done, per_item(p, b, 1, 0))
                    if biased and b == 1:
                        act.wait_ge(bvz_ready, p * 1 + 1)
                    copy_hi(z_hi[:, :], z_ps[:, :], bvz[:, 0:1] if biased else None, z_hi_ready)

                def turn_of(q, p, b):
                    act.wait_ge(t_done, per_item(p, b, NTURN, q + 1))
                    act.activation(turned_into(pT_hi, q), turned_from(q), ACT.Copy).then_inc(pT_hi_ready, 1)

                def o_of(a, p, b):
                    act.wait_ge(o_done, per_item(p, b, 2, a - 1))
                    ge(act, x_added, per_item(p, b, 2, a - 3))
                    act.activation(o_sb[:, a, :], bank_of("O", a)[:, :], ACT.Copy).then_inc(o_read, 1)

                def body(p):
                    for b in range(B):
                        on = lambda kind: ran(kind, p, b)
                        if on("Q"):
                            q_of(p, b)
                        exp_of(0, p, b)
                        if on("Q"):
                            k_of(p, b)
                        exp_of(1, p, b)
                        for q in t_of[0]:
                            turn_of(q, p, b)
                        if on("PVB"):
                            z_of(p, b)
                        for q in t_of[1]:
                            turn_of(q, p, b)
                        if on("VT") and not narrow_first:
                            vt_of(p, b)
                        exp_of(2, p, b)
                        if on("VT") and narrow_first:
                            vt_of(p, b)
                        exp_of(3, p, b)
                        if on("O"):
                            o_of(0, p, b)
                            o_of(1, p, b)
                        if on("VR"):
                            vr_of(p, b)
                        for q in t_of[2] + t_of[3]:
                            turn_of(q, p, b)

                q_of(0, -1), k_of(0, -1), vt_of(0, -1), vr_of(0, -1)
                body(0)
                with act.Fori(1, NP - 1) as p:
                    body(p)
                body(NP - 1)
                z_of(NP, 0)
                o_of(0, NP, 0)
                o_of(1, NP, 0)

            @block.vector
            def _(dve):
                def bias_qk(p):
                    dve.wait_ge(b_loaded, p * 48 + 48)
                    ge(dve, k_ready, per_item(p, 0, 1, 0))
                    dve.tensor_scalar(bqk[:, 0:1], b_stage[:, 0:1], Q_SCALE, None, ALU.mult)
                    dve.tensor_copy(bqk[:, 1:2], b_stage[:, 1:2]).then_inc(bqk_ready, 1)

                def bias_v(p):
                    dve.wait_ge(b_loaded, p * 48 + 48)
                    ge(dve, z_ready, per_item(p, 0, 1, 0))
                    dve.tensor_copy(bvz[:, :], b_stage[:, 2:3]).then_inc(bvz_ready, 1)

                def sub_hi(dst, src, bias, hi, done):
                    if bias is None:
                        dve.tensor_tensor(dst, src, as_f32(hi), ALU.subtract).then_inc(done, 1)
                    else:
                        dve.scalar_tensor_tensor(dst, src, bias, as_f32(hi), ALU.add, ALU.subtract).then_inc(done, 1)

                def q_of(p, b):
                    dve.wait_ge(q_hi_ready, per_item(p, b, 1, 2))
                    sub_hi(q_lo[:, (b + 1) % 2, :], bank_of("Q", 0)[:, :], bqk[:, 0:1] if biased else None,
                           q_hi[:, (b + 1) % 2, :], q_ready)

                def k_of(p, b):
                    dve.wait_ge(k_hi_ready, per_item(p, b, 1, 2))
                    sub_hi(k_lo[:, (b + 1) % 2, :], bank_of("K", 0)[:, :], bqk[:, 1:2] if biased else None,
                           k_hi[:, (b + 1) % 2, :], k_ready)

                def vr_of(p, b):
                    dve.wait_ge(v_hi_ready, per_item(p, b, 1, 2))
                    sub_hi(v_lo[:, (b + 1) % 2, :, 0:3:2, :],
                           bank_of("VR", 0)[:, :].rearrange("p (t h e) -> p t h e", t=TPB, h=2), None,
                           v_hi[:, (b + 1) % 2, :, 0:3:2, :], v_ready)

                def max_of(i, p, b):
                    j = place[i]
                    dve.wait_ge(s_done, per_item(p, b, TPB, i + 1))
                    edges = [n for n, (_, kind) in enumerate(seen[j]) if kind is not None]
                    kinds = [seen[j][n][1] for n in edges]
                    tiles = s_ps[i % 2][:, :, 0:width[j]].rearrange("p h (t n) -> p h t n", n=P)
                    tiles = tiles[:, :, edges[0]:edges[-1] + 1:max(1, edges[-1] - edges[0]), :]
                    mask = m.masks[:, kinds[0]:kinds[-1] + 1, :].rearrange("p (a k) n -> p a k n", a=1) \
                        .to_broadcast([P, 2, len(kinds), P])
                    dve.tensor_tensor(tiles, tiles, mask, ALU.add).then_inc(masked, 1)
                    dve.wait_ge(masked, per_item(p, b, TPB, i + 1))
                    dve.tensor_reduce(negmax[:, j, :], s_ps[i % 2][:, :, 0:width[j]], AX.X, ALU.max,
                                      negate=True).then_inc(max_ready, 1)

                def rsum_of(i, p, b):
                    dve.wait_ge(exp_ready, per_item(p, b, 2 * TPB, 2 * i + 2))
                    dve.reciprocal(rsum[:, place[i], :], sums[:, place[i], :]).then_inc(rsum_ready, 1)

                def norm_first(p, b):
                    j = place[0]
                    dve.wait_ge(rsum_ready, per_item(p, b, TPB, 1))
                    for h in range(2):
                        tile = probs[:, j, h, 0:width[j]]
                        dve.tensor_scalar(tile, tile, rsum[:, j, h:h + 1], None, ALU.mult).then_inc(norm0_ready, 1)

                def z_of(p, b):
                    dve.wait_ge(z_hi_ready, per_item(p, b, 1, 0))
                    sub_hi(z_lo[:, :], z_ps[:, :], bvz[:, 0:1] if biased else None, z_hi[:, :], z_ready)

                def turn_of(q, p, b):
                    dve.wait_ge(pT_hi_ready, per_item(p, b, NTURN, q + 1))
                    dve.tensor_tensor(turned_into(pT_lo, q), turned_from(q), as_f32(turned_into(pT_hi, q)),
                                      ALU.subtract).then_inc(pT_ready, 1)

                def body(p):
                    for b in range(B):
                        on = lambda kind: ran(kind, p, b)
                        max_of(0, p, b)
                        if on("Q"):
                            q_of(p, b)
                        max_of(1, p, b)
                        rsum_of(0, p, b)
                        norm_first(p, b)
                        if on("Q"):
                            k_of(p, b)
                        rsum_of(1, p, b)
                        for q in t_of[0]:
                            turn_of(q, p, b)
                        if on("PVB"):
                            z_of(p, b)
                            if b == 0 and biased:
                                bias_v(p)
                        if narrow_first:
                            max_of(2, p, b)
                        for q in t_of[1]:
                            turn_of(q, p, b)
                        if not narrow_first:
                            max_of(2, p, b)
                        max_of(3, p, b)
                        rsum_of(2, p, b)
                        rsum_of(3, p, b)
                        if b == B - 2 and biased and ran("Q", p, b + 1):
                            bias_qk(p + 1)
                        if on("VR"):
                            vr_of(p, b)
                        for q in t_of[2] + t_of[3]:
                            turn_of(q, p, b)

                if biased:
                    bias_qk(0)
                    bias_v(0)
                q_of(0, -1), k_of(0, -1), vr_of(0, -1)
                body(0)
                with dve.Fori(1, NP - 1) as p:
                    body(p)
                body(NP - 1)
                z_of(NP, 0)

            @block.tensor
            def _(pe):
                def project(kind, i, hi, lo, p, b):
                    wait_bank_free(pe, kind, 0, p, b)
                    cols = slice(S * ((b + 1) % B), S * ((b + 1) % B) + S)
                    out = bank_of(kind, 0)
                    n = 0
                    for k in range(KD):
                        for w, a in ((w_hi, hi), (w_hi, lo), (w_lo, hi)):
                            last = pe.matmul(out[:, :], w[:, i, k, :], a[:, k, cols], start=(n == 0), stop=(n == 5))
                            n += 1
                    return last

                def q_of(p, b):
                    pe.wait_ge(w_ready, (p + (1 if b == B - 1 else 0)) * 3 + 1)
                    project("Q", 0, m.uT_hi, m.uT_lo, p, b).then_inc(q_done, 1)

                def k_of(p, b):
                    pe.wait_ge(w_ready, (p + (1 if b == B - 1 else 0)) * 3 + 2)
                    project("K", 1, m.cT_hi, m.cT_lo, p, b).then_inc(k_done, 1)

                def vt_of(p, b):
                    pe.wait_ge(w_ready, (p + (1 if b == B - 1 else 0)) * 3 + 3)
                    project("VT", 2, m.cT_hi, m.cT_lo, p, b).then_inc(vt_done, 1)

                def vr_of(p, b):
                    wait_bank_free(pe, "VR", 0, p, b)
                    pe.wait_ge(vT_ready, per_item(p, b, 1, 2))
                    for t in range(TPB):
                        last = pe.transpose(bank_of("VR", 0)[:, P * t:P * t + P], vT[:, P * t:P * t + P], m.ident[:, :])
                    last.then_inc(vr_done, 1)

                def scores(i, p, b):
                    j = place[i]
                    if i == 0:
                        pe.wait_ge(q_ready, per_item(p, b, 1, 1))
                        pe.wait_ge(k_ready, per_item(p, b, 1, 1))
                    ge(pe, exp_ready, per_item(p, b, 2 * TPB, 2 * i - 2))
                    cols = slice(P * first_key[j], P * first_key[j] + width[j])
                    for n, (q, k) in enumerate(((q_hi, k_hi), (q_hi, k_lo), (q_lo, k_hi))):
                        for h in range(2):
                            rows = slice(DH * h, DH * h + DH)
                            last = pe.matmul(s_ps[i % 2][:, h, 0:width[j]], q[rows, b % 2, P * j:P * j + P],
                                             k[rows, b % 2, cols], start=(n == 0), stop=(n == 2))
                    last.then_inc(s_done, 1)

                def turn(q, p, b):
                    i, hs = turns[q]
                    j = place[i]
                    wait_bank_free(pe, "T", q, p, b)
                    if i == 0:
                        pe.wait_ge(norm0_ready, per_item(p, b, 2, hs[-1] + 1))
                    else:
                        pe.wait_ge(norm_ready, per_item(p, b, 2 * (TPB - 1), 2 * (i - 1) + hs[-1] + 1))
                    n = 0
                    for h in hs:
                        for t in range(width[j] // P):
                            last = pe.transpose(bank_of("T", q)[:, P * n:P * n + P], probs[:, j, h, P * t:P * t + P],
                                                m.ident[:, :])
                            n += 1
                    last.then_inc(t_done, 1)

                def values(g, i, opens):
                    spans = []
                    for t in range(TPB):
                        js = [j for j in (2 * g, 2 * g + 1) if t in [x[0] for x in seen[j]]]
                        if js:
                            spans.append((t, js))
                    todo = [(h, t, js, w, a) for h in range(2) for t, js in spans
                            for w, a in ((v_hi, pT_hi), (v_hi, pT_lo), (v_lo, pT_hi))]
                    both = [x for x in todo if len(x[2]) == 2]
                    todo = both[:1] + [x for x in todo if len(x[2]) == 1] + both[1:]
                    for n, (h, t, js, w, a) in enumerate(todo):
                        c0, c1 = P * (js[0] % 2), P * (js[-1] % 2) + P
                        last = pe.matmul(z_ps[:, 2 * P * g + c0:2 * P * g + c1],
                                         w[:, i, t, h:h + 2, :], a[:, g, h, t, c0:c1],
                                         start=(opens and n == 0), stop=(n == len(todo) - 1),
                                         skip_group_check=True)
                    return last

                def pva(p, b):
                    pe.wait_ge(pT_ready, per_item(p, b, NTURN, t_of[1][-1] + 1))
                    pe.wait_ge(v_ready, per_item(p, b, 1, 1))
                    ge(pe, z_ready, per_item(p, b, 1, 0))
                    values(place[0] // 2, b % 2, True).then_inc(pva_done, 1)

                def pvb(p, b):
                    pe.wait_ge(pT_ready, per_item(p, b, NTURN, 0))
                    values(place[2] // 2, (b - 1) % 2, False).then_inc(pvb_done, 1)

                def out_of(a, p, b):
                    wait_bank_free(pe, "O", a, p, b)
                    if a == 0:
                        pe.wait_ge(z_ready, per_item(p, b, 1, 0))
                        pe.wait_ge(wo_ready, p + (0 if b == 0 else 1))
                    out = bank_of("O", a)
                    n = 0
                    for t in range(2):
                        cols = slice(P * (2 * a + t), P * (2 * a + t) + P)
                        for z, w in ((z_hi, wo_hi), (z_hi, wo_lo), (z_lo, wo_hi)):
                            last = pe.matmul(out[:, D * t:D * t + D], z[:, cols], w[:, :], start=(n == 0),
                                             stop=(n == 5), skip_group_check=True)
                            n += 1
                    last.then_inc(o_done, 1)

                def body(p):
                    for b in range(B):
                        for kind, q in order:
                            if not ran(kind, p, b):
                                continue
                            if kind == "S":
                                scores(q, p, b)
                            elif kind == "PVB":
                                pvb(p, b)
                            elif kind == "PVA":
                                pva(p, b)
                            elif kind == "Q":
                                q_of(p, b)
                            elif kind == "K":
                                k_of(p, b)
                            elif kind == "VT":
                                vt_of(p, b)
                            elif kind == "VR":
                                vr_of(p, b)
                            elif kind == "T":
                                turn(q, p, b)
                            else:
                                out_of(q, p, b)

                pe.wait_ge(zeroed, 4)
                q_of(0, -1), k_of(0, -1), vt_of(0, -1), vr_of(0, -1)
                body(0)
                with pe.Fori(1, NP - 1) as p:
                    body(p)
                body(NP - 1)
                pvb(NP, 0)
                out_of(0, NP, 0)
                out_of(1, NP, 0)



def expert_inputs(nc, m, g, a):
    with ExitStack() as ctx:
        sb = lambda n, s, d: ctx.enter_context(nc.sbuf_tensor(f"gin_{n}", s, d))
        make = ctx.enter_context(cleared_semaphores(nc))
        sem = lambda n: make(f"gin_{n}")
        st, st2 = Statistics(sb, "st"), Statistics(sb, "st2")
        u, t_sb = sb("u", [P, NT, D], F32), sb("t", [P, NT, D], F32)
        uT = sb("uT", [P, KD, TOK], F32)
        wg, alpha = sb("wg", [P, KD, E], F32), sb("alpha", [P, E], F32)
        rows = sb("rows", [E * NF + 2 * E * KD, P], F32)
        b2 = sb("b2", [E, D], F32)
        logit = sb("logit", [P, NT, E], F32)
        names = ("eq", "cand", "first", "rest", "eq2", "cand2", "second", "g1", "g2")
        v = {n: sb(n, [P, NT, E], F32) for n in names}
        c = {n: sb(n, [P, NT], F32) for n in ("m1", "i1", "m2", "i2", "gap", "ex", "one_ex", "p1", "p2")}
        down = sb("down", [P, E], F32)
        combT = sb("combT", [E, TOK], F32)
        banks = [ctx.enter_context(nc.psum_tensor(f"gin_ps{i}", [P, BANK], F32)) for i in range(4)]
        combT_ps = ctx.enter_context(nc.psum_tensor("gin_cT", [P, TOK], F32))
        small_loaded, rows_loaded = sem("small_loaded"), sem("rows_loaded")
        iota_ready, u_ready = sem("iota_ready"), sem("u_ready")
        dve_step, var_ready, sqrt_ready, var2_ready, sqrt2_ready = \
            sem("dve_step"), sem("var_ready"), sem("sqrt_ready"), sem("var2_ready"), sem("sqrt2_ready")
        u_turned, uT_ready, t_ready, turned, hi_ready, lo_ready = \
            sem("u_turned"), sem("uT_ready"), sem("t_ready"), sem("turned"), sem("hi_ready"), sem("lo_ready")
        logits_done, logits_read, rows_turned, rows_read = \
            sem("logits_done"), sem("logits_read"), sem("rows_turned"), sem("rows_read")
        gap_ready, ex_ready, comb_ready = sem("gap_ready"), sem("ex_ready"), sem("comb_ready")
        comb_turned, combT_ready, bias_done, bias_added = \
            sem("comb_turned"), sem("combT_ready"), sem("bias_done"), sem("bias_added")
        NJ = NT // 2

        with nc.Block() as block:
            @block.sync
            def _(sp):
                sp.dma_start(wg[:, :, :], a["L0_ffn_Wg"].rearrange("(k d) e -> d k e", k=KD)).then_inc(small_loaded, 16)
                sp.dma_start(alpha[:, :], a["L0_ffn_alpha"].rearrange("(a e) -> a e", a=1).to_broadcast([P, E])) \
                    .then_inc(small_loaded, 16)
                sp.dma_start(b2[:, :], a["L0_ffn_fc2_b"]).then_inc(small_loaded, 16)
                n = E * NF
                sp.dma_start(rows[0:n, :], a["L0_ffn_fc1_b"].rearrange("e (f p) -> (e f) p", p=P)).then_inc(rows_loaded, 16)
                for name in ("L0_ffn_ln_w", "L0_ffn_ln_b"):
                    sp.dma_start(rows[n:n + E * KD, :], a[name].rearrange("e (k p) -> (e k) p", p=P)) \
                        .then_inc(rows_loaded, 16)
                    n += E * KD

            @block.gpsimd
            def _(pool):
                pool.iota(down[:, :], pattern=[[-1, E]], base=E, channel_multiplier=0,
                          allow_small_or_imprecise_dtypes=True).then_inc(iota_ready, 1)

            @block.scalar
            def _(act):
                act.wait_ge(var_ready, 1)
                act.activation(st.sd[:, :], st.veps[:, :], ACT.Sqrt).then_inc(sqrt_ready, 1)
                act.wait_ge(var2_ready, 1)
                act.activation(st2.sd[:, :], st2.veps[:, :], ACT.Sqrt).then_inc(sqrt2_ready, 1)
                act.wait_ge(rows_turned, 1)
                act.activation(g.columns[:, :], combT_ps[:, 0:rows.shape[0]], ACT.Copy).then_inc(rows_read, 1)
                for n in range(NJ):
                    act.wait_ge(u_turned, n + 1)
                    act.activation(uT[:, :, 2 * P * n:2 * P * (n + 1)],
                                   banks[n % 2][:, :].rearrange("p (k t) -> p k t", k=KD), ACT.Copy).then_inc(uT_ready, 1)
                for n in range(NJ):
                    act.wait_ge(turned, n + 1)
                    act.activation(m.uT_hi[:, :, 2 * P * n:2 * P * (n + 1)],
                                   banks[2 + n % 2][:, :].rearrange("p (k t) -> p k t", k=KD), ACT.Copy) \
                        .then_inc(hi_ready, 1)
                act.wait_ge(gap_ready, 1)
                act.activation(c["ex"][:, :], c["gap"][:, :], ACT.Exp).then_inc(ex_ready, 1)
                for b in range(B):
                    act.wait_ge(comb_turned, b + 1)
                    act.activation(combT[:, b * S:(b + 1) * S], combT_ps[0:E, b * S:(b + 1) * S], ACT.Copy) \
                        .then_inc(combT_ready, 1)

            @block.vector
            def _(dve):
                chain = Chain(dve, dve_step)

                def step(instruction):
                    chain.inc(instruction)
                    chain.wait()

                def over_experts(col):
                    return col[:, :].rearrange("p (t a) -> p t a", a=1).to_broadcast([P, NT, E])

                def over_tokens(row):
                    return row[:, :].rearrange("p (a e) -> p a e", a=1).to_broadcast([P, NT, E])

                norm_rows(dve, chain, m.x, u, st, var_ready, sqrt_ready)
                chain.wait()
                dve.tensor_copy(st.t1[:, :], st.rstd[:, :]).then_inc(u_ready, 1)
                norm_rows(dve, chain, u, t_sb, st2, var2_ready, sqrt2_ready)
                chain.wait()
                dve.tensor_copy(st2.t1[:, :], st2.rstd[:, :]).then_inc(t_ready, 1)
                for n in range(NJ):
                    dve.wait_ge(hi_ready, n + 1)
                    cols = slice(2 * P * n, 2 * P * (n + 1))
                    dve.tensor_tensor(m.uT_lo[:, :, cols], banks[2 + n % 2][:, :].rearrange("p (k t) -> p k t", k=KD),
                                      as_f32(m.uT_hi[:, :, cols]), ALU.subtract).then_inc(lo_ready, 1)
                dve.wait_ge(logits_done, 1)
                dve.wait_ge(iota_ready, 1)
                dve.wait_ge(small_loaded, 48)
                step(dve.tensor_copy(logit[:, :, :], banks[0][:, 0:NT * E].rearrange("p (t e) -> p t e", e=E)))
                step(dve.tensor_reduce(c["m1"][:, :], logit[:, :, :], AX.X, ALU.max))
                step(dve.tensor_tensor(v["eq"][:, :, :], logit[:, :, :], over_experts(c["m1"]), ALU.is_equal))
                step(dve.tensor_tensor(v["cand"][:, :, :], v["eq"][:, :, :], over_tokens(down), ALU.mult))
                step(dve.tensor_reduce(c["i1"][:, :], v["cand"][:, :, :], AX.X, ALU.max))
                step(dve.tensor_tensor(v["first"][:, :, :], v["cand"][:, :, :], over_experts(c["i1"]), ALU.is_equal))
                step(dve.scalar_tensor_tensor(v["rest"][:, :, :], v["first"][:, :, :], -3.0e38, logit[:, :, :],
                                              ALU.mult, ALU.add))
                step(dve.tensor_reduce(c["m2"][:, :], v["rest"][:, :, :], AX.X, ALU.max))
                step(dve.tensor_tensor(v["eq2"][:, :, :], v["rest"][:, :, :], over_experts(c["m2"]), ALU.is_equal))
                step(dve.tensor_tensor(v["cand2"][:, :, :], v["eq2"][:, :, :], over_tokens(down), ALU.mult))
                step(dve.tensor_reduce(c["i2"][:, :], v["cand2"][:, :, :], AX.X, ALU.max))
                step(dve.tensor_tensor(v["second"][:, :, :], v["cand2"][:, :, :], over_experts(c["i2"]), ALU.is_equal))
                dve.tensor_tensor(c["gap"][:, :], c["m2"][:, :], c["m1"][:, :], ALU.subtract).then_inc(gap_ready, 1)
                dve.wait_ge(ex_ready, 1)
                step(dve.tensor_scalar(c["one_ex"][:, :], c["ex"][:, :], 1.0, None, ALU.add))
                step(dve.reciprocal(c["p1"][:, :], c["one_ex"][:, :]))
                step(dve.tensor_tensor(c["p2"][:, :], c["ex"][:, :], c["p1"][:, :], ALU.mult))
                step(dve.tensor_tensor(v["g1"][:, :, :], v["first"][:, :, :], over_experts(c["p1"]), ALU.mult))
                step(dve.tensor_tensor(v["g2"][:, :, :], v["second"][:, :, :], over_experts(c["p2"]), ALU.mult))
                step(dve.tensor_tensor(v["cand"][:, :, :], v["g1"][:, :, :], v["g2"][:, :, :], ALU.add))
                dve.tensor_tensor(g.comb[:, :, :], v["cand"][:, :, :], over_tokens(alpha), ALU.mult).then_inc(comb_ready, 1)
                dve.wait_ge(comb_ready, 1)
                dve.tensor_copy(g.comb_e[:, :, :].rearrange("p e t -> p t e"), g.comb[:, :, :])
                for n in range(NJ):
                    dve.wait_ge(bias_done, n + 1)
                    dve.tensor_tensor(m.x[:, 2 * n:2 * n + 2, :], m.x[:, 2 * n:2 * n + 2, :],
                                      banks[2 + n % 2][:, :].rearrange("p (t d) -> p t d", t=2), ALU.add) \
                        .then_inc(bias_added, 1)

            @block.tensor
            def _(pe):
                pe.wait_ge(rows_loaded, 48)
                nr = rows.shape[0]
                pe.transpose(combT_ps[:, 0:nr], rows[:, :], m.ident[0:nr, 0:nr]).then_inc(rows_turned, 1)
                for n in range(NJ):
                    if n == 0:
                        pe.wait_ge(u_ready, 1)
                    else:
                        ge(pe, uT_ready, n - 1)
                    for k in range(KD):
                        for j in range(2):
                            last = pe.transpose(banks[n % 2][:, (2 * k + j) * P:(2 * k + j + 1) * P],
                                                u[:, 2 * n + j, k * P:(k + 1) * P], m.ident[:, :])
                    last.then_inc(u_turned, 1)
                for n in range(NJ):
                    if n == 0:
                        pe.wait_ge(t_ready, 1)
                    ge(pe, lo_ready, n - 1)
                    for k in range(KD):
                        for j in range(2):
                            last = pe.transpose(banks[2 + n % 2][:, (2 * k + j) * P:(2 * k + j + 1) * P],
                                                t_sb[:, 2 * n + j, k * P:(k + 1) * P], m.ident[:, :])
                    last.then_inc(turned, 1)
                pe.wait_ge(uT_ready, NJ)
                pe.wait_ge(small_loaded, 48)
                for t in range(NT):
                    for k in range(KD):
                        last = pe.matmul(banks[0][:, E * t:E * t + E], uT[:, k, P * t:P * t + P], wg[:, k, :],
                                         start=(k == 0), stop=(k == KD - 1), skip_group_check=True)
                last.then_inc(logits_done, 1)
                pe.wait_ge(comb_ready, 1)
                pe.wait_ge(rows_read, 1)
                for b in range(B):
                    for t in range(TPB * b, TPB * b + TPB):
                        last = pe.transpose(combT_ps[0:E, P * t:P * t + P], g.comb[:, t, :], m.ident[:, :])
                    last.then_inc(comb_turned, 1)
                pe.wait_ge(lo_ready, NJ)
                for n in range(NJ):
                    if n % 2 == 0:
                        pe.wait_ge(combT_ready, n // 2 + 1)
                    ge(pe, bias_added, n - 1)
                    for t in range(2):
                        cols = slice(P * (2 * n + t), P * (2 * n + t) + P)
                        last = pe.matmul(banks[2 + n % 2][:, D * t:D * t + D], combT[:, cols], b2[:, :],
                                         start=(t == 0), stop=(t == 1), skip_group_check=True)
                    last.then_inc(bias_done, 1)


def experts(nc, m, g, w1_dram, w2_dram):
    STEPS = B * NF
    RING = 4
    LASTB = (B - 1) * NF
    with ExitStack() as ctx:
        sb = lambda n, s, d: ctx.enter_context(nc.sbuf_tensor(f"ex_{n}", s, d))
        make = ctx.enter_context(cleared_semaphores(nc))
        sem = lambda n: make(f"ex_{n}")
        w1_stage, w2_stage = sb("w1_stage", [P, KD, F], F32), sb("w2_stage", [P, NF, D], F32)
        w1_hi, w1_lo = sb("w1_hi", [P, KD, F], F32R), sb("w1_lo", [P, KD, F], F32R)
        w2_hi, w2_lo = sb("w2_hi", [P, NF, D], F32R), sb("w2_lo", [P, NF, D], F32R)
        lnw, lnb, b1 = sb("lnw", [P, KD], F32), sb("lnb", [P, KD], F32), sb("b1", [P, NF], F32)
        comb = sb("comb", [P, NT], F32)
        a_sb = sb("a", [P, RING, S], F32)
        a_hi, a_lo = sb("a_hi", [P, RING, S], F32R), sb("a_lo", [P, RING, S], F32R)
        h_ps = [ctx.enter_context(nc.psum_tensor(f"ex_h{i}", [P, BANK], F32)) for i in range(2)]
        y_ps = [ctx.enter_context(nc.psum_tensor(f"ex_y{i}", [P, TPB, D], F32)) for i in range(2)]
        b_ps = ctx.enter_context(nc.psum_tensor("ex_b", [P, BANK], F32))

        w1_loaded, w2_loaded = sem("w1_loaded"), sem("w2_loaded")
        small_ready, w1_hi_ready, w1_ready, w2_hi_ready, w2_ready = \
            sem("small_ready"), sem("w1_hi_ready"), sem("w1_ready"), sem("w2_hi_ready"), sem("w2_ready")
        bias_done, b1_ready, comb_ready = sem("bias_done"), sem("b1_ready"), sem("comb_ready")
        h_done, a_ready, a_hi_ready, a_lo_ready, y_done, x_added = \
            sem("h_done"), sem("a_ready"), sem("a_hi_ready"), sem("a_lo_ready"), sem("y_done"), sem("x_added")

        def at(e, n, c):
            return e * n + c

        def is_last(e):
            return isinstance(e, int) and e == E - 1

        def is_first(e):
            return isinstance(e, int) and e == 0

        with nc.Block() as block:
            @block.sync
            def _(sp):
                w1_view = w1_dram.rearrange("e (k d) f -> e d k f", k=KD)
                w2_view = w2_dram.rearrange("e (f p) d -> e p f d", p=P)

                def load(e):
                    if not is_first(e):
                        sp.wait_ge(w1_ready, at(e, NF, 0))
                        sp.wait_ge(bias_done, at(e, 1, 0))
                    sp.dma_start(w1_stage[:, :, :], w1_view[e]).then_inc(w1_loaded, 16)
                    if not is_first(e):
                        sp.wait_ge(w2_ready, at(e, NF, 0))
                    sp.dma_start(w2_stage[:, :, :], w2_view[e]).then_inc(w2_loaded, 16)

                load(0)
                with sp.Fori(1, E) as e:
                    load(e)

            @block.gpsimd
            def _(pool):
                def split_w2(e, f):
                    if f == 0:
                        pool.wait_ge(w2_loaded, at(e, 16, 16))
                    if not is_first(e):
                        pool.wait_ge(y_done, at(e, STEPS, LASTB - STEPS + f + 1))
                    one = m.one[:, 0:1].to_broadcast([P, D])
                    pool.tensor_tensor(w2_hi[:, f, :], w2_stage[:, f, :], one, ALU.mult).then_inc(w2_hi_ready, 1)
                    pool.wait_ge(w2_hi_ready, at(e, NF, f + 1))
                    pool.tensor_tensor(w2_lo[:, f, :], w2_stage[:, f, :], as_f32(w2_hi[:, f, :]),
                                       ALU.subtract).then_inc(w2_ready, 1)

                for f in range(NF):
                    split_w2(0, f)
                with pool.Fori(1, E) as e:
                    for f in range(NF):
                        split_w2(e, f)

            @block.scalar
            def _(act):
                def body(e):
                    for s in range(STEPS):
                        if s == 0:
                            act.wait_ge(b1_ready, at(e, 1, 1))
                        act.wait_ge(h_done, at(e, STEPS, s + 1))
                        if not (is_first(e) and s < RING):
                            act.wait_ge(a_lo_ready, at(e, STEPS, s - RING + 1))
                        act.activation(a_sb[:, s % RING, :], h_ps[s % 2][:, :], ACT.Gelu_apprx_tanh,
                                       bias=b1[:, s % NF:s % NF + 1]).then_inc(a_ready, 1)

                body(0)
                with act.Fori(1, E - 1) as e:
                    body(e)
                body(E - 1)

            @block.vector
            def _(dve):
                def small(e):
                    dve.tensor_scalar(lnw[:, :], g.lnw[:, bass.ds(e * KD, KD)], 1.0, None, ALU.mult).then_inc(small_ready, 1)
                    dve.tensor_scalar(lnb[:, :], g.lnb[:, bass.ds(e * KD, KD)], 1.0, None, ALU.mult).then_inc(small_ready, 1)

                def split_w1(e, f):
                    if f == 0:
                        dve.wait_ge(w1_loaded, at(e, 16, 16))
                        dve.wait_ge(small_ready, at(e, 2, 2))
                    if not is_first(e):
                        dve.wait_ge(h_done, at(e, STEPS, LASTB - STEPS + f + 1))
                    cols = slice(P * f, P * f + P)
                    for k in range(KD):
                        dve.tensor_scalar(w1_hi[:, k, cols], w1_stage[:, k, cols], lnw[:, k:k + 1], None,
                                          ALU.mult).then_inc(w1_hi_ready, 1)
                    dve.wait_ge(w1_hi_ready, at(e, KD * NF, KD * (f + 1)))
                    for k in range(KD):
                        last = dve.scalar_tensor_tensor(w1_lo[:, k, cols], w1_stage[:, k, cols], lnw[:, k:k + 1],
                                                        as_f32(w1_hi[:, k, cols]), ALU.mult, ALU.subtract)
                    last.then_inc(w1_ready, 1)

                def bias(e):
                    dve.wait_ge(bias_done, at(e, 1, 1))
                    if not is_first(e):
                        dve.wait_ge(a_ready, at(e, STEPS, 0))
                    dve.tensor_tensor(b1[:, :], b_ps[:, 0:NF], g.fc1b[:, bass.ds(e * NF, NF)], ALU.add).then_inc(b1_ready, 1)

                def halves(e, s):
                    dve.wait_ge(a_ready, at(e, STEPS, s + 1))
                    dve.tensor_copy(a_hi[:, s % RING, :], a_sb[:, s % RING, :]).then_inc(a_hi_ready, 1)
                    dve.wait_ge(a_hi_ready, at(e, STEPS, s + 1))
                    dve.tensor_tensor(a_lo[:, s % RING, :], a_sb[:, s % RING, :], as_f32(a_hi[:, s % RING, :]),
                                      ALU.subtract).then_inc(a_lo_ready, 1)

                def add_y(e, b):
                    dve.wait_ge(y_done, at(e, STEPS, (b + 1) * NF))
                    dve.wait_ge(comb_ready, at(e, 1, 1 if b >= 0 else 0))
                    for t in range(TPB):
                        tile = m.x[:, TPB * (b % B) + t, :]
                        dve.scalar_tensor_tensor(tile, y_ps[b % 2][:, t, :], comb[:, TPB * (b % B) + t:TPB * (b % B) + t + 1],
                                                 tile, ALU.mult, ALU.add).then_inc(x_added, 1)

                def body(e):
                    for s in range(STEPS):
                        halves(e, s)
                        if s >= LASTB and not is_last(e):
                            split_w1(e + 1, s - LASTB)
                        if s % NF == 1 and not (is_first(e) and s == 1):
                            add_y(e, s // NF - 1)
                        if s == 1:
                            if not is_first(e):
                                dve.wait_ge(x_added, at(e, NT, 0))
                            dve.tensor_scalar(comb[:, :], g.comb_e[:, bass.ds(e, 1), :].rearrange("p a t -> p (a t)"),
                                              1.0, None, ALU.mult).then_inc(comb_ready, 1)
                        if s == LASTB - 2 and not is_last(e):
                            dve.wait_ge(bias_done, at(e, 1, 1))
                            dve.wait_ge(w1_ready, at(e, NF, NF))
                            small(e + 1)
                    if not is_last(e):
                        bias(e + 1)

                small(0)
                for f in range(NF):
                    split_w1(0, f)
                bias(0)
                body(0)
                with dve.Fori(1, E - 1) as e:
                    body(e)
                body(E - 1)
                add_y(E, -1)

            @block.tensor
            def _(pe):
                def bias(e):
                    pe.wait_ge(w1_loaded, at(e, 16, 16))
                    pe.wait_ge(small_ready, at(e, 2, 2))
                    if not is_first(e):
                        pe.wait_ge(b1_ready, at(e, 1, 0))
                    for f in range(NF):
                        for k in range(KD):
                            last = pe.matmul(b_ps[:, f:f + 1], w1_stage[:, k, P * f:P * f + P], lnb[:, k:k + 1],
                                             start=(k == 0), stop=(k == KD - 1), skip_group_check=True)
                    last.then_inc(bias_done, 1)

                def hidden(e, s):
                    b, f = s // NF, s % NF
                    if b == 0:
                        pe.wait_ge(w1_ready, at(e, NF, f + 1))
                    if not (is_first(e) and s < 2):
                        pe.wait_ge(a_ready, at(e, STEPS, s - 1))
                    cols = slice(S * b, S * b + S)
                    n = 0
                    for k in range(KD):
                        for w, t in ((w1_hi, m.uT_hi), (w1_hi, m.uT_lo), (w1_lo, m.uT_hi)):
                            last = pe.matmul(h_ps[s % 2][:, :], w[:, k, P * f:P * f + P], t[:, k, cols],
                                             start=(n == 0), stop=(n == 5))
                            n += 1
                    last.then_inc(h_done, 1)

                def output(e, s):
                    b, f = s // NF, s % NF
                    pe.wait_ge(a_lo_ready, at(e, STEPS, s + 1))
                    if b == 0:
                        pe.wait_ge(w2_ready, at(e, NF, f + 1))
                    if f == 0 and not (is_first(e) and b < 2):
                        pe.wait_ge(x_added, at(e, NT, TPB * (b - 1)))
                    for t in range(TPB):
                        cols = slice(P * t, P * t + P)
                        for n, (a, w) in enumerate(((a_hi, w2_hi), (a_hi, w2_lo), (a_lo, w2_hi))):
                            last = pe.matmul(y_ps[b % 2][:, t, :], a[:, s % RING, cols], w[:, f, :],
                                             start=(f == 0 and n == 0 and t % 2 == 0),
                                             stop=(f == NF - 1 and n == 2), skip_group_check=True)
                    last.then_inc(y_done, 1)

                def body(e):
                    for s in range(STEPS):
                        if s + 2 < STEPS:
                            hidden(e, s + 2)
                        elif not is_last(e):
                            hidden(e + 1, s + 2 - STEPS)
                        output(e, s)
                        if s == LASTB and not is_last(e):
                            bias(e + 1)

                bias(0)
                hidden(0, 0)
                hidden(0, 1)
                body(0)
                with pe.Fori(1, E - 1) as e:
                    body(e)
                body(E - 1)


def adapters(nc, m, uT, a):
    N, HD = E, DH
    NC = N * HD // P
    with ExitStack() as ctx:
        sb = lambda n, s, d: ctx.enter_context(nc.sbuf_tensor(f"ad_{n}", s, d))
        make = ctx.enter_context(cleared_semaphores(nc))
        sem = lambda n: make(f"ad_{n}")
        raw = {"base": sb("base", [P, KD, D], F32), "enc": sb("enc", [P, KD, N * HD], F32),
               "dec": sb("dec", [P, NC, D], F32)}
        down, up = sb("down", [P, KD, N, HD], F32), sb("up", [HD, N, D], F32)
        hi = {n: sb(n + "_hi", list(t.shape), F32R) for n, t in raw.items()}
        lo = {n: sb(n + "_lo", list(t.shape), F32R) for n, t in raw.items()}
        vec_rows = sb("vec_rows", [2 * N + NC, P], F32)
        vec = sb("vec", [P, 2 * N + NC], F32)
        b_dec, b_enc = vec[:, 0:2 * N], vec[:, 2 * N:2 * N + NC]
        b_down_rows, b_down = sb("b_down_rows", [N, HD], F32), sb("b_down", [HD, N], F32)
        b_base, b_up = sb("b_base", [P, D], F32), sb("b_up", [P, N, D], F32)
        index = sb("index", [P, N], mybir.dt.int32)
        index_f, falling, rising = sb("index_f", [P, N], F32), sb("falling", [P, N], F32), sb("rising", [P, N], F32)
        h32 = sb("h32", [P, 2, S], F32)
        h_hi, h_lo = sb("h_hi", [P, NC, S], F32R), sb("h_lo", [P, NC, S], F32R)
        diff, square = sb("diff", [P, 2, S], F32), sb("square", [P, S], F32)
        loss = sb("loss", [P, 2 * N], F32)
        names = ("sum8", "eq", "cand", "best", "pick", "chosen")
        v = {n: sb("v_" + n, [P, N], F32) for n in names}
        c = {n: sb("c_" + n, [P, 1], F32) for n in ("low", "first", "adapter", "negative", "wrapped", "least", "most")}
        sel_down, sel_up = sb("sel_down", [P, KD, HD], F32), sb("sel_up", [HD, D], F32)
        sd_hi, sd_lo = sb("sd_hi", [P, KD, HD], F32R), sb("sd_lo", [P, KD, HD], F32R)
        su_hi, su_lo = sb("su_hi", [HD, D], F32R), sb("su_lo", [HD, D], F32R)
        sel_b, sel_bd, bd_terms = sb("sel_b", [P, D], F32), sb("sel_bd", [HD, 1], F32), sb("bd_terms", [HD, N], F32)
        mid, mid_hi, mid_lo = sb("mid", [HD, S], F32), sb("mid_hi", [HD, S], F32R), sb("mid_lo", [HD, S], F32R)
        e_ps = [ctx.enter_context(nc.psum_tensor(f"ad_e{i}", [P, BANK], F32)) for i in range(2)]
        r_ps = [ctx.enter_context(nc.psum_tensor(f"ad_r{i}", [P, BANK], F32)) for i in range(4)]
        o_ps = ctx.enter_context(nc.psum_tensor("ad_o", [P, BANK], F32))
        s_ps = ctx.enter_context(nc.psum_tensor("ad_s", [P, BANK], F32))

        w_loaded, row_loaded, bias_loaded, late_loaded = sem("w_loaded"), sem("row_loaded"), sem("bias_loaded"), sem("late_loaded")
        iota_ready = sem("iota_ready")
        w_hi_ready, w_ready, rows_turned, vec_ready = sem("w_hi_ready"), sem("w_ready"), sem("rows_turned"), sem("vec_ready")
        enc_done, h32_ready, h_hi_ready, h_ready = sem("enc_done"), sem("h32_ready"), sem("h_hi_ready"), sem("h_ready")
        dec_done, diff_ready, loss_ready, loss_summed = sem("dec_done"), sem("diff_ready"), sem("loss_ready"), sem("loss_summed")
        dve_step, picked = sem("dve_step"), sem("picked")
        down_done, mid_ready, mid_split, out_done, x_added = \
            sem("down_done"), sem("mid_ready"), sem("mid_split"), sem("out_done"), sem("x_added")

        jobs = [(ch, dh, e) for ch in range(NC) for dh in range(KD) for e in range(2)]
        NJ = len(jobs)

        def out_bank(i):
            return e_ps[i][:, :]

        with nc.Block() as block:
            @block.sync
            def _(sp):
                sp.dma_start(raw["enc"][:, :, :].rearrange("p k (n h) -> p k n h", n=N)[:, 0, :, :],
                             a["L1_ffn_W_enc"].rearrange("n (k d) h -> k d n h", k=KD)[0]).then_inc(w_loaded, 16)
                sp.dma_start(raw["enc"][:, :, :].rearrange("p k (n h) -> p k n h", n=N)[:, 1, :, :],
                             a["L1_ffn_W_enc"].rearrange("n (k d) h -> k d n h", k=KD)[1]).then_inc(w_loaded, 16)
                sp.dma_start(raw["dec"][:, :, :], a["L1_ffn_W_dec"].rearrange("(c m) h d -> (m h) c d", m=2)) \
                    .then_inc(w_loaded, 16)
                sp.dma_start(raw["base"][:, :, :], a["L1_ffn_W_base"].rearrange("(k d) e -> d k e", k=KD)) \
                    .then_inc(w_loaded, 16)
                for k in range(KD):
                    sp.dma_start(down[:, k, :, :], a["L1_ffn_W_down"].rearrange("n (k d) r -> k d n r", k=KD)[k]) \
                        .then_inc(late_loaded, 16)
                sp.dma_start(up[:, :, :], a["L1_ffn_W_up"].rearrange("n r d -> r n d")).then_inc(late_loaded, 16)

            @block.gpsimd
            def _(pool):
                pool.iota(falling[:, :], pattern=[[-1, N]], base=N, channel_multiplier=0,
                          allow_small_or_imprecise_dtypes=True).then_inc(iota_ready, 1)
                pool.wait_ge(iota_ready, 1)
                pool.iota(rising[:, :], pattern=[[1, N]], base=0, channel_multiplier=0,
                          allow_small_or_imprecise_dtypes=True).then_inc(iota_ready, 1)

            @block.scalar
            def _(act):
                act.dma_start(vec_rows[0:2 * N, :], a["L1_ffn_b_dec"].rearrange("n (k p) -> (n k) p", p=P)) \
                    .then_inc(row_loaded, 16)
                act.dma_start(vec_rows[2 * N:2 * N + NC, :], a["L1_ffn_b_enc"].rearrange("(c m) h -> c (m h)", m=2)).then_inc(row_loaded, 16)
                act.dma_start(b_down_rows[:, :], a["L1_ffn_b_down"]).then_inc(row_loaded, 16)
                row = lambda t: t.rearrange("(a n) -> a n", a=1)
                act.dma_start(b_base[:, :], row(a["L1_ffn_b_base"]).to_broadcast([P, D])).then_inc(bias_loaded, 16)
                act.dma_start(index[:, :], row(a["L1_ffn_connected_idx"]).to_broadcast([P, N])).then_inc(bias_loaded, 16)
                act.dma_start(b_up[:, :, :].rearrange("p n d -> p (n d)"),
                              a["L1_ffn_b_up"].rearrange("(a n) d -> a (n d)", a=1).to_broadcast([P, N * D])) \
                    .then_inc(bias_loaded, 16)

                def middle(b):
                    act.wait_ge(down_done, b + 1)
                    act.wait_ge(picked, b + 1)
                    act.activation(mid[:, :], o_ps[0:HD, :], ACT.Relu, bias=sel_bd[:, 0:1]).then_inc(mid_ready, 1)
                    act.activation(mid_hi[:, :], o_ps[0:HD, :], ACT.Relu, bias=sel_bd[:, 0:1]).then_inc(mid_ready, 1)

                act.wait_ge(vec_ready, 2)
                for b in range(B + 1):
                    if b < B:
                        for ch in range(NC):
                            n = NC * b + ch
                            act.wait_ge(enc_done, n + 1)
                            ge(act, h_ready, n - 1)
                            act.activation(h32[:, ch % 2, :], e_ps[ch % 2][:, :], ACT.Relu, bias=b_enc[:, ch:ch + 1]) \
                                .then_inc(h32_ready, 1)
                            act.activation(h_hi[:, ch, :], e_ps[ch % 2][:, :], ACT.Relu, bias=b_enc[:, ch:ch + 1]) \
                                .then_inc(h_hi_ready, 1)
                        for q in range(NJ):
                            ch, dh, e = jobs[q]
                            col = (2 * ch + e) * KD + dh
                            act.wait_ge(diff_ready, NJ * b + q + 1)
                            ge(act, loss_summed, b)
                            ge(act, loss_ready, NJ * b + q)
                            act.activation(square[:, :], diff[:, q % 2, :], ACT.Square,
                                           accum_out=loss[:, col:col + 1]).then_inc(loss_ready, 1)
                    if b >= 1:
                        middle(b - 1)

            @block.vector
            def _(dve):
                chain = Chain(dve, dve_step)

                def step(instruction):
                    chain.inc(instruction)
                    chain.wait()

                dve.wait_ge(w_loaded, 64)
                for n in ("enc", "dec", "base"):
                    dve.tensor_copy(hi[n][:, :, :], raw[n][:, :, :]).then_inc(w_hi_ready, 1)
                for i, n in enumerate(("enc", "dec", "base")):
                    dve.wait_ge(w_hi_ready, i + 1)
                    dve.tensor_tensor(lo[n][:, :, :], raw[n][:, :, :], as_f32(hi[n][:, :, :]),
                                      ALU.subtract).then_inc(w_ready, 1)
                dve.wait_ge(rows_turned, 1)
                dve.tensor_copy(vec[:, :], s_ps[:, 0:2 * N + NC]).then_inc(vec_ready, 1)
                dve.tensor_copy(b_down[:, :], s_ps[0:HD, 64:64 + N]).then_inc(vec_ready, 1)
                dve.wait_ge(vec_ready, 2)
                dve.wait_ge(bias_loaded, 48)
                dve.wait_ge(iota_ready, 2)
                step(dve.tensor_copy(index_f[:, :], index[:, :]))

                def choose(b):
                    dve.wait_ge(loss_summed, b + 1)
                    step(dve.tensor_reduce(v["sum8"][:, :], s_ps[:, 0:2 * N].rearrange("p (n k) -> p n k", k=KD), AX.X, ALU.add))
                    step(dve.tensor_reduce(c["low"][:, :], v["sum8"][:, :], AX.X, ALU.min))
                    step(dve.tensor_scalar(v["eq"][:, :], v["sum8"][:, :], c["low"][:, 0:1], None, ALU.is_equal))
                    step(dve.tensor_tensor(v["cand"][:, :], v["eq"][:, :], falling[:, :], ALU.mult))
                    step(dve.tensor_reduce(c["first"][:, :], v["cand"][:, :], AX.X, ALU.max))
                    step(dve.tensor_scalar(v["best"][:, :], falling[:, :], c["first"][:, 0:1], None, ALU.is_equal))
                    step(dve.tensor_tensor(v["pick"][:, :], v["best"][:, :], index_f[:, :], ALU.mult))
                    step(dve.tensor_reduce(c["adapter"][:, :], v["pick"][:, :], AX.X, ALU.add))
                    step(dve.tensor_scalar(c["negative"][:, :], c["adapter"][:, :], 0.0, float(N), ALU.is_lt, ALU.mult))
                    step(dve.tensor_tensor(c["wrapped"][:, :], c["adapter"][:, :], c["negative"][:, :], ALU.add))
                    step(dve.tensor_scalar(c["most"][:, :], c["wrapped"][:, :], 0.0, float(N - 1), ALU.max, ALU.min))
                    step(dve.tensor_scalar(v["chosen"][:, :], rising[:, :], c["most"][:, 0:1], None, ALU.is_equal))
                    if b > 0:
                        dve.wait_ge(out_done, 2 * b)
                        dve.wait_ge(x_added, 2 * b)
                    else:
                        dve.wait_ge(late_loaded, 48)
                    one = v["chosen"]
                    chain.inc(dve.tensor_scalar(sel_down[:, :, :], down[:, :, 0, :], one[:, 0:1], None, ALU.mult))
                    chain.inc(dve.tensor_scalar(sel_up[:, :], up[:, 0, :], one[0:HD, 0:1], None, ALU.mult))
                    chain.inc(dve.scalar_tensor_tensor(sel_b[:, :], b_up[:, 0, :], one[:, 0:1], b_base[:, :], ALU.mult, ALU.add))
                    chain.inc(dve.tensor_tensor(bd_terms[:, :], b_down[:, :], one[0:HD, :], ALU.mult))
                    for n in range(1, N):
                        chain.wait()
                        chain.inc(dve.scalar_tensor_tensor(sel_down[:, :, :], down[:, :, n, :], one[:, n:n + 1],
                                                           sel_down[:, :, :], ALU.mult, ALU.add))
                        chain.inc(dve.scalar_tensor_tensor(sel_up[:, :], up[:, n, :], one[0:HD, n:n + 1],
                                                           sel_up[:, :], ALU.mult, ALU.add))
                        chain.inc(dve.scalar_tensor_tensor(sel_b[:, :], b_up[:, n, :], one[:, n:n + 1],
                                                           sel_b[:, :], ALU.mult, ALU.add))
                    chain.wait()
                    chain.inc(dve.tensor_reduce(sel_bd[:, :], bd_terms[:, :], AX.X, ALU.add))
                    chain.inc(dve.tensor_copy(sd_hi[:, :, :], sel_down[:, :, :]))
                    chain.inc(dve.tensor_copy(su_hi[:, :], sel_up[:, :]))
                    chain.wait()
                    chain.inc(dve.tensor_tensor(sd_lo[:, :, :], sel_down[:, :, :], as_f32(sd_hi[:, :, :]), ALU.subtract))
                    dve.tensor_tensor(su_lo[:, :], sel_up[:, :], as_f32(su_hi[:, :]), ALU.subtract).then_inc(picked, 1)

                for b in range(B + 1):
                    if b < B:
                        for ch in range(NC):
                            dve.wait_ge(h32_ready, NC * b + ch + 1)
                            dve.wait_ge(h_hi_ready, NC * b + ch + 1)
                            dve.tensor_tensor(h_lo[:, ch, :], h32[:, ch % 2, :], as_f32(h_hi[:, ch, :]),
                                              ALU.subtract).then_inc(h_ready, 1)
                        for q in range(NJ):
                            ch, dh, e = jobs[q]
                            col = (2 * ch + e) * KD + dh
                            dve.wait_ge(dec_done, NJ * b + q + 1)
                            ge(dve, loss_ready, NJ * b + q - 1)
                            dve.scalar_tensor_tensor(diff[:, q % 2, :], r_ps[q % 4][:, :], b_dec[:, col:col + 1],
                                                     uT[:, dh, S * b:S * b + S], ALU.add, ALU.subtract) \
                                .then_inc(diff_ready, 1)
                    if b >= 1:
                        dve.wait_ge(mid_ready, 2 * b)
                        dve.tensor_tensor(mid_lo[:, :], mid[:, :], as_f32(mid_hi[:, :]), ALU.subtract).then_inc(mid_split, 1)
                        t0 = TPB * (b - 1)
                        for t in range(TPB):
                            chain.inc(dve.tensor_tensor(m.x[:, t0 + t, :], m.x[:, t0 + t, :], sel_b[:, :], ALU.add))
                        chain.wait()
                        for i in range(2):
                            dve.wait_ge(out_done, 2 * (b - 1) + i + 1)
                            rows = m.x[:, t0 + 2 * i:t0 + 2 * i + 2, :]
                            dve.tensor_tensor(rows, rows, out_bank(i).rearrange("p (t d) -> p t d", t=2),
                                              ALU.add).then_inc(x_added, 1)
                    if b < B:
                        choose(b)

            @block.tensor
            def _(pe):
                pe.wait_ge(row_loaded, 48)
                nr = 2 * N + NC
                pe.transpose(s_ps[:, 0:nr], vec_rows[:, :], m.ident[0:nr, 0:nr])
                pe.transpose(s_ps[0:HD, 64:64 + N], b_down_rows[:, :], m.ident[0:N, 0:N]).then_inc(rows_turned, 1)
                pe.wait_ge(w_ready, 3)

                def three(out, w_hi, w_lo, b_hi, b_lo, first, last_, **more):
                    pe.matmul(out, w_hi, b_hi, start=first, stop=False, **more)
                    pe.matmul(out, w_hi, b_lo, start=False, stop=False, **more)
                    return pe.matmul(out, w_lo, b_hi, start=False, stop=last_, **more)

                for b in range(B + 1):
                    if b < B:
                        cols = slice(S * b, S * b + S)
                        for ch in range(NC):
                            if ch >= 2:
                                pe.wait_ge(h_hi_ready, NC * b + ch - 1)
                            elif b >= 2:
                                pe.wait_ge(x_added, 2 * (b - 1))
                            if ch < 2 and b >= 1:
                                pe.wait_ge(h_hi_ready, NC * b)
                            for k in range(KD):
                                f = slice(P * ch, P * ch + P)
                                last = three(e_ps[ch % 2][:, :], hi["enc"][:, k, f], lo["enc"][:, k, f],
                                             m.uT_hi[:, k, cols], m.uT_lo[:, k, cols], k == 0, k == KD - 1)
                            last.then_inc(enc_done, 1)
                        for q in range(0, NJ, 2):
                            ch, dh, _ = jobs[q]
                            pe.wait_ge(h_ready, NC * b + ch + 1)
                            ge(pe, diff_ready, NJ * b + q - 2)
                            d = slice(P * dh, P * dh + P)
                            for n, (w, h) in enumerate(((hi, h_hi), (hi, h_lo), (lo, h_hi))):
                                for e in range(2):
                                    rows = slice(HD * e, HD * e + HD)
                                    last = pe.matmul(r_ps[(q + e) % 4][:, :], w["dec"][rows, ch, d], h[rows, ch, :],
                                                     start=(n == 0), stop=(n == 2))
                                    if n == 2:
                                        last.then_inc(dec_done, 1)
                        pe.wait_ge(loss_ready, NJ * (b + 1))
                        pe.wait_ge(vec_ready, 2)
                        if b >= 1:
                            pe.wait_ge(picked, b)
                        pe.matmul(s_ps[:, 0:2 * N], m.one[:, :], loss[:, :], start=True, stop=True).then_inc(loss_summed, 1)
                    if b >= 1:
                        cols = slice(S * (b - 1), S * b)
                        pe.wait_ge(picked, b)
                        ge(pe, mid_ready, 2 * (b - 1))
                        for k in range(KD):
                            last = three(o_ps[0:HD, :], sd_hi[:, k, :], sd_lo[:, k, :],
                                         m.uT_hi[:, k, cols], m.uT_lo[:, k, cols], k == 0, k == KD - 1)
                        last.then_inc(down_done, 1)
                        for i in range(2):
                            pe.wait_ge(h_hi_ready, NC * min(b + 1, B))
                            for j in range(2):
                                t = slice(S * (b - 1) + P * (2 * i + j), S * (b - 1) + P * (2 * i + j) + P)
                                for k in range(KD):
                                    three(out_bank(i)[:, D * j:D * j + D], m.uT_hi[:, k, t], m.uT_lo[:, k, t],
                                          hi["base"][:, k, :], lo["base"][:, k, :], j == 0 and k == 0, False,
                                          skip_group_check=True)
                        for i in range(2):
                            if i == 0:
                                pe.wait_ge(mid_split, b)
                            for j in range(2):
                                t = slice(P * (2 * i + j), P * (2 * i + j) + P)
                                last = three(out_bank(i)[:, D * j:D * j + D], mid_hi[:, t], mid_lo[:, t],
                                             su_hi[:, :], su_lo[:, :], False, True, skip_group_check=True)
                            last.then_inc(out_done, 1)


def causal(j):
    return [(t, UP if t == j else None) for t in range(j + 1)]


def banded(j):
    return [(t, {-1: LOW, 0: None, 1: UP}[t - j]) for t in range(max(0, j - 1), min(TPB, j + 2))]


def write_out(nc, m, out_dram):
    with nc.semaphore("stored") as stored:
        with nc.Block() as block:
            @block.sync
            def _(sp):
                for b in range(B):
                    sp.dma_start(out_dram[b * S:(b + 1) * S, :].rearrange("(t p) d -> p t d", p=P),
                                 m.x[:, TPB * b:TPB * b + TPB, :]).then_inc(stored, 16)
                sp.wait_ge(stored, 16 * B)


def program(nc, a, out):
    x_dram = a["x"].rearrange("b s d -> (b s) d")
    ctx_dram = a["ctx_1024"].rearrange("b s d -> (b s) d")
    out_dram = out.rearrange("b s d -> (b s) d")
    with ExitStack() as ctx:
        sb = lambda n, s, d: ctx.enter_context(nc.sbuf_tensor(n, s, d))
        m = Shared(sb)

        def head_major(w):
            view = w.rearrange("(p h) (k d) e -> p h d k e", h=2, k=KD)
            return lambda dst, p: [(dst[:, :, DH * h:DH * h + DH], view[p, h]) for h in range(2)]

        def column_major(w):
            view = w.rearrange("(k d) (p n) -> p d k n", k=KD, n=P)
            return lambda dst, p: [(dst, view[p])]

        def head_bias(w):
            view = w.rearrange("(p h) (e a) -> p (h e) a", h=2, a=1)
            return lambda p: view[p]

        wo0 = a["L0_xattn_W_O"].rearrange("(p h) e d -> p (h e) d", h=2)
        wo1 = a["L1_xattn_Wo"].rearrange("(p n) d -> p n d", n=P)
        attention_inputs(nc, m, "in0", x_dram, ctx_dram, a["L0_xattn_b_O"])
        attention(nc, m, "att0", head_major(a["L0_xattn_W_Q"]), head_major(a["L0_xattn_W_K"]),
                  head_major(a["L0_xattn_W_V"]), lambda p: wo0[p], head_bias(a["L0_xattn_b_Q"]),
                  head_bias(a["L0_xattn_b_K"]), head_bias(a["L0_xattn_b_V"]), causal)
        with ExitStack() as inner:
            g = Gates(lambda n, shape, dtype: inner.enter_context(nc.sbuf_tensor(n, shape, dtype)))
            expert_inputs(nc, m, g, a)
            experts(nc, m, g, a["L0_ffn_fc1_w"], a["L0_ffn_fc2_w"])
        attention_inputs(nc, m, "in1", None, None, None)
        attention(nc, m, "att1", column_major(a["L1_xattn_Wq"]), column_major(a["L1_xattn_Wk"]),
                  column_major(a["L1_xattn_Wv"]), lambda p: wo1[p], None, None, None, banded)
        with nc.sbuf_tensor("uT32", [P, KD, TOK], F32) as uT32:
            attention_inputs(nc, m, "in2", None, None, None, uT32)
            adapters(nc, m, uT32, a)
        write_out(nc, m, out_dram)

def kernel(**inputs):
    import numpy as _np
    import concourse.bacc as _bacc
    from concourse import mybir as _mybir
    from concourse.bass_utils import run_bass_kernel_spmd as _run

    nc = _bacc.Bacc("TRN2", target_bir_lowering=False, num_devices=1)
    arrays, args = {}, {}
    for name in inputs:
        array = _np.ascontiguousarray(inputs[name])
        arrays[f"in_{name}"] = array
        args[name] = nc.dram_tensor(f"in_{name}", array.shape, _mybir.dt.from_np(array.dtype),
                                    kind="ExternalInput").ap()
    out = nc.dram_tensor("out_0", (4, 512, 256), _mybir.dt.float32, kind="ExternalOutput").ap()
    program(nc, args, out)
    result = _run(nc, [arrays], core_ids=[0])
    return result.results[0]["out_0"]
```

```python
from contextlib import ExitStack, contextmanager

import concourse.bass as bass
from concourse import mybir

F32 = mybir.dt.float32
F32R = mybir.dt.float32r
BF16 = mybir.dt.bfloat16
ALU = mybir.AluOpType
ACT = mybir.ActivationFunctionType
AX = mybir.AxisListType

P = 128
D = 256
KD = D // P
B = 4
S = 512
TOK = B * S
NT = TOK // P
TPB = S // P
H = 16
DH = 64
NP = H // 2
LN_EPS = 1e-5
Q_SCALE = DH ** -0.5
MASKED = -(2.0 ** 100)
LOW, UP = 0, 1
E = 8
F = 1024
NF = F // P
BANK = 512


def ge(eng, sem, count):
    if isinstance(count, int) and count <= 0:
        return
    eng.wait_ge(sem, count)


def as_f32(ap):
    return ap.bitcast(F32)


@contextmanager
def cleared_semaphores(nc):
    made = []

    def make(name):
        made.append(nc.alloc_semaphore(name))
        return made[-1]

    yield make
    nc.clear_and_free_semaphores(made)
    nc.all_engine_barrier()


class Shared:

    def __init__(self, sb):
        self.x = sb("x_sb", [P, NT, D], F32)
        self.uT_hi, self.uT_lo = sb("uT_hi", [P, KD, TOK], F32R), sb("uT_lo", [P, KD, TOK], F32R)
        self.cT_hi, self.cT_lo = sb("cT_hi", [P, KD, TOK], F32R), sb("cT_lo", [P, KD, TOK], F32R)
        self.ident, self.one = sb("ident", [P, P], F32), sb("one", [P, P], F32)
        self.masks = sb("masks", [P, 2, P], F32)
        self.bn, self.mv = sb("bn", [P, NT, 6], F32), sb("mv", [P, NT, 2], F32)
        self.consts = sb("consts", [P, 2], F32)


class PairWeights:

    def __init__(self, sb, sem, tag, wq, wk, wv, wo, biases=None):
        self.w = sb(tag + "_w_stage", [P, 3, KD, P], F32)
        self.wo = sb(tag + "_wo_stage", [P, D], F32)
        self.b = sb(tag + "_b_stage", [P, 3], F32)
        self.w_loaded, self.wo_loaded, self.b_loaded = \
            (sem(tag + n) for n in ("_w_loaded", "_wo_loaded", "_b_loaded"))
        self.w_dram, self.wo_dram, self.biases = (wq, wk, wv), wo, biases
        self.dmas = sum(len(w(self.w[:, 0, :, :], 0)) for w in self.w_dram)

    def load(self, sp, p):
        for i, w in enumerate(self.w_dram):
            for dst, src in w(self.w[:, i, :, :], p):
                sp.dma_start(dst, src).then_inc(self.w_loaded, 16)
        sp.dma_start(self.wo[:, :], self.wo_dram(p)).then_inc(self.wo_loaded, 16)
        if self.biases is not None:
            for i, bias in enumerate(self.biases):
                sp.dma_start(self.b[:, i:i + 1], bias(p)).then_inc(self.b_loaded, 16)


class Experts:

    def __init__(self, sb, psum, sem):
        self.columns = sb("g_columns", [P, E * NF + 2 * E * KD], F32)
        self.comb, self.comb_e = sb("g_comb", [P, NT, E], F32), sb("g_comb_e", [P, E, NT], F32)
        self.fc1b = self.columns[:, 0:E * NF]
        self.lnw = self.columns[:, E * NF:E * NF + E * KD]
        self.lnb = self.columns[:, E * NF + E * KD:E * NF + 2 * E * KD]
        self.root_u = sb("g_root_u", [P, NT], F32)
        self.wg, self.alpha = sb("g_wg", [P, KD, E], F32), sb("g_alpha", [P, E], F32)
        self.wg_hi, self.wg_lo = sb("g_wg_hi", [P, KD, E], F32R), sb("g_wg_lo", [P, KD, E], F32R)
        self.logit_ps = psum("g_logit_ps", [P, BANK], F32)
        self.rows, self.b2 = sb("g_rows", [E * NF + 2 * E * KD, P], F32), sb("g_b2", [E, D], F32)
        self.w1_stage, self.w2_stage = sb("w1_stage", [P, KD, F], F32), sb("w2_stage", [P, NF, D], F32)
        self.small_loaded, self.rows_loaded, self.w1_loaded, self.w2_loaded = \
            (sem(n) for n in ("g_small_loaded", "g_rows_loaded", "w1_loaded", "w2_loaded"))

    def load(self, sp, a):
        sp.dma_start(self.wg[:, :, :], a["L0_ffn_Wg"].rearrange("(k d) e -> d k e", k=KD)).then_inc(self.small_loaded, 16)
        sp.dma_start(self.alpha[:, :], a["L0_ffn_alpha"].rearrange("(a e) -> a e", a=1).to_broadcast([P, E])) \
            .then_inc(self.small_loaded, 16)
        sp.dma_start(self.b2[:, :], a["L0_ffn_fc2_b"]).then_inc(self.small_loaded, 16)
        n = E * NF
        sp.dma_start(self.rows[0:n, :], a["L0_ffn_fc1_b"].rearrange("e (f p) -> (e f) p", p=P)) \
            .then_inc(self.rows_loaded, 16)
        for name in ("L0_ffn_ln_w", "L0_ffn_ln_b"):
            sp.dma_start(self.rows[n:n + E * KD, :], a[name].rearrange("e (k p) -> (e k) p", p=P)) \
                .then_inc(self.rows_loaded, 16)
            n += E * KD
        sp.dma_start(self.w1_stage[:, :, :], a["L0_ffn_fc1_w"].rearrange("e (k d) f -> e d k f", k=KD)[0]) \
            .then_inc(self.w1_loaded, 16)
        sp.dma_start(self.w2_stage[:, :, :], a["L0_ffn_fc2_w"].rearrange("e (f p) d -> e p f d", p=P)[0]) \
            .then_inc(self.w2_loaded, 16)


class Adapters:

    def __init__(self, sb, sem):
        nc_ = E * DH // P
        self.enc, self.dec = sb("ad_enc", [P, KD, E * DH], F32), sb("ad_dec", [P, nc_, D], F32)
        self.base = sb("ad_base", [P, KD, D], F32)
        self.down, self.up = sb("ad_down", [P, KD, E, DH], F32), sb("ad_up", [DH, E, D], F32)
        self.vec_rows, self.b_down_rows = sb("ad_vec_rows", [2 * E + nc_, P], F32), sb("ad_b_down_rows", [E, DH], F32)
        self.b_base, self.b_up = sb("ad_b_base", [P, D], F32), sb("ad_b_up", [P, E, D], F32)
        self.index = sb("ad_index", [P, E], mybir.dt.int32)
        self.w_loaded, self.row_loaded, self.bias_loaded, self.late_loaded = \
            (sem("ad_" + n) for n in ("w_loaded", "row_loaded", "bias_loaded", "late_loaded"))

    def load(self, sp, a):
        n_dec = 2 * E
        row = lambda t: t.rearrange("(a n) -> a n", a=1)
        for k in range(KD):
            sp.dma_start(self.enc[:, :, :].rearrange("p k (n h) -> p k n h", n=E)[:, k, :, :],
                         a["L1_ffn_W_enc"].rearrange("n (k d) h -> k d n h", k=KD)[k]).then_inc(self.w_loaded, 16)
        sp.dma_start(self.dec[:, :, :], a["L1_ffn_W_dec"].rearrange("(c m) h d -> (m h) c d", m=2)) \
            .then_inc(self.w_loaded, 16)
        sp.dma_start(self.base[:, :, :], a["L1_ffn_W_base"].rearrange("(k d) e -> d k e", k=KD)).then_inc(self.w_loaded, 16)
        sp.dma_start(self.vec_rows[0:n_dec, :], a["L1_ffn_b_dec"].rearrange("n (k p) -> (n k) p", p=P)) \
            .then_inc(self.row_loaded, 16)
        sp.dma_start(self.vec_rows[n_dec:, :], a["L1_ffn_b_enc"].rearrange("(c m) h -> c (m h)", m=2)) \
            .then_inc(self.row_loaded, 16)
        sp.dma_start(self.b_down_rows[:, :], a["L1_ffn_b_down"]).then_inc(self.row_loaded, 16)
        sp.dma_start(self.b_base[:, :], row(a["L1_ffn_b_base"]).to_broadcast([P, D])).then_inc(self.bias_loaded, 16)
        sp.dma_start(self.index[:, :], row(a["L1_ffn_connected_idx"]).to_broadcast([P, E])).then_inc(self.bias_loaded, 16)
        sp.dma_start(self.b_up[:, :, :].rearrange("p n d -> p (n d)"),
                     a["L1_ffn_b_up"].rearrange("(a n) d -> a (n d)", a=1).to_broadcast([P, E * D])) \
            .then_inc(self.bias_loaded, 16)
        for k in range(KD):
            sp.dma_start(self.down[:, k, :, :], a["L1_ffn_W_down"].rearrange("n (k d) r -> k d n r", k=KD)[k]) \
                .then_inc(self.late_loaded, 16)
        sp.dma_start(self.up[:, :, :], a["L1_ffn_W_up"].rearrange("n r d -> r n d")).then_inc(self.late_loaded, 16)


class Chain:

    def __init__(self, eng, sem):
        self.eng, self.sem, self.count = eng, sem, 0

    def inc(self, instruction):
        self.count += 1
        instruction.then_inc(self.sem, 1)

    def wait(self):
        self.eng.wait_ge(self.sem, self.count)


def batch_statistics(dve, chain, m, b):
    for t in range(TPB * b, TPB * b + TPB):
        chain.inc(dve.bn_stats(m.bn[:, t, :], m.x[:, t, :]))
    chain.wait()
    for t in range(TPB * b, TPB * b + TPB):
        chain.inc(dve.bn_aggr(m.mv[:, t, :], m.bn[:, t, :]))


def norm_inputs(nc, m, tag, prefetch, x_dram=None, ctx_dram=None, uT32=None, experts=None):
    with ExitStack() as ctx:
        sb = lambda n, s, d: ctx.enter_context(nc.sbuf_tensor(f"{tag}_{n}", s, d))
        make = ctx.enter_context(cleared_semaphores(nc))
        sem = lambda n: make(f"{tag}_{n}")
        first = x_dram is not None
        col = {n: sb(n, [P, NT], F32) for n in ("veps", "sd", "r0", "t1", "t2", "t3", "r1", "v_u", "veps2", "sd2",
                                                "s0", "s1", "s2", "s3", "r2", "r12")}
        u = sb("u", [P, NT, D], F32)
        c = sb("c", [P, NT, D], F32) if first else None
        banks = [ctx.enter_context(nc.psum_tensor(f"{tag}_ps{i}", [P, BANK], F32)) for i in range(4)]
        x_loaded, c_loaded = ([sem(f"{n}_loaded{b}") for b in range(B)] for n in ("x", "c"))
        const_step, const_ready = sem("const_step"), sem("const_ready")
        dve_step, var_ready, sqrt_ready = sem("dve_step"), sem("var_ready"), sem("sqrt_ready")
        rstd_ready, u_dve_ready, u_pool_ready = sem("rstd_ready"), sem("u_dve_ready"), sem("u_pool_ready")
        wg_hi_ready, wg_ready = sem("wg_hi_ready"), sem("wg_ready")
        turned, hi_ready, lo_ready = sem("turned"), sem("hi_ready"), sem("lo_ready")
        f32_ready = sem("f32_ready")

        jobs = ([(c, m.cT_hi, m.cT_lo, g) for g in range(NT // 2)] if first else []) + \
               [(u, m.uT_hi, m.uT_lo, g) for g in range(NT // 2)]
        n_c = len(jobs) - NT // 2
        rstd = col["r12"] if experts is not None else col["r1"]

        def normalise(eng, t):
            return eng.tensor_scalar(u[:, t, :], m.x[:, t, :], m.mv[:, t, 0:1], rstd[:, t:t + 1], ALU.subtract, ALU.mult)

        with nc.Block() as block:
            @block.sync
            def _(sp):
                if first:
                    for b in range(B):
                        rows = slice(b * S, (b + 1) * S)
                        sp.dma_start(m.x[:, TPB * b:TPB * b + TPB, :],
                                     x_dram[rows, :].rearrange("(t p) d -> p t d", p=P)).then_inc(x_loaded[b], 16)
                prefetch(sp)

            @block.gpsimd
            def _(pool):
                if first:
                    make_constants(pool, m, const_step, const_ready)
                    pool.wait_ge(const_ready, 1)
                pool.wait_ge(rstd_ready, 1)
                for n, t in enumerate(range(3, NT, 4)):
                    ge(pool, u_pool_ready, n)
                    normalise(pool, t).then_inc(u_pool_ready, 1)

            @block.scalar
            def _(act):
                if first:
                    for b in range(B):
                        rows = slice(b * S, (b + 1) * S)
                        act.dma_start(c[:, TPB * b:TPB * b + TPB, :],
                                      ctx_dram[rows, :].rearrange("(t p) d -> p t d", p=P)).then_inc(c_loaded[b], 16)
                roots = [("sd", "veps")] + ([("sd2", "veps2")] if experts is not None else [])

                def root(i):
                    out, src = roots[i]
                    act.wait_ge(var_ready, i + 1)
                    act.activation(col[out][:, :], col[src][:, :], ACT.Sqrt).then_inc(sqrt_ready, 1)

                if not first:
                    for i in range(len(roots)):
                        root(i)
                for n, (_, hi, lo, g) in enumerate(jobs):
                    if first and n == n_c - 2:
                        root(0)
                    act.wait_ge(turned, n + 1)
                    act.activation(hi[:, :, 2 * P * g:2 * P * (g + 1)],
                                   banks[n % 4][:, :].rearrange("p (k t) -> p k t", k=KD), ACT.Copy) \
                        .then_inc(hi_ready, 1)
                    if uT32 is not None:
                        act.activation(uT32[:, :, 2 * P * g:2 * P * (g + 1)],
                                       banks[n % 4][:, :].rearrange("p (k t) -> p k t", k=KD), ACT.Copy) \
                            .then_inc(f32_ready, 1)

            @block.vector
            def _(dve):
                chain = Chain(dve, dve_step)

                def step(instruction):
                    chain.inc(instruction)
                    chain.wait()

                def inverse_root(veps, sd, names):
                    r0, t1, t2, t3, out = (col[n] for n in names)
                    step(dve.reciprocal(r0[:, :], col[sd][:, :]))
                    step(dve.tensor_tensor(t1[:, :], r0[:, :], r0[:, :], ALU.mult))
                    step(dve.tensor_tensor(t2[:, :], t1[:, :], col[veps][:, :], ALU.mult))
                    step(dve.tensor_scalar(t3[:, :], t2[:, :], -0.5, 1.5, ALU.mult, ALU.add))
                    step(dve.tensor_tensor(out[:, :], r0[:, :], t3[:, :], ALU.mult))

                def lo_of(n):
                    _, hi, lo, g = jobs[n]
                    dve.wait_ge(hi_ready, n + 1)
                    if uT32 is not None:
                        dve.wait_ge(f32_ready, n + 1)
                    cols = slice(2 * P * g, 2 * P * (g + 1))
                    dve.tensor_tensor(lo[:, :, cols], banks[n % 4][:, :].rearrange("p (k t) -> p k t", k=KD),
                                      as_f32(hi[:, :, cols]), ALU.subtract).then_inc(lo_ready, 1)

                if first:
                    for b in range(B):
                        dve.wait_ge(x_loaded[b], 16)
                        batch_statistics(dve, chain, m, b)
                        if b == 0:
                            lo_of(0)
                            lo_of(1)
                        elif b == 1:
                            lo_of(2)
                            lo_of(3)
                    chain.wait()
                dve.tensor_scalar(col["veps"][:, :], m.mv[:, :, 1], LN_EPS, None, ALU.add).then_inc(var_ready, 1)
                if first:
                    lo_of(4)
                    lo_of(5)
                dve.wait_ge(sqrt_ready, 1)
                dve.wait_ge(var_ready, 1)
                inverse_root("veps", "sd", ("r0", "t1", "t2", "t3", "r1"))
                if experts is not None:
                    step(dve.tensor_tensor(col["s0"][:, :], col["r1"][:, :], col["r1"][:, :], ALU.mult))
                    step(dve.tensor_tensor(col["v_u"][:, :], col["s0"][:, :], m.mv[:, :, 1], ALU.mult))
                    dve.tensor_scalar(col["veps2"][:, :], col["v_u"][:, :], LN_EPS, None, ALU.add).then_inc(var_ready, 1)
                    dve.wait_ge(sqrt_ready, 2)
                    dve.wait_ge(var_ready, 2)
                    inverse_root("veps2", "sd2", ("s1", "t1", "s2", "s3", "r2"))
                    step(dve.tensor_tensor(experts.root_u[:, :], col["veps2"][:, :], col["r2"][:, :], ALU.mult))
                    step(dve.tensor_tensor(col["r12"][:, :], col["r1"][:, :], col["r2"][:, :], ALU.mult))
                dve.tensor_copy(col["t1"][:, :], rstd[:, :]).then_inc(rstd_ready, 1)
                for t in range(6):
                    if t % 4 != 3:
                        normalise(dve, t).then_inc(u_dve_ready, 1)
                if experts is not None:
                    dve.wait_ge(experts.small_loaded, 48)
                    dve.tensor_copy(experts.wg_hi[:, :, :], experts.wg[:, :, :]).then_inc(wg_hi_ready, 1)
                    dve.wait_ge(wg_hi_ready, 1)
                    dve.tensor_tensor(experts.wg_lo[:, :, :], experts.wg[:, :, :], as_f32(experts.wg_hi[:, :, :]),
                                      ALU.subtract).then_inc(wg_ready, 1)
                for n in range(6 if first else 0, len(jobs)):
                    lo_of(n)
                    for t in (2 * (n - n_c) + 6, 2 * (n - n_c) + 7):
                        if 6 <= t < NT and t % 4 != 3:
                            normalise(dve, t).then_inc(u_dve_ready, 1)

            @block.tensor
            def _(pe):
                if first:
                    pe.wait_ge(const_ready, 1)

                def logits_of(g):
                    pe.wait_ge(lo_ready, g + 1)
                    if g == 0:
                        pe.wait_ge(wg_ready, 1)
                    for t in (2 * g, 2 * g + 1):
                        cols = slice(P * t, P * t + P)
                        n = 0
                        for k in range(KD):
                            for u_half, w in ((m.uT_hi, experts.wg_hi), (m.uT_hi, experts.wg_lo), (m.uT_lo, experts.wg_hi)):
                                pe.matmul(experts.logit_ps[:, E * t:E * t + E], u_half[:, k, cols], w[:, k, :],
                                          start=(n == 0), stop=(n == 5), skip_group_check=True)
                                n += 1

                for n, (src, _, _, g) in enumerate(jobs):
                    if n < n_c:
                        pe.wait_ge(c_loaded[g // 2], 16)
                    else:
                        pe.wait_ge(u_dve_ready, (2 * g + 2) - (g + 1) // 2)
                        ge(pe, u_pool_ready, (g + 1) // 2)
                    if n >= 4:
                        pe.wait_ge(lo_ready, n - 3)
                    for k in range(KD):
                        for j in range(2):
                            last = pe.transpose(banks[n % 4][:, (2 * k + j) * P:(2 * k + j + 1) * P],
                                                src[:, 2 * g + j, k * P:(k + 1) * P], m.ident[:, :])
                    last.then_inc(turned, 1)
                    if experts is not None and g >= 1:
                        logits_of(g - 1)
                if experts is not None:
                    logits_of(NT // 2 - 1)


def make_constants(pool, m, step, ready):
    pool.memset(m.ident[:, :], 0.0).then_inc(step, 1)
    pool.memset(m.masks[:, :, :], 0.0).then_inc(step, 1)
    pool.memset(m.consts[:, 0:1], 1.0).then_inc(step, 1)
    pool.memset(m.consts[:, 1:2], Q_SCALE).then_inc(step, 1)
    n = 4
    for tile, q_step, k_step, compare, fill in (
            (m.ident[:, :], 1, -1, ALU.not_equal, 1.0),
            (m.masks[:, LOW, :], -1, 1, ALU.is_ge, MASKED),
            (m.masks[:, UP, :], 1, -1, ALU.is_ge, MASKED)):
        pool.wait_ge(step, n)
        pool.affine_select(out=tile, in_=tile, compare_op=compare, fill=fill, base=0, pattern=[[k_step, P]],
                           channel_multiplier=q_step).then_inc(step, 1)
        n += 1
    pool.wait_ge(step, n)
    pool.memset(m.one[:, :], 1.0).then_inc(ready, 1)


def attention(nc, m, tag, weights, blocks_of, bo=None):
    biased = weights.biases is not None
    seen = [blocks_of(j) for j in range(TPB)]
    first_key = [s[0][0] for s in seen]
    width = [P * len(s) for s in seen]
    place = list(range(TPB))[::-1]
    turns = []
    for i in range(TPB):
        turns += [(i, (0, 1))] if 2 * width[place[i]] <= BANK else [(i, (0,)), (i, (1,))]
    t_of = [[q for q, (ii, _) in enumerate(turns) if ii == i] for i in range(TPB)]
    NTURN = len(turns)
    narrow_first = len(t_of[0]) < len(t_of[1])
    order = [("S", 0), ("Q", 0), ("S", 1), ("K", 0), ("PVB", 0)] + [("T", q) for q in t_of[0]] + \
            [("S", 2), ("S", 3)] + [("T", q) for q in t_of[1]] + \
            [("VT", 0), ("O", 0), ("O", 1), ("VR", 0), ("PVA", 0)] + [("T", q) for q in t_of[2] + t_of[3]]
    ring_jobs = [o for o in order if o[0] in ("Q", "K", "VT", "VR", "T", "O")]
    RING = 3
    assert len(ring_jobs) % RING == 0
    next_item, ends_before = ("Q", "K", "VT", "VR"), ("PVB", "O")

    with ExitStack() as ctx:
        sb = lambda n, s, d: ctx.enter_context(nc.sbuf_tensor(f"{tag}_{n}", s, d))
        make = ctx.enter_context(cleared_semaphores(nc))
        sem = lambda n: make(f"{tag}_{n}")
        w_stage, wo_stage, b_stage = weights.w, weights.wo, weights.b
        w_hi, w_lo = sb("w_hi", [P, 3, KD, P], F32R), sb("w_lo", [P, 3, KD, P], F32R)
        wo_hi, wo_lo = sb("wo_hi", [P, D], F32R), sb("wo_lo", [P, D], F32R)
        bqk, bvz = sb("bqk", [P, 2], F32), sb("bvz", [P, 1], F32)
        q_hi, q_lo = sb("q_hi", [P, 2, S], F32R), sb("q_lo", [P, 2, S], F32R)
        k_hi, k_lo = sb("k_hi", [P, 2, S], F32R), sb("k_lo", [P, 2, S], F32R)
        vT = sb("vT", [P, S], F32)
        v_hi, v_lo = sb("v_hi", [P, 2, TPB, 3, DH], F32R), sb("v_lo", [P, 2, TPB, 3, DH], F32R)
        probs = sb("probs", [P, TPB, 2, S], F32)
        negmax, sums, rsum = sb("negmax", [P, TPB, 2], F32), sb("sums", [P, TPB, 2], F32), sb("rsum", [P, TPB, 2], F32)
        pT_hi, pT_lo = (sb(n, [P, 2, 2, TPB, 2 * P], F32R) for n in ("pT_hi", "pT_lo"))
        z_hi, z_lo = sb("z_hi", [P, S], F32R), sb("z_lo", [P, S], F32R)
        o_sb = sb("o_sb", [P, 2, BANK], F32)
        s_ps = [ctx.enter_context(nc.psum_tensor(f"{tag}_s{i}", [P, 2, BANK], F32)) for i in range(2)]
        ring = [ctx.enter_context(nc.psum_tensor(f"{tag}_ring{i}", [P, BANK], F32)) for i in range(RING)]
        z_ps = ctx.enter_context(nc.psum_tensor(f"{tag}_z", [P, BANK], F32))

        w_loaded, wo_loaded, b_loaded = weights.w_loaded, weights.wo_loaded, weights.b_loaded
        bo_added = sem("bo_added")
        w_step, w_ready, wo_step, wo_ready = sem("w_step"), sem("w_ready"), sem("wo_step"), sem("wo_ready")
        dve_step, bqk_ready, bvz_ready, zeroed, o_read = sem("dve_step"), sem("bqk_ready"), sem("bvz_ready"), sem("zeroed"), sem("o_read")
        s_done, q_done, k_done, vt_done, vr_done = sem("s_done"), sem("q_done"), sem("k_done"), sem("vt_done"), sem("vr_done")
        t_done, pva_done, pvb_done, o_done = sem("t_done"), sem("pva_done"), sem("pvb_done"), sem("o_done")
        max_ready, exp_ready, rsum_ready, norm_ready = sem("max_ready"), sem("exp_ready"), sem("rsum_ready"), sem("norm_ready")
        masked, norm0_ready = sem("masked"), sem("norm0_ready")
        q_hi_ready, k_hi_ready, vT_ready, v_hi_ready = sem("q_hi_ready"), sem("k_hi_ready"), sem("vT_ready"), sem("v_hi_ready")
        q_ready, k_ready, v_ready = sem("q_ready"), sem("k_ready"), sem("v_ready")
        pT_hi_ready, pT_ready, z_hi_ready, z_ready, x_added = \
            sem("pT_hi_ready"), sem("pT_ready"), sem("z_hi_ready"), sem("z_ready"), sem("x_added")

        def per_item(p, b, n, c):
            return p * (B * n) + (b * n + c)

        def ran(kind, p, b):
            if isinstance(p, int):
                it = B * p + b
                if it < 0:
                    return kind in next_item
                if it == 0:
                    return kind not in ends_before
                if it == B * NP - 1:
                    return kind not in next_item
                if it == B * NP:
                    return kind in ends_before
            return True

        def bank_of(kind, q):
            return ring[ring_jobs.index((kind, q)) % RING]

        def wait_bank_free(pe, kind, q, p, b):
            k, bb = ring_jobs.index((kind, q)), b
            while True:
                k -= RING
                if k < 0:
                    k, bb = k + len(ring_jobs), bb - 1
                if isinstance(p, int) and B * p + bb < -1:
                    return
                kk, qq = ring_jobs[k]
                if ran(kk, p, bb):
                    break
            sem, n, c = {"Q": (q_ready, 1, 2), "K": (k_ready, 1, 2), "VT": (vT_ready, 1, 2), "VR": (v_ready, 1, 2),
                         "T": (pT_ready, NTURN, qq + 1), "O": (o_read, 2, qq - 1)}[kk]
            pe.wait_ge(sem, per_item(p, bb, n, c))

        def turned_from(q):
            i, hs = turns[q]
            j = place[i]
            return bank_of("T", q)[:, 0:width[j] * len(hs)].rearrange(
                "p (h t n) -> p h t n", h=len(hs), n=P)

        def turned_into(half, q):
            i, hs = turns[q]
            j = place[i]
            k0, n = first_key[j], width[j] // P
            return half[:, j // 2, hs[0]:hs[-1] + 1, k0:k0 + n, P * (j % 2):P * (j % 2) + P]

        with nc.Block() as block:
            @block.sync
            def _(sp):
                with sp.Fori(1, NP) as p:
                    sp.wait_ge(wo_ready, p * 1)
                    if biased:
                        sp.wait_ge(bvz_ready, p * 1)
                    weights.load(sp, p)

            @block.gpsimd
            def _(pool):
                for half in (v_hi, v_lo):
                    for i in range(2):
                        pool.memset(as_f32(half[:, i, :, 1, :]), 0.0).then_inc(zeroed, 1)

                one, scale = (m.consts[:, i:i + 1] for i in range(2))

                def split_w(i, p):
                    done = {0: q_done, 1: k_done, 2: vt_done}[i]
                    if i == 0:
                        pool.wait_ge(w_loaded, p * (16 * weights.dmas) + 16 * weights.dmas)
                    ge(pool, done, per_item(p, 0, 1, 0))
                    w = w_stage[:, i, :, :].rearrange("p k n -> p (k n)")
                    hi, lo = (half[:, i, :, :].rearrange("p k n -> p (k n)") for half in (w_hi, w_lo))
                    steps = p * 4 + (i + 1 if i else 0)
                    if i == 0:
                        pool.tensor_tensor(w, w, scale.to_broadcast([P, KD * P]), ALU.mult).then_inc(w_step, 1)
                        pool.wait_ge(w_step, steps + 1)
                        steps = steps + 1
                    pool.tensor_tensor(hi, w, one.to_broadcast([P, KD * P]), ALU.mult).then_inc(w_step, 1)
                    pool.wait_ge(w_step, steps + 1)
                    pool.tensor_tensor(lo, w, as_f32(hi), ALU.subtract).then_inc(w_ready, 1)

                def split_wo(p):
                    pool.wait_ge(wo_loaded, p * 16 + 16)
                    ge(pool, o_done, per_item(p, 0, 2, 0))
                    pool.tensor_tensor(wo_hi[:, :], wo_stage[:, :], one.to_broadcast([P, D]), ALU.mult).then_inc(wo_step, 1)
                    pool.wait_ge(wo_step, p * 1 + 1)
                    pool.tensor_tensor(wo_lo[:, :], wo_stage[:, :], as_f32(wo_hi[:, :]), ALU.subtract).then_inc(wo_ready, 1)

                def norm_of(i, p, b):
                    j = place[i]
                    pool.wait_ge(rsum_ready, per_item(p, b, TPB, i + 1))
                    for h in range(2):
                        tile = probs[:, j, h, 0:width[j]]
                        pool.tensor_tensor(tile, tile, rsum[:, j, h:h + 1].to_broadcast([P, width[j]]), ALU.mult) \
                            .then_inc(norm_ready, 1)

                def x_of(a, p, b):
                    pool.wait_ge(o_read, per_item(p, b, 2, a - 1))
                    ge(pool, x_added, per_item(p, b, 2, a - 3))
                    t0 = TPB * ((b - 1) % B) + 2 * a
                    rows = m.x[:, t0:t0 + 2, :].rearrange("p t d -> p (t d)")
                    pool.tensor_tensor(rows, rows, o_sb[:, a, :], ALU.add).then_inc(x_added, 1)

                def body(p):
                    for b in range(B):
                        if b == B - 2 and ran("Q", p, b + 1):
                            split_w(0, p + 1)
                            split_w(1, p + 1)
                        norm_of(1, p, b)
                        norm_of(2, p, b)
                        norm_of(3, p, b)
                        if b == B - 2 and ran("Q", p, b + 1):
                            split_w(2, p + 1)
                        if bo is not None and isinstance(p, int) and p == 0:
                            for t in range(TPB * b, TPB * b + TPB):
                                pool.tensor_tensor(m.x[:, t, :], m.x[:, t, :], bo[:, :], ALU.add).then_inc(bo_added, 1)
                            pool.wait_ge(bo_added, TPB * b + TPB)
                        if ran("O", p, b):
                            if b == 0:
                                split_wo(p)
                            x_of(0, p, b)
                            x_of(1, p, b)

                for i in range(3):
                    split_w(i, 0)
                split_wo(0)
                body(0)
                with pool.Fori(1, NP - 1) as p:
                    body(p)
                body(NP - 1)
                x_of(0, NP, 0)
                x_of(1, NP, 0)

            @block.scalar
            def _(act):
                def copy_hi(dst, src, bias, done):
                    if bias is None:
                        act.activation(dst, src, ACT.Copy).then_inc(done, 1)
                    else:
                        act.activation(dst, src, ACT.Identity, bias=bias).then_inc(done, 1)

                def q_of(p, b):
                    act.wait_ge(q_done, per_item(p, b, 1, 2))
                    if biased and (b == B - 1 or b == -1):
                        act.wait_ge(bqk_ready, (p + (1 if b == B - 1 else 0)) * 1 + 1)
                    copy_hi(q_hi[:, (b + 1) % 2, :], bank_of("Q", 0)[:, :], bqk[:, 0:1] if biased else None, q_hi_ready)

                def k_of(p, b):
                    act.wait_ge(k_done, per_item(p, b, 1, 2))
                    copy_hi(k_hi[:, (b + 1) % 2, :], bank_of("K", 0)[:, :], bqk[:, 1:2] if biased else None, k_hi_ready)

                def vt_of(p, b):
                    act.wait_ge(vt_done, per_item(p, b, 1, 2))
                    act.activation(vT[:, :], bank_of("VT", 0)[:, :], ACT.Copy).then_inc(vT_ready, 1)

                def vr_of(p, b):
                    act.wait_ge(vr_done, per_item(p, b, 1, 2))
                    act.activation(v_hi[:, (b + 1) % 2, :, 0:3:2, :],
                                   bank_of("VR", 0)[:, :].rearrange("p (t h e) -> p t h e", t=TPB, h=2),
                                   ACT.Copy).then_inc(v_hi_ready, 1)

                def exp_of(i, p, b):
                    j = place[i]
                    act.wait_ge(max_ready, per_item(p, b, TPB, i + 1))
                    ge(act, t_done, per_item(p, b, NTURN, t_of[i][-1] + 1 - NTURN))
                    for h in range(2):
                        act.activation(probs[:, j, h, 0:width[j]], s_ps[i % 2][:, h, 0:width[j]], ACT.Exp,
                                       bias=negmax[:, j, h:h + 1], accum_out=sums[:, j, h:h + 1]) \
                            .then_inc(exp_ready, 1)

                def z_of(p, b):
                    act.wait_ge(pvb_done, per_item(p, b, 1, 0))
                    if biased and b == 1:
                        act.wait_ge(bvz_ready, p * 1 + 1)
                    copy_hi(z_hi[:, :], z_ps[:, :], bvz[:, 0:1] if biased else None, z_hi_ready)

                def turn_of(q, p, b):
                    act.wait_ge(t_done, per_item(p, b, NTURN, q + 1))
                    act.activation(turned_into(pT_hi, q), turned_from(q), ACT.Copy).then_inc(pT_hi_ready, 1)

                def o_of(a, p, b):
                    act.wait_ge(o_done, per_item(p, b, 2, a - 1))
                    ge(act, x_added, per_item(p, b, 2, a - 3))
                    act.activation(o_sb[:, a, :], bank_of("O", a)[:, :], ACT.Copy).then_inc(o_read, 1)

                def body(p):
                    for b in range(B):
                        on = lambda kind: ran(kind, p, b)
                        if on("Q"):
                            q_of(p, b)
                        exp_of(0, p, b)
                        if on("Q"):
                            k_of(p, b)
                        exp_of(1, p, b)
                        for q in t_of[0]:
                            turn_of(q, p, b)
                        if on("PVB"):
                            z_of(p, b)
                        for q in t_of[1]:
                            turn_of(q, p, b)
                        if on("VT") and not narrow_first:
                            vt_of(p, b)
                        exp_of(2, p, b)
                        if on("VT") and narrow_first:
                            vt_of(p, b)
                        exp_of(3, p, b)
                        if on("O"):
                            o_of(0, p, b)
                            o_of(1, p, b)
                        if on("VR"):
                            vr_of(p, b)
                        for q in t_of[2] + t_of[3]:
                            turn_of(q, p, b)

                q_of(0, -1), k_of(0, -1), vt_of(0, -1), vr_of(0, -1)
                body(0)
                with act.Fori(1, NP - 1) as p:
                    body(p)
                body(NP - 1)
                z_of(NP, 0)
                o_of(0, NP, 0)
                o_of(1, NP, 0)

            @block.vector
            def _(dve):
                chain = Chain(dve, dve_step)

                def statistics_of(b):
                    dve.wait_ge(x_added, B * 2 * (NP - 1) + 2 * b + 2)
                    batch_statistics(dve, chain, m, b)

                def bias_qk(p):
                    dve.wait_ge(b_loaded, p * 48 + 48)
                    ge(dve, k_ready, per_item(p, 0, 1, 0))
                    dve.tensor_scalar(bqk[:, 0:1], b_stage[:, 0:1], Q_SCALE, None, ALU.mult)
                    dve.tensor_copy(bqk[:, 1:2], b_stage[:, 1:2]).then_inc(bqk_ready, 1)

                def bias_v(p):
                    dve.wait_ge(b_loaded, p * 48 + 48)
                    ge(dve, z_ready, per_item(p, 0, 1, 0))
                    dve.tensor_copy(bvz[:, :], b_stage[:, 2:3]).then_inc(bvz_ready, 1)

                def sub_hi(dst, src, bias, hi, done):
                    if bias is None:
                        dve.tensor_tensor(dst, src, as_f32(hi), ALU.subtract).then_inc(done, 1)
                    else:
                        dve.scalar_tensor_tensor(dst, src, bias, as_f32(hi), ALU.add, ALU.subtract).then_inc(done, 1)

                def q_of(p, b):
                    dve.wait_ge(q_hi_ready, per_item(p, b, 1, 2))
                    sub_hi(q_lo[:, (b + 1) % 2, :], bank_of("Q", 0)[:, :], bqk[:, 0:1] if biased else None,
                           q_hi[:, (b + 1) % 2, :], q_ready)

                def k_of(p, b):
                    dve.wait_ge(k_hi_ready, per_item(p, b, 1, 2))
                    sub_hi(k_lo[:, (b + 1) % 2, :], bank_of("K", 0)[:, :], bqk[:, 1:2] if biased else None,
                           k_hi[:, (b + 1) % 2, :], k_ready)

                def vr_of(p, b):
                    dve.wait_ge(v_hi_ready, per_item(p, b, 1, 2))
                    sub_hi(v_lo[:, (b + 1) % 2, :, 0:3:2, :],
                           bank_of("VR", 0)[:, :].rearrange("p (t h e) -> p t h e", t=TPB, h=2), None,
                           v_hi[:, (b + 1) % 2, :, 0:3:2, :], v_ready)

                def max_of(i, p, b):
                    j = place[i]
                    dve.wait_ge(s_done, per_item(p, b, TPB, i + 1))
                    edges = [n for n, (_, kind) in enumerate(seen[j]) if kind is not None]
                    kinds = [seen[j][n][1] for n in edges]
                    tiles = s_ps[i % 2][:, :, 0:width[j]].rearrange("p h (t n) -> p h t n", n=P)
                    tiles = tiles[:, :, edges[0]:edges[-1] + 1:max(1, edges[-1] - edges[0]), :]
                    mask = m.masks[:, kinds[0]:kinds[-1] + 1, :].rearrange("p (a k) n -> p a k n", a=1) \
                        .to_broadcast([P, 2, len(kinds), P])
                    dve.tensor_tensor(tiles, tiles, mask, ALU.add).then_inc(masked, 1)
                    dve.wait_ge(masked, per_item(p, b, TPB, i + 1))
                    dve.tensor_reduce(negmax[:, j, :], s_ps[i % 2][:, :, 0:width[j]], AX.X, ALU.max,
                                      negate=True).then_inc(max_ready, 1)

                def rsum_of(i, p, b):
                    dve.wait_ge(exp_ready, per_item(p, b, 2 * TPB, 2 * i + 2))
                    dve.reciprocal(rsum[:, place[i], :], sums[:, place[i], :]).then_inc(rsum_ready, 1)

                def norm_first(p, b):
                    j = place[0]
                    dve.wait_ge(rsum_ready, per_item(p, b, TPB, 1))
                    for h in range(2):
                        tile = probs[:, j, h, 0:width[j]]
                        dve.tensor_scalar(tile, tile, rsum[:, j, h:h + 1], None, ALU.mult).then_inc(norm0_ready, 1)

                def z_of(p, b):
                    dve.wait_ge(z_hi_ready, per_item(p, b, 1, 0))
                    sub_hi(z_lo[:, :], z_ps[:, :], bvz[:, 0:1] if biased else None, z_hi[:, :], z_ready)

                def turn_of(q, p, b):
                    dve.wait_ge(pT_hi_ready, per_item(p, b, NTURN, q + 1))
                    dve.tensor_tensor(turned_into(pT_lo, q), turned_from(q), as_f32(turned_into(pT_hi, q)),
                                      ALU.subtract).then_inc(pT_ready, 1)

                def body(p):
                    for b in range(B):
                        on = lambda kind: ran(kind, p, b)
                        max_of(0, p, b)
                        if on("Q"):
                            q_of(p, b)
                        max_of(1, p, b)
                        rsum_of(0, p, b)
                        norm_first(p, b)
                        if on("Q"):
                            k_of(p, b)
                        rsum_of(1, p, b)
                        for q in t_of[0]:
                            turn_of(q, p, b)
                        if on("PVB"):
                            z_of(p, b)
                            if b == 0 and biased:
                                bias_v(p)
                        if narrow_first:
                            max_of(2, p, b)
                        for q in t_of[1]:
                            turn_of(q, p, b)
                        if not narrow_first:
                            max_of(2, p, b)
                        max_of(3, p, b)
                        rsum_of(2, p, b)
                        rsum_of(3, p, b)
                        if b == B - 2 and biased and ran("Q", p, b + 1):
                            bias_qk(p + 1)
                        if on("VR"):
                            vr_of(p, b)
                        for q in t_of[2] + t_of[3]:
                            turn_of(q, p, b)
                        if isinstance(p, int) and p == NP - 1 and b >= 2:
                            statistics_of(b - 2)
                            if b == B - 1:
                                statistics_of(b - 1)

                if biased:
                    bias_qk(0)
                    bias_v(0)
                q_of(0, -1), k_of(0, -1), vr_of(0, -1)
                body(0)
                with dve.Fori(1, NP - 1) as p:
                    body(p)
                body(NP - 1)
                z_of(NP, 0)
                statistics_of(B - 1)
                chain.wait()

            @block.tensor
            def _(pe):
                def project(kind, i, hi, lo, p, b):
                    wait_bank_free(pe, kind, 0, p, b)
                    cols = slice(S * ((b + 1) % B), S * ((b + 1) % B) + S)
                    out = bank_of(kind, 0)
                    n = 0
                    for k in range(KD):
                        for w, a in ((w_hi, hi), (w_hi, lo), (w_lo, hi)):
                            last = pe.matmul(out[:, :], w[:, i, k, :], a[:, k, cols], start=(n == 0), stop=(n == 5))
                            n += 1
                    return last

                def q_of(p, b):
                    pe.wait_ge(w_ready, (p + (1 if b == B - 1 else 0)) * 3 + 1)
                    project("Q", 0, m.uT_hi, m.uT_lo, p, b).then_inc(q_done, 1)

                def k_of(p, b):
                    pe.wait_ge(w_ready, (p + (1 if b == B - 1 else 0)) * 3 + 2)
                    project("K", 1, m.cT_hi, m.cT_lo, p, b).then_inc(k_done, 1)

                def vt_of(p, b):
                    pe.wait_ge(w_ready, (p + (1 if b == B - 1 else 0)) * 3 + 3)
                    project("VT", 2, m.cT_hi, m.cT_lo, p, b).then_inc(vt_done, 1)

                def vr_of(p, b):
                    wait_bank_free(pe, "VR", 0, p, b)
                    pe.wait_ge(vT_ready, per_item(p, b, 1, 2))
                    for t in range(TPB):
                        last = pe.transpose(bank_of("VR", 0)[:, P * t:P * t + P], vT[:, P * t:P * t + P], m.ident[:, :])
                    last.then_inc(vr_done, 1)

                def scores(i, p, b):
                    j = place[i]
                    if i == 0:
                        pe.wait_ge(q_ready, per_item(p, b, 1, 1))
                        pe.wait_ge(k_ready, per_item(p, b, 1, 1))
                    ge(pe, exp_ready, per_item(p, b, 2 * TPB, 2 * i - 2))
                    cols = slice(P * first_key[j], P * first_key[j] + width[j])
                    for n, (q, k) in enumerate(((q_hi, k_hi), (q_hi, k_lo), (q_lo, k_hi))):
                        for h in range(2):
                            rows = slice(DH * h, DH * h + DH)
                            last = pe.matmul(s_ps[i % 2][:, h, 0:width[j]], q[rows, b % 2, P * j:P * j + P],
                                             k[rows, b % 2, cols], start=(n == 0), stop=(n == 2))
                    last.then_inc(s_done, 1)

                def turn(q, p, b):
                    i, hs = turns[q]
                    j = place[i]
                    wait_bank_free(pe, "T", q, p, b)
                    if i == 0:
                        pe.wait_ge(norm0_ready, per_item(p, b, 2, hs[-1] + 1))
                    else:
                        pe.wait_ge(norm_ready, per_item(p, b, 2 * (TPB - 1), 2 * (i - 1) + hs[-1] + 1))
                    n = 0
                    for h in hs:
                        for t in range(width[j] // P):
                            last = pe.transpose(bank_of("T", q)[:, P * n:P * n + P], probs[:, j, h, P * t:P * t + P],
                                                m.ident[:, :])
                            n += 1
                    last.then_inc(t_done, 1)

                def values(g, i, opens):
                    spans = []
                    for t in range(TPB):
                        js = [j for j in (2 * g, 2 * g + 1) if t in [x[0] for x in seen[j]]]
                        if js:
                            spans.append((t, js))
                    todo = [(h, t, js, w, a) for h in range(2) for t, js in spans
                            for w, a in ((v_hi, pT_hi), (v_hi, pT_lo), (v_lo, pT_hi))]
                    both = [x for x in todo if len(x[2]) == 2]
                    todo = both[:1] + [x for x in todo if len(x[2]) == 1] + both[1:]
                    for n, (h, t, js, w, a) in enumerate(todo):
                        c0, c1 = P * (js[0] % 2), P * (js[-1] % 2) + P
                        last = pe.matmul(z_ps[:, 2 * P * g + c0:2 * P * g + c1],
                                         w[:, i, t, h:h + 2, :], a[:, g, h, t, c0:c1],
                                         start=(opens and n == 0), stop=(n == len(todo) - 1),
                                         skip_group_check=True)
                    return last

                def pva(p, b):
                    pe.wait_ge(pT_ready, per_item(p, b, NTURN, t_of[1][-1] + 1))
                    pe.wait_ge(v_ready, per_item(p, b, 1, 1))
                    ge(pe, z_ready, per_item(p, b, 1, 0))
                    values(place[0] // 2, b % 2, True).then_inc(pva_done, 1)

                def pvb(p, b):
                    pe.wait_ge(pT_ready, per_item(p, b, NTURN, 0))
                    values(place[2] // 2, (b - 1) % 2, False).then_inc(pvb_done, 1)

                def out_of(a, p, b):
                    wait_bank_free(pe, "O", a, p, b)
                    if a == 0:
                        pe.wait_ge(z_ready, per_item(p, b, 1, 0))
                        pe.wait_ge(wo_ready, p + (0 if b == 0 else 1))
                    out = bank_of("O", a)
                    n = 0
                    for t in range(2):
                        cols = slice(P * (2 * a + t), P * (2 * a + t) + P)
                        for z, w in ((z_hi, wo_hi), (z_hi, wo_lo), (z_lo, wo_hi)):
                            last = pe.matmul(out[:, D * t:D * t + D], z[:, cols], w[:, :], start=(n == 0),
                                             stop=(n == 5), skip_group_check=True)
                            n += 1
                    last.then_inc(o_done, 1)

                def body(p):
                    for b in range(B):
                        for kind, q in order:
                            if not ran(kind, p, b):
                                continue
                            if kind == "S":
                                scores(q, p, b)
                            elif kind == "PVB":
                                pvb(p, b)
                            elif kind == "PVA":
                                pva(p, b)
                            elif kind == "Q":
                                q_of(p, b)
                            elif kind == "K":
                                k_of(p, b)
                            elif kind == "VT":
                                vt_of(p, b)
                            elif kind == "VR":
                                vr_of(p, b)
                            elif kind == "T":
                                turn(q, p, b)
                            else:
                                out_of(q, p, b)

                pe.wait_ge(zeroed, 4)
                q_of(0, -1), k_of(0, -1), vt_of(0, -1), vr_of(0, -1)
                body(0)
                with pe.Fori(1, NP - 1) as p:
                    body(p)
                body(NP - 1)
                pvb(NP, 0)
                out_of(0, NP, 0)
                out_of(1, NP, 0)



def gates(nc, m, g):
    with ExitStack() as ctx:
        sb = lambda n, s, d: ctx.enter_context(nc.sbuf_tensor(f"gate_{n}", s, d))
        make = ctx.enter_context(cleared_semaphores(nc))
        sem = lambda n: make(f"gate_{n}")
        logit = sb("logit", [P, NT, E], F32)
        names = ("eq", "cand", "first", "rest", "eq2", "cand2", "second", "g1", "g2")
        v = {n: sb(n, [P, NT, E], F32) for n in names}
        c = {n: sb(n, [P, NT], F32) for n in ("m1", "i1", "m2", "i2", "gap", "ex", "one_ex", "p1", "p2")}
        down = sb("down", [P, E], F32)
        combT = sb("combT", [E, TOK], F32)
        banks = [ctx.enter_context(nc.psum_tensor(f"gate_ps{i}", [P, BANK], F32)) for i in range(2)]
        combT_ps = ctx.enter_context(nc.psum_tensor("gate_cT", [P, TOK], F32))
        iota_ready, dve_step = sem("iota_ready"), sem("dve_step")
        rows_turned, rows_read = sem("rows_turned"), sem("rows_read")
        gap_ready, ex_ready, comb_ready = sem("gap_ready"), sem("ex_ready"), sem("comb_ready")
        comb_turned, combT_ready, bias_done, bias_added = \
            sem("comb_turned"), sem("combT_ready"), sem("bias_done"), sem("bias_added")
        NJ = NT // 2

        with nc.Block() as block:
            @block.gpsimd
            def _(pool):
                pool.iota(down[:, :], pattern=[[-1, E]], base=E, channel_multiplier=0,
                          allow_small_or_imprecise_dtypes=True).then_inc(iota_ready, 1)

            @block.scalar
            def _(act):
                act.wait_ge(rows_turned, 1)
                act.activation(g.columns[:, :], combT_ps[:, 0:g.rows.shape[0]], ACT.Copy).then_inc(rows_read, 1)
                act.wait_ge(gap_ready, 1)
                act.activation(c["ex"][:, :], c["gap"][:, :], ACT.Exp).then_inc(ex_ready, 1)
                for b in range(B):
                    act.wait_ge(comb_turned, b + 1)
                    act.activation(combT[:, b * S:(b + 1) * S], combT_ps[0:E, b * S:(b + 1) * S], ACT.Copy) \
                        .then_inc(combT_ready, 1)

            @block.vector
            def _(dve):
                chain = Chain(dve, dve_step)

                def step(instruction):
                    chain.inc(instruction)
                    chain.wait()

                def over_experts(col):
                    return col[:, :].rearrange("p (t a) -> p t a", a=1).to_broadcast([P, NT, E])

                def over_tokens(row):
                    return row[:, :].rearrange("p (a e) -> p a e", a=1).to_broadcast([P, NT, E])

                dve.wait_ge(iota_ready, 1)
                step(dve.tensor_tensor(logit[:, :, :], g.logit_ps[:, 0:NT * E].rearrange("p (t e) -> p t e", e=E),
                                       over_experts(g.root_u), ALU.mult))
                step(dve.tensor_reduce(c["m1"][:, :], logit[:, :, :], AX.X, ALU.max))
                step(dve.tensor_tensor(v["eq"][:, :, :], logit[:, :, :], over_experts(c["m1"]), ALU.is_equal))
                step(dve.tensor_tensor(v["cand"][:, :, :], v["eq"][:, :, :], over_tokens(down), ALU.mult))
                step(dve.tensor_reduce(c["i1"][:, :], v["cand"][:, :, :], AX.X, ALU.max))
                step(dve.tensor_tensor(v["first"][:, :, :], v["cand"][:, :, :], over_experts(c["i1"]), ALU.is_equal))
                step(dve.scalar_tensor_tensor(v["rest"][:, :, :], v["first"][:, :, :], -3.0e38, logit[:, :, :],
                                              ALU.mult, ALU.add))
                step(dve.tensor_reduce(c["m2"][:, :], v["rest"][:, :, :], AX.X, ALU.max))
                step(dve.tensor_tensor(v["eq2"][:, :, :], v["rest"][:, :, :], over_experts(c["m2"]), ALU.is_equal))
                step(dve.tensor_tensor(v["cand2"][:, :, :], v["eq2"][:, :, :], over_tokens(down), ALU.mult))
                step(dve.tensor_reduce(c["i2"][:, :], v["cand2"][:, :, :], AX.X, ALU.max))
                step(dve.tensor_tensor(v["second"][:, :, :], v["cand2"][:, :, :], over_experts(c["i2"]), ALU.is_equal))
                dve.tensor_tensor(c["gap"][:, :], c["m2"][:, :], c["m1"][:, :], ALU.subtract).then_inc(gap_ready, 1)
                dve.wait_ge(ex_ready, 1)
                step(dve.tensor_scalar(c["one_ex"][:, :], c["ex"][:, :], 1.0, None, ALU.add))
                step(dve.reciprocal(c["p1"][:, :], c["one_ex"][:, :]))
                step(dve.tensor_tensor(c["p2"][:, :], c["ex"][:, :], c["p1"][:, :], ALU.mult))
                step(dve.tensor_tensor(v["g1"][:, :, :], v["first"][:, :, :], over_experts(c["p1"]), ALU.mult))
                step(dve.tensor_tensor(v["g2"][:, :, :], v["second"][:, :, :], over_experts(c["p2"]), ALU.mult))
                step(dve.tensor_tensor(v["cand"][:, :, :], v["g1"][:, :, :], v["g2"][:, :, :], ALU.add))
                dve.tensor_tensor(g.comb[:, :, :], v["cand"][:, :, :], over_tokens(g.alpha), ALU.mult).then_inc(comb_ready, 1)
                dve.wait_ge(comb_ready, 1)
                dve.tensor_copy(g.comb_e[:, :, :].rearrange("p e t -> p t e"), g.comb[:, :, :])
                for n in range(NJ):
                    dve.wait_ge(bias_done, n + 1)
                    dve.tensor_tensor(m.x[:, 2 * n:2 * n + 2, :], m.x[:, 2 * n:2 * n + 2, :],
                                      banks[n % 2][:, :].rearrange("p (t d) -> p t d", t=2), ALU.add) \
                        .then_inc(bias_added, 1)

            @block.tensor
            def _(pe):
                pe.wait_ge(g.rows_loaded, 48)
                nr = g.rows.shape[0]
                pe.transpose(combT_ps[:, 0:nr], g.rows[:, :], m.ident[0:nr, 0:nr]).then_inc(rows_turned, 1)
                pe.wait_ge(comb_ready, 1)
                pe.wait_ge(rows_read, 1)
                for b in range(B):
                    for t in range(TPB * b, TPB * b + TPB):
                        last = pe.transpose(combT_ps[0:E, P * t:P * t + P], g.comb[:, t, :], m.ident[:, :])
                    last.then_inc(comb_turned, 1)
                for n in range(NJ):
                    if n % 2 == 0:
                        pe.wait_ge(combT_ready, n // 2 + 1)
                    ge(pe, bias_added, n - 1)
                    for t in range(2):
                        cols = slice(P * (2 * n + t), P * (2 * n + t) + P)
                        last = pe.matmul(banks[n % 2][:, D * t:D * t + D], combT[:, cols], g.b2[:, :],
                                         start=(t == 0), stop=(t == 1), skip_group_check=True)
                    last.then_inc(bias_done, 1)


def experts(nc, m, g, w1_dram, w2_dram):
    STEPS = B * NF
    RING = 4
    LASTB = (B - 1) * NF
    with ExitStack() as ctx:
        sb = lambda n, s, d: ctx.enter_context(nc.sbuf_tensor(f"ex_{n}", s, d))
        make = ctx.enter_context(cleared_semaphores(nc))
        sem = lambda n: make(f"ex_{n}")
        w1_stage, w2_stage = g.w1_stage, g.w2_stage
        w1_hi, w1_lo = sb("w1_hi", [P, KD, F], F32R), sb("w1_lo", [P, KD, F], F32R)
        w2_hi, w2_lo = sb("w2_hi", [P, NF, D], F32R), sb("w2_lo", [P, NF, D], F32R)
        lnw, lnb, b1 = sb("lnw", [P, KD], F32), sb("lnb", [P, KD], F32), sb("b1", [P, NF], F32)
        comb = sb("comb", [P, NT], F32)
        a_sb = sb("a", [P, RING, S], F32)
        a_hi, a_lo = sb("a_hi", [P, RING, S], F32R), sb("a_lo", [P, RING, S], F32R)
        h_ps = [ctx.enter_context(nc.psum_tensor(f"ex_h{i}", [P, BANK], F32)) for i in range(2)]
        y_ps = [ctx.enter_context(nc.psum_tensor(f"ex_y{i}", [P, TPB, D], F32)) for i in range(2)]
        b_ps = ctx.enter_context(nc.psum_tensor("ex_b", [P, BANK], F32))

        w1_loaded, w2_loaded = g.w1_loaded, g.w2_loaded
        dve_step = sem("dve_step")
        small_ready, w1_hi_ready, w1_ready, w2_hi_ready, w2_ready = \
            sem("small_ready"), sem("w1_hi_ready"), sem("w1_ready"), sem("w2_hi_ready"), sem("w2_ready")
        bias_done, b1_ready, comb_ready = sem("bias_done"), sem("b1_ready"), sem("comb_ready")
        h_done, a_ready, a_hi_ready, a_lo_ready, y_done, x_added = \
            sem("h_done"), sem("a_ready"), sem("a_hi_ready"), sem("a_lo_ready"), sem("y_done"), sem("x_added")

        def at(e, n, c):
            return e * n + c

        def is_last(e):
            return isinstance(e, int) and e == E - 1

        def is_first(e):
            return isinstance(e, int) and e == 0

        with nc.Block() as block:
            @block.sync
            def _(sp):
                w1_view = w1_dram.rearrange("e (k d) f -> e d k f", k=KD)
                w2_view = w2_dram.rearrange("e (f p) d -> e p f d", p=P)

                with sp.Fori(1, E) as e:
                    sp.wait_ge(w1_ready, at(e, NF, 0))
                    sp.wait_ge(bias_done, at(e, 1, 0))
                    sp.dma_start(w1_stage[:, :, :], w1_view[e]).then_inc(w1_loaded, 16)
                    sp.wait_ge(w2_ready, at(e, NF, 0))
                    sp.dma_start(w2_stage[:, :, :], w2_view[e]).then_inc(w2_loaded, 16)

            @block.gpsimd
            def _(pool):
                def split_w2(e, f):
                    if f == 0:
                        pool.wait_ge(w2_loaded, at(e, 16, 16))
                    if not is_first(e):
                        pool.wait_ge(y_done, at(e, STEPS, LASTB - STEPS + f + 1))
                    one = m.one[:, 0:1].to_broadcast([P, D])
                    pool.tensor_tensor(w2_hi[:, f, :], w2_stage[:, f, :], one, ALU.mult).then_inc(w2_hi_ready, 1)
                    pool.wait_ge(w2_hi_ready, at(e, NF, f + 1))
                    pool.tensor_tensor(w2_lo[:, f, :], w2_stage[:, f, :], as_f32(w2_hi[:, f, :]),
                                       ALU.subtract).then_inc(w2_ready, 1)

                for f in range(NF):
                    split_w2(0, f)
                with pool.Fori(1, E) as e:
                    for f in range(NF):
                        split_w2(e, f)

            @block.scalar
            def _(act):
                def body(e):
                    for s in range(STEPS):
                        if s == 0:
                            act.wait_ge(b1_ready, at(e, 1, 1))
                        act.wait_ge(h_done, at(e, STEPS, s + 1))
                        if not (is_first(e) and s < RING):
                            act.wait_ge(a_lo_ready, at(e, STEPS, s - RING + 1))
                        act.activation(a_sb[:, s % RING, :], h_ps[s % 2][:, :], ACT.Gelu_apprx_tanh,
                                       bias=b1[:, s % NF:s % NF + 1]).then_inc(a_ready, 1)

                body(0)
                with act.Fori(1, E - 1) as e:
                    body(e)
                body(E - 1)

            @block.vector
            def _(dve):
                chain = Chain(dve, dve_step)

                def statistics_of(b):
                    dve.wait_ge(x_added, (E - 1) * NT + TPB * (b + 1))
                    batch_statistics(dve, chain, m, b)

                def small(e):
                    dve.tensor_scalar(lnw[:, :], g.lnw[:, bass.ds(e * KD, KD)], 1.0, None, ALU.mult).then_inc(small_ready, 1)
                    dve.tensor_scalar(lnb[:, :], g.lnb[:, bass.ds(e * KD, KD)], 1.0, None, ALU.mult).then_inc(small_ready, 1)

                def split_w1(e, f):
                    if f == 0:
                        dve.wait_ge(w1_loaded, at(e, 16, 16))
                        dve.wait_ge(small_ready, at(e, 2, 2))
                    if not is_first(e):
                        dve.wait_ge(h_done, at(e, STEPS, LASTB - STEPS + f + 1))
                    cols = slice(P * f, P * f + P)
                    for k in range(KD):
                        dve.tensor_scalar(w1_hi[:, k, cols], w1_stage[:, k, cols], lnw[:, k:k + 1], None,
                                          ALU.mult).then_inc(w1_hi_ready, 1)
                    dve.wait_ge(w1_hi_ready, at(e, KD * NF, KD * (f + 1)))
                    for k in range(KD):
                        last = dve.scalar_tensor_tensor(w1_lo[:, k, cols], w1_stage[:, k, cols], lnw[:, k:k + 1],
                                                        as_f32(w1_hi[:, k, cols]), ALU.mult, ALU.subtract)
                    last.then_inc(w1_ready, 1)

                def bias(e):
                    dve.wait_ge(bias_done, at(e, 1, 1))
                    if not is_first(e):
                        dve.wait_ge(a_ready, at(e, STEPS, 0))
                    dve.tensor_tensor(b1[:, :], b_ps[:, 0:NF], g.fc1b[:, bass.ds(e * NF, NF)], ALU.add).then_inc(b1_ready, 1)

                def halves(e, s):
                    dve.wait_ge(a_ready, at(e, STEPS, s + 1))
                    dve.tensor_copy(a_hi[:, s % RING, :], a_sb[:, s % RING, :]).then_inc(a_hi_ready, 1)
                    dve.wait_ge(a_hi_ready, at(e, STEPS, s + 1))
                    dve.tensor_tensor(a_lo[:, s % RING, :], a_sb[:, s % RING, :], as_f32(a_hi[:, s % RING, :]),
                                      ALU.subtract).then_inc(a_lo_ready, 1)

                def add_y(e, b):
                    dve.wait_ge(y_done, at(e, STEPS, (b + 1) * NF))
                    dve.wait_ge(comb_ready, at(e, 1, 1 if b >= 0 else 0))
                    for t in range(TPB):
                        tile = m.x[:, TPB * (b % B) + t, :]
                        dve.scalar_tensor_tensor(tile, y_ps[b % 2][:, t, :], comb[:, TPB * (b % B) + t:TPB * (b % B) + t + 1],
                                                 tile, ALU.mult, ALU.add).then_inc(x_added, 1)

                def body(e):
                    for s in range(STEPS):
                        halves(e, s)
                        if s >= LASTB and not is_last(e):
                            split_w1(e + 1, s - LASTB)
                        if s % NF == 1 and not (is_first(e) and s == 1):
                            add_y(e, s // NF - 1)
                        if is_last(e) and s % NF == 4 and s > NF:
                            statistics_of(s // NF - 1)
                        if s == 1:
                            if not is_first(e):
                                dve.wait_ge(x_added, at(e, NT, 0))
                            dve.tensor_scalar(comb[:, :], g.comb_e[:, bass.ds(e, 1), :].rearrange("p a t -> p (a t)"),
                                              1.0, None, ALU.mult).then_inc(comb_ready, 1)
                        if s == LASTB - 2 and not is_last(e):
                            dve.wait_ge(bias_done, at(e, 1, 1))
                            dve.wait_ge(w1_ready, at(e, NF, NF))
                            small(e + 1)
                    if not is_last(e):
                        bias(e + 1)

                small(0)
                for f in range(NF):
                    split_w1(0, f)
                bias(0)
                body(0)
                with dve.Fori(1, E - 1) as e:
                    body(e)
                body(E - 1)
                add_y(E, -1)
                statistics_of(B - 1)
                chain.wait()

            @block.tensor
            def _(pe):
                def bias(e):
                    pe.wait_ge(w1_loaded, at(e, 16, 16))
                    pe.wait_ge(small_ready, at(e, 2, 2))
                    if not is_first(e):
                        pe.wait_ge(b1_ready, at(e, 1, 0))
                    for f in range(NF):
                        for k in range(KD):
                            last = pe.matmul(b_ps[:, f:f + 1], w1_stage[:, k, P * f:P * f + P], lnb[:, k:k + 1],
                                             start=(k == 0), stop=(k == KD - 1), skip_group_check=True)
                    last.then_inc(bias_done, 1)

                def hidden(e, s):
                    b, f = s // NF, s % NF
                    if b == 0:
                        pe.wait_ge(w1_ready, at(e, NF, f + 1))
                    if not (is_first(e) and s < 2):
                        pe.wait_ge(a_ready, at(e, STEPS, s - 1))
                    cols = slice(S * b, S * b + S)
                    n = 0
                    for k in range(KD):
                        for w, t in ((w1_hi, m.uT_hi), (w1_hi, m.uT_lo), (w1_lo, m.uT_hi)):
                            last = pe.matmul(h_ps[s % 2][:, :], w[:, k, P * f:P * f + P], t[:, k, cols],
                                             start=(n == 0), stop=(n == 5))
                            n += 1
                    last.then_inc(h_done, 1)

                def output(e, s):
                    b, f = s // NF, s % NF
                    pe.wait_ge(a_lo_ready, at(e, STEPS, s + 1))
                    if b == 0:
                        pe.wait_ge(w2_ready, at(e, NF, f + 1))
                    if f == 0 and not (is_first(e) and b < 2):
                        pe.wait_ge(x_added, at(e, NT, TPB * (b - 1)))
                    for t in range(TPB):
                        cols = slice(P * t, P * t + P)
                        for n, (a, w) in enumerate(((a_hi, w2_hi), (a_hi, w2_lo), (a_lo, w2_hi))):
                            last = pe.matmul(y_ps[b % 2][:, t, :], a[:, s % RING, cols], w[:, f, :],
                                             start=(f == 0 and n == 0 and t % 2 == 0),
                                             stop=(f == NF - 1 and n == 2), skip_group_check=True)
                    last.then_inc(y_done, 1)

                def body(e):
                    for s in range(STEPS):
                        if s + 2 < STEPS:
                            hidden(e, s + 2)
                        elif not is_last(e):
                            hidden(e + 1, s + 2 - STEPS)
                        output(e, s)
                        if s == LASTB and not is_last(e):
                            bias(e + 1)

                bias(0)
                hidden(0, 0)
                hidden(0, 1)
                body(0)
                with pe.Fori(1, E - 1) as e:
                    body(e)
                body(E - 1)


def adapters(nc, m, uT, w):
    N, HD = E, DH
    NC = N * HD // P
    with ExitStack() as ctx:
        sb = lambda n, s, d: ctx.enter_context(nc.sbuf_tensor(f"ad_{n}", s, d))
        make = ctx.enter_context(cleared_semaphores(nc))
        sem = lambda n: make(f"ad_{n}")
        raw = {"base": w.base, "enc": w.enc, "dec": w.dec}
        down, up = w.down, w.up
        hi = {n: sb(n + "_hi", list(t.shape), F32R) for n, t in raw.items()}
        lo = {n: sb(n + "_lo", list(t.shape), F32R) for n, t in raw.items()}
        vec_rows, b_down_rows = w.vec_rows, w.b_down_rows
        vec = sb("vec", [P, 2 * N + NC], F32)
        b_dec, b_enc = vec[:, 0:2 * N], vec[:, 2 * N:2 * N + NC]
        b_down = sb("b_down", [HD, N], F32)
        b_base, b_up, index = w.b_base, w.b_up, w.index
        index_f, falling, rising = sb("index_f", [P, N], F32), sb("falling", [P, N], F32), sb("rising", [P, N], F32)
        h32 = sb("h32", [P, 2, S], F32)
        h_hi, h_lo = sb("h_hi", [P, NC, S], F32R), sb("h_lo", [P, NC, S], F32R)
        diff, square = sb("diff", [P, 2, S], F32), sb("square", [P, S], F32)
        loss = sb("loss", [P, 2 * N], F32)
        names = ("sum8", "eq", "cand", "best", "pick", "chosen")
        v = {n: sb("v_" + n, [P, N], F32) for n in names}
        c = {n: sb("c_" + n, [P, 1], F32) for n in ("low", "first", "adapter", "negative", "wrapped", "least", "most")}
        sel_down, sel_up = sb("sel_down", [P, KD, HD], F32), sb("sel_up", [HD, D], F32)
        sd_hi, sd_lo = sb("sd_hi", [P, KD, HD], F32R), sb("sd_lo", [P, KD, HD], F32R)
        su_hi, su_lo = sb("su_hi", [HD, D], F32R), sb("su_lo", [HD, D], F32R)
        term, sel_b, sel_bd, bd_terms = sb("term", [P, D], F32), sb("sel_b", [P, D], F32), sb("sel_bd", [HD, 1], F32), sb("bd_terms", [HD, N], F32)
        mid, mid_hi, mid_lo = sb("mid", [HD, S], F32), sb("mid_hi", [HD, S], F32R), sb("mid_lo", [HD, S], F32R)
        e_ps = [ctx.enter_context(nc.psum_tensor(f"ad_e{i}", [P, BANK], F32)) for i in range(2)]
        r_ps = [ctx.enter_context(nc.psum_tensor(f"ad_r{i}", [P, BANK], F32)) for i in range(4)]
        o_ps = ctx.enter_context(nc.psum_tensor("ad_o", [P, BANK], F32))
        s_ps = ctx.enter_context(nc.psum_tensor("ad_s", [P, BANK], F32))

        w_loaded, row_loaded, bias_loaded, late_loaded = w.w_loaded, w.row_loaded, w.bias_loaded, w.late_loaded
        iota_ready = sem("iota_ready")
        w_hi_ready, w_ready, rows_turned, vec_ready = sem("w_hi_ready"), sem("w_ready"), sem("rows_turned"), sem("vec_ready")
        enc_done, h32_ready, h_hi_ready, h_ready = sem("enc_done"), sem("h32_ready"), sem("h_hi_ready"), sem("h_ready")
        dec_done, diff_ready, loss_ready, loss_summed = sem("dec_done"), sem("diff_ready"), sem("loss_ready"), sem("loss_summed")
        dve_step, pool_step, chosen_ready, picked, bias_added = \
            sem("dve_step"), sem("pool_step"), sem("chosen_ready"), sem("picked"), sem("bias_added")
        down_done, mid_ready, mid_split, out_done, x_added = \
            sem("down_done"), sem("mid_ready"), sem("mid_split"), sem("out_done"), sem("x_added")

        jobs = [(ch, dh, e) for ch in range(NC) for dh in range(KD) for e in range(2)]
        NJ = len(jobs)

        def out_bank(i):
            return r_ps[i][:, :]

        with nc.Block() as block:
            @block.gpsimd
            def _(pool):
                pool.iota(falling[:, :], pattern=[[-1, N]], base=N, channel_multiplier=0,
                          allow_small_or_imprecise_dtypes=True).then_inc(iota_ready, 1)
                pool.wait_ge(iota_ready, 1)
                pool.iota(rising[:, :], pattern=[[1, N]], base=0, channel_multiplier=0,
                          allow_small_or_imprecise_dtypes=True).then_inc(iota_ready, 1)
                chain = Chain(pool, pool_step)
                pool.wait_ge(iota_ready, 2)
                for b in range(B + 1):
                    if b < B:
                        for ch in range(NC):
                            pool.wait_ge(h32_ready, NC * b + ch + 1)
                            pool.wait_ge(h_hi_ready, NC * b + ch + 1)
                            ge(pool, dec_done, NJ * b)
                            pool.tensor_tensor(h_lo[:, ch, :], h32[:, ch % 2, :], as_f32(h_hi[:, ch, :]),
                                               ALU.subtract).then_inc(h_ready, 1)
                            pool.wait_ge(h_ready, NC * b + ch + 1)
                    if b >= 1:
                        pool.wait_ge(chosen_ready, b)
                        if b == 1:
                            pool.wait_ge(bias_loaded, 48)
                        one = v["chosen"]
                        for n in range(N):
                            chain.inc(pool.tensor_tensor(term[:, :], b_up[:, n, :], one[:, n:n + 1].to_broadcast([P, D]), ALU.mult))
                            chain.wait()
                            chain.inc(pool.tensor_tensor(sel_b[:, :], term[:, :], b_base[:, :] if n == 0 else sel_b[:, :], ALU.add))
                            chain.wait()
                        for t in range(TPB * (b - 1), TPB * b):
                            pool.tensor_tensor(m.x[:, t, :], m.x[:, t, :], sel_b[:, :], ALU.add).then_inc(bias_added, 1)
                            pool.wait_ge(bias_added, t + 1)

            @block.scalar
            def _(act):
                def middle(b):
                    act.wait_ge(down_done, b + 1)
                    act.wait_ge(picked, b + 1)
                    act.activation(mid[:, :], o_ps[0:HD, :], ACT.Relu, bias=sel_bd[:, 0:1]).then_inc(mid_ready, 1)
                    act.activation(mid_hi[:, :], o_ps[0:HD, :], ACT.Relu, bias=sel_bd[:, 0:1]).then_inc(mid_ready, 1)

                act.wait_ge(vec_ready, 2)
                for b in range(B + 1):
                    if b < B:
                        for ch in range(NC):
                            n = NC * b + ch
                            act.wait_ge(enc_done, n + 1)
                            ge(act, h_ready, n - 1)
                            act.activation(h32[:, ch % 2, :], e_ps[ch % 2][:, :], ACT.Relu, bias=b_enc[:, ch:ch + 1]) \
                                .then_inc(h32_ready, 1)
                            act.activation(h_hi[:, ch, :], e_ps[ch % 2][:, :], ACT.Relu, bias=b_enc[:, ch:ch + 1]) \
                                .then_inc(h_hi_ready, 1)
                        for q in range(NJ):
                            ch, dh, e = jobs[q]
                            col = (2 * ch + e) * KD + dh
                            act.wait_ge(diff_ready, NJ * b + q + 1)
                            ge(act, loss_summed, b)
                            ge(act, loss_ready, NJ * b + q)
                            act.activation(square[:, :], diff[:, q % 2, :], ACT.Square,
                                           accum_out=loss[:, col:col + 1]).then_inc(loss_ready, 1)
                    if b >= 1:
                        middle(b - 1)

            @block.vector
            def _(dve):
                chain = Chain(dve, dve_step)

                def step(instruction):
                    chain.inc(instruction)
                    chain.wait()

                dve.wait_ge(w_loaded, 64)
                for i, n in enumerate(("enc", "dec", "base")):
                    dve.tensor_copy(hi[n][:, :, :], raw[n][:, :, :]).then_inc(w_hi_ready, 1)
                    dve.wait_ge(w_hi_ready, i + 1)
                    dve.tensor_tensor(lo[n][:, :, :], raw[n][:, :, :], as_f32(hi[n][:, :, :]),
                                      ALU.subtract).then_inc(w_ready, 1)
                dve.wait_ge(rows_turned, 1)
                dve.tensor_copy(vec[:, :], s_ps[:, 0:2 * N + NC]).then_inc(vec_ready, 1)
                dve.tensor_copy(b_down[:, :], s_ps[0:HD, 64:64 + N]).then_inc(vec_ready, 1)
                dve.wait_ge(vec_ready, 2)
                dve.wait_ge(bias_loaded, 48)
                dve.wait_ge(iota_ready, 2)
                step(dve.tensor_copy(index_f[:, :], index[:, :]))

                def choose(b):
                    dve.wait_ge(loss_summed, b + 1)
                    step(dve.tensor_reduce(v["sum8"][:, :], s_ps[:, 0:2 * N].rearrange("p (n k) -> p n k", k=KD), AX.X, ALU.add))
                    step(dve.tensor_reduce(c["low"][:, :], v["sum8"][:, :], AX.X, ALU.min))
                    step(dve.tensor_scalar(v["eq"][:, :], v["sum8"][:, :], c["low"][:, 0:1], None, ALU.is_equal))
                    step(dve.tensor_tensor(v["cand"][:, :], v["eq"][:, :], falling[:, :], ALU.mult))
                    step(dve.tensor_reduce(c["first"][:, :], v["cand"][:, :], AX.X, ALU.max))
                    step(dve.tensor_scalar(v["best"][:, :], falling[:, :], c["first"][:, 0:1], None, ALU.is_equal))
                    step(dve.tensor_tensor(v["pick"][:, :], v["best"][:, :], index_f[:, :], ALU.mult))
                    step(dve.tensor_reduce(c["adapter"][:, :], v["pick"][:, :], AX.X, ALU.add))
                    step(dve.tensor_scalar(c["negative"][:, :], c["adapter"][:, :], 0.0, float(N), ALU.is_lt, ALU.mult))
                    step(dve.tensor_tensor(c["wrapped"][:, :], c["adapter"][:, :], c["negative"][:, :], ALU.add))
                    step(dve.tensor_scalar(c["most"][:, :], c["wrapped"][:, :], 0.0, float(N - 1), ALU.max, ALU.min))
                    ge(dve, bias_added, TPB * b)
                    dve.tensor_scalar(v["chosen"][:, :], rising[:, :], c["most"][:, 0:1], None, ALU.is_equal) \
                        .then_inc(chosen_ready, 1)
                    dve.wait_ge(chosen_ready, b + 1)
                    chain.inc(dve.tensor_tensor(bd_terms[:, :], b_down[:, :], v["chosen"][0:HD, :], ALU.mult))

                def add_adapter(n):
                    one = v["chosen"]
                    if n == 0:
                        chain.inc(dve.tensor_scalar(sel_down[:, :, :], down[:, :, 0, :], one[:, 0:1], None, ALU.mult))
                        chain.inc(dve.tensor_scalar(sel_up[:, :], up[:, 0, :], one[0:HD, 0:1], None, ALU.mult))
                        return
                    chain.wait()
                    chain.inc(dve.scalar_tensor_tensor(sel_down[:, :, :], down[:, :, n, :], one[:, n:n + 1],
                                                       sel_down[:, :, :], ALU.mult, ALU.add))
                    chain.inc(dve.scalar_tensor_tensor(sel_up[:, :], up[:, n, :], one[0:HD, n:n + 1],
                                                       sel_up[:, :], ALU.mult, ALU.add))

                def halves(b):
                    chain.wait()
                    ge(dve, out_done, 2 * b)
                    ge(dve, mid_ready, 2 * b)
                    chain.inc(dve.tensor_reduce(sel_bd[:, :], bd_terms[:, :], AX.X, ALU.add))
                    chain.inc(dve.tensor_copy(sd_hi[:, :, :], sel_down[:, :, :]))
                    chain.inc(dve.tensor_copy(su_hi[:, :], sel_up[:, :]))
                    chain.wait()
                    chain.inc(dve.tensor_tensor(sd_lo[:, :, :], sel_down[:, :, :], as_f32(sd_hi[:, :, :]), ALU.subtract))
                    dve.tensor_tensor(su_lo[:, :], sel_up[:, :], as_f32(su_hi[:, :]), ALU.subtract).then_inc(picked, 1)

                EARLY = 3
                for b in range(B + 1):
                    if b >= 1:
                        choose(b - 1)
                        if b == 1:
                            dve.wait_ge(late_loaded, 48)
                        for n in range(EARLY):
                            add_adapter(n)
                    for q in range(NJ):
                        if b < B:
                            ch, dh, e = jobs[q]
                            col = (2 * ch + e) * KD + dh
                            dve.wait_ge(dec_done, NJ * b + q + 1)
                            ge(dve, loss_ready, NJ * b + q - 1)
                            dve.scalar_tensor_tensor(diff[:, q % 2, :], r_ps[q % 4][:, :], b_dec[:, col:col + 1],
                                                     uT[:, dh, S * b:S * b + S], ALU.add, ALU.subtract) \
                                .then_inc(diff_ready, 1)
                        if b >= 1:
                            if q < N - EARLY:
                                add_adapter(EARLY + q)
                            if q == N - EARLY:
                                halves(b - 1)
                    if b >= 1:
                        dve.wait_ge(mid_ready, 2 * b)
                        dve.tensor_tensor(mid_lo[:, :], mid[:, :], as_f32(mid_hi[:, :]), ALU.subtract).then_inc(mid_split, 1)
                        dve.wait_ge(bias_added, TPB * b)
                        for i in range(2):
                            dve.wait_ge(out_done, 2 * (b - 1) + i + 1)
                            t = TPB * (b - 1) + 2 * i
                            rows = m.x[:, t:t + 2, :]
                            dve.tensor_tensor(rows, rows, out_bank(i).rearrange("p (t d) -> p t d", t=2),
                                              ALU.add).then_inc(x_added, 1)

            @block.tensor
            def _(pe):
                pe.wait_ge(row_loaded, 48)
                nr = 2 * N + NC
                pe.transpose(s_ps[:, 0:nr], vec_rows[:, :], m.ident[0:nr, 0:nr])
                pe.transpose(s_ps[0:HD, 64:64 + N], b_down_rows[:, :], m.ident[0:N, 0:N]).then_inc(rows_turned, 1)

                def three(out, w_hi, w_lo, b_hi, b_lo, first, last_, **more):
                    pe.matmul(out, w_hi, b_hi, start=first, stop=False, **more)
                    pe.matmul(out, w_hi, b_lo, start=False, stop=False, **more)
                    return pe.matmul(out, w_lo, b_hi, start=False, stop=last_, **more)

                def sum_losses(b):
                    pe.wait_ge(loss_ready, NJ * (b + 1))
                    pe.wait_ge(vec_ready, 2)
                    ge(pe, chosen_ready, b)
                    pe.matmul(s_ps[:, 0:2 * N], m.one[:, :], loss[:, :], start=True, stop=True).then_inc(loss_summed, 1)

                for b in range(B + 1):
                    if b < B:
                        cols = slice(S * b, S * b + S)
                        for ch in range(NC):
                            if b == 0 and ch == 0:
                                pe.wait_ge(w_ready, 1)
                            ge(pe, h_hi_ready, NC * b + ch - 1)
                            for k in range(KD):
                                f = slice(P * ch, P * ch + P)
                                last = three(e_ps[ch % 2][:, :], hi["enc"][:, k, f], lo["enc"][:, k, f],
                                             m.uT_hi[:, k, cols], m.uT_lo[:, k, cols], k == 0, k == KD - 1)
                            last.then_inc(enc_done, 1)
                            if b >= 1 and ch == 0:
                                sum_losses(b - 1)
                        for q in range(0, NJ, 2):
                            ch, dh, _ = jobs[q]
                            if b == 0 and q == 0:
                                pe.wait_ge(w_ready, 2)
                            pe.wait_ge(h_ready, NC * b + ch + 1)
                            ge(pe, diff_ready, NJ * b + q - 2)
                            if b >= 2 and q == 0:
                                pe.wait_ge(x_added, 2 * (b - 1))
                            d = slice(P * dh, P * dh + P)
                            for n, (half, h) in enumerate(((hi, h_hi), (hi, h_lo), (lo, h_hi))):
                                for e in range(2):
                                    rows = slice(HD * e, HD * e + HD)
                                    last = pe.matmul(r_ps[(q + e) % 4][:, :], half["dec"][rows, ch, d], h[rows, ch, :],
                                                     start=(n == 0), stop=(n == 2))
                                    if n == 2:
                                        last.then_inc(dec_done, 1)
                    else:
                        sum_losses(B - 1)
                    if b >= 1:
                        cols = slice(S * (b - 1), S * b)
                        if b == 1:
                            pe.wait_ge(w_ready, 3)
                        for i in range(2):
                            pe.wait_ge(diff_ready, NJ * min(b + 1, B) - 2 + i)
                            if b == B:
                                pe.wait_ge(x_added, 2 * (B - 1))
                            for j in range(2):
                                t = slice(S * (b - 1) + P * (2 * i + j), S * (b - 1) + P * (2 * i + j) + P)
                                for k in range(KD):
                                    three(out_bank(i)[:, D * j:D * j + D], m.uT_hi[:, k, t], m.uT_lo[:, k, t],
                                          hi["base"][:, k, :], lo["base"][:, k, :], j == 0 and k == 0, False,
                                          skip_group_check=True)
                            if i == 0:
                                pe.wait_ge(picked, b)
                                ge(pe, mid_ready, 2 * (b - 1))
                                for k in range(KD):
                                    last = three(o_ps[0:HD, :], sd_hi[:, k, :], sd_lo[:, k, :],
                                                 m.uT_hi[:, k, cols], m.uT_lo[:, k, cols], k == 0, k == KD - 1)
                                last.then_inc(down_done, 1)
                        for i in range(2):
                            if i == 0:
                                pe.wait_ge(mid_split, b)
                            for j in range(2):
                                t = slice(P * (2 * i + j), P * (2 * i + j) + P)
                                last = three(out_bank(i)[:, D * j:D * j + D], mid_hi[:, t], mid_lo[:, t],
                                             su_hi[:, :], su_lo[:, :], False, True, skip_group_check=True)
                            last.then_inc(out_done, 1)


def causal(j):
    return [(t, UP if t == j else None) for t in range(j + 1)]


def banded(j):
    return [(t, {-1: LOW, 0: None, 1: UP}[t - j]) for t in range(max(0, j - 1), min(TPB, j + 2))]


def write_out(nc, m, out_dram):
    with nc.semaphore("stored") as stored:
        with nc.Block() as block:
            @block.sync
            def _(sp):
                for b in range(B):
                    sp.dma_start(out_dram[b * S:(b + 1) * S, :].rearrange("(t p) d -> p t d", p=P),
                                 m.x[:, TPB * b:TPB * b + TPB, :]).then_inc(stored, 16)
                sp.wait_ge(stored, 16 * B)


def program(nc, a, out):
    x_dram = a["x"].rearrange("b s d -> (b s) d")
    ctx_dram = a["ctx_1024"].rearrange("b s d -> (b s) d")
    out_dram = out.rearrange("b s d -> (b s) d")
    with ExitStack() as ctx:
        sb = lambda n, s, d: ctx.enter_context(nc.sbuf_tensor(n, s, d))
        m = Shared(sb)

        def head_major(w):
            view = w.rearrange("(p h) (k d) e -> p h d k e", h=2, k=KD)
            return lambda dst, p: [(dst[:, :, DH * h:DH * h + DH], view[p, h]) for h in range(2)]

        def column_major(w):
            view = w.rearrange("(k d) (p n) -> p d k n", k=KD, n=P)
            return lambda dst, p: [(dst, view[p])]

        def head_bias(w):
            view = w.rearrange("(p h) (e a) -> p (h e) a", h=2, a=1)
            return lambda p: view[p]

        wo0 = a["L0_xattn_W_O"].rearrange("(p h) e d -> p (h e) d", h=2)
        wo1 = a["L1_xattn_Wo"].rearrange("(p n) d -> p n d", n=P)
        with ExitStack() as inner:
            inner_sb = lambda n, shape, dtype: inner.enter_context(nc.sbuf_tensor(n, shape, dtype))
            sem = inner.enter_context(cleared_semaphores(nc))
            weights = PairWeights(inner_sb, sem, "att0", head_major(a["L0_xattn_W_Q"]), head_major(a["L0_xattn_W_K"]),
                                  head_major(a["L0_xattn_W_V"]), lambda p: wo0[p],
                                  [head_bias(a["L0_xattn_" + n]) for n in ("b_Q", "b_K", "b_V")])
            bo, bo_loaded = inner_sb("bo", [P, D], F32), sem("bo_loaded")

            def prefetch(sp):
                weights.load(sp, 0)
                sp.dma_start(bo[:, :], a["L0_xattn_b_O"].rearrange("(a n) -> a n", a=1).to_broadcast([P, D])) \
                    .then_inc(bo_loaded, 16)
                sp.wait_ge(bo_loaded, 16)

            norm_inputs(nc, m, "in0", prefetch, x_dram, ctx_dram)
            attention(nc, m, "att0", weights, causal, bo)
        with ExitStack() as inner:
            g = Experts(lambda n, shape, dtype: inner.enter_context(nc.sbuf_tensor(n, shape, dtype)),
                        lambda n, shape, dtype: inner.enter_context(nc.psum_tensor(n, shape, dtype)),
                        inner.enter_context(cleared_semaphores(nc)))
            norm_inputs(nc, m, "in_e", lambda sp: g.load(sp, a), experts=g)
            gates(nc, m, g)
            experts(nc, m, g, a["L0_ffn_fc1_w"], a["L0_ffn_fc2_w"])
        with ExitStack() as inner:
            weights = PairWeights(lambda n, shape, dtype: inner.enter_context(nc.sbuf_tensor(n, shape, dtype)),
                                  inner.enter_context(cleared_semaphores(nc)), "att1", column_major(a["L1_xattn_Wq"]),
                                  column_major(a["L1_xattn_Wk"]), column_major(a["L1_xattn_Wv"]), lambda p: wo1[p])
            norm_inputs(nc, m, "in1", lambda sp: weights.load(sp, 0))
            attention(nc, m, "att1", weights, banded)
        with ExitStack() as inner:
            uT32 = inner.enter_context(nc.sbuf_tensor("uT32", [P, KD, TOK], F32))
            w = Adapters(lambda n, shape, dtype: inner.enter_context(nc.sbuf_tensor(n, shape, dtype)),
                         inner.enter_context(cleared_semaphores(nc)))
            norm_inputs(nc, m, "in2", lambda sp: w.load(sp, a), uT32=uT32)
            adapters(nc, m, uT32, w)
        write_out(nc, m, out_dram)

def kernel(**inputs):
    import numpy as _np
    import concourse.bacc as _bacc
    from concourse import mybir as _mybir
    from concourse.bass_utils import run_bass_kernel_spmd as _run

    nc = _bacc.Bacc("TRN2", target_bir_lowering=False, num_devices=1)
    arrays, args = {}, {}
    for name in inputs:
        array = _np.ascontiguousarray(inputs[name])
        arrays[f"in_{name}"] = array
        args[name] = nc.dram_tensor(f"in_{name}", array.shape, _mybir.dt.from_np(array.dtype),
                                    kind="ExternalInput").ap()
    out = nc.dram_tensor("out_0", (4, 512, 256), _mybir.dt.float32, kind="ExternalOutput").ap()
    program(nc, args, out)
    result = _run(nc, [arrays], core_ids=[0])
    return result.results[0]["out_0"]
```

```python
from contextlib import ExitStack, contextmanager

import concourse.bass as bass
from concourse import mybir

F32 = mybir.dt.float32
F32R = mybir.dt.float32r
ALU = mybir.AluOpType
ACT = mybir.ActivationFunctionType
AX = mybir.AxisListType

P = 128
D = 256
KD = D // P
B = 4
S = 512
TOK = B * S
NT = TOK // P
TPB = S // P
H = 16
DH = 64
NP = H // 2
LN_EPS = 1e-5
Q_SCALE = DH ** -0.5
MASKED = -(2.0 ** 100)
LOW, UP = 0, 1
E = 8
F = 1024
NF = F // P
BANK = 512


def ge(eng, sem, count):
    if isinstance(count, int) and count <= 0:
        return
    eng.wait_ge(sem, count)


def as_f32(ap):
    return ap.bitcast(F32)


@contextmanager
def cleared_semaphores(nc):
    made = []

    def make(name):
        made.append(nc.alloc_semaphore(name))
        return made[-1]

    yield make
    nc.clear_and_free_semaphores(made)
    nc.all_engine_barrier()


class Shared:

    def __init__(self, sb):
        self.x = sb("x_sb", [P, NT, D], F32)
        self.uT_hi, self.uT_lo = sb("uT_hi", [P, KD, TOK], F32R), sb("uT_lo", [P, KD, TOK], F32R)
        self.cT_hi, self.cT_lo = sb("cT_hi", [P, KD, TOK], F32R), sb("cT_lo", [P, KD, TOK], F32R)
        self.ident, self.one = sb("ident", [P, P], F32), sb("one", [P, P], F32)
        self.masks = sb("masks", [P, 2, P], F32)
        self.bn, self.mv = sb("bn", [P, NT, 6], F32), sb("mv", [P, NT, 2], F32)
        self.spare, self.spare_used = sb("spare", [P, 16], F32), 0
        self.consts = sb("consts", [P, 2], F32)


class PairWeights:

    def __init__(self, sb, sem, tag, wq, wk, wv, wo, biases=None):
        self.w = sb(tag + "_w_stage", [P, 3, KD, P], F32)
        self.wo = sb(tag + "_wo_stage", [P, D], F32)
        self.b = sb(tag + "_b_stage", [P, 3], F32)
        self.w_loaded, self.wo_loaded, self.b_loaded = \
            (sem(tag + n) for n in ("_w_loaded", "_wo_loaded", "_b_loaded"))
        self.w_dram, self.wo_dram, self.biases = (wq, wk, wv), wo, biases
        self.dmas = sum(len(w(self.w[:, 0, :, :], 0)) for w in self.w_dram)

    def load(self, sp, p):
        for i, w in enumerate(self.w_dram):
            for dst, src in w(self.w[:, i, :, :], p):
                sp.dma_start(dst, src).then_inc(self.w_loaded, 16)
        sp.dma_start(self.wo[:, :], self.wo_dram(p)).then_inc(self.wo_loaded, 16)
        if self.biases is not None:
            for i, bias in enumerate(self.biases):
                sp.dma_start(self.b[:, i:i + 1], bias(p)).then_inc(self.b_loaded, 16)


class Experts:

    def __init__(self, sb, psum, sem):
        self.columns = sb("g_columns", [P, E * NF + 2 * E * KD], F32)
        self.comb, self.comb_e = sb("g_comb", [P, NT, E], F32), sb("g_comb_e", [P, E, NT], F32)
        self.fc1b = self.columns[:, 0:E * NF]
        self.lnw = self.columns[:, E * NF:E * NF + E * KD]
        self.lnb = self.columns[:, E * NF + E * KD:E * NF + 2 * E * KD]
        self.root_u = sb("g_root_u", [P, NT], F32)
        self.wg, self.alpha = sb("g_wg", [P, KD, E], F32), sb("g_alpha", [P, E], F32)
        self.wg_halves = sb("g_wg_halves", [P, KD, 2, E], F32R)
        self.logit_ps = psum("g_logit_ps", [P, BANK], F32)
        self.rows = sb("g_rows", [E * NF + 2 * E * KD, P], F32)
        self.b2_row, self.b2_loaded = sb("g_b2_row", [P, D], F32), sem("g_b2_loaded")
        self.w1_stage, self.w2_stage = sb("w1_stage", [P, KD, F], F32), sb("w2_stage", [P, NF, D], F32)
        self.small_loaded, self.rows_loaded, self.w1_loaded, self.w2_loaded = \
            (sem(n) for n in ("g_small_loaded", "g_rows_loaded", "w1_loaded", "w2_loaded"))

    def load(self, sp, a):
        sp.dma_start(self.wg[:, :, :], a["L0_ffn_Wg"].rearrange("(k d) e -> d k e", k=KD)).then_inc(self.small_loaded, 16)
        sp.dma_start(self.alpha[:, :], a["L0_ffn_alpha"].rearrange("(a e) -> a e", a=1).to_broadcast([P, E])) \
            .then_inc(self.small_loaded, 16)
        sp.dma_start(self.b2_row[:, :], a["L0_ffn_fc2_b"].rearrange("(e a) d -> e a d", a=1)[0].to_broadcast([P, D])) \
            .then_inc(self.b2_loaded, 16)
        n = E * NF
        sp.dma_start(self.rows[0:n, :], a["L0_ffn_fc1_b"].rearrange("e (f p) -> (e f) p", p=P)) \
            .then_inc(self.rows_loaded, 16)
        for name in ("L0_ffn_ln_w", "L0_ffn_ln_b"):
            sp.dma_start(self.rows[n:n + E * KD, :], a[name].rearrange("e (k p) -> (e k) p", p=P)) \
                .then_inc(self.rows_loaded, 16)
            n += E * KD
        sp.dma_start(self.w1_stage[:, :, :], a["L0_ffn_fc1_w"].rearrange("e (k d) f -> e d k f", k=KD)[0]) \
            .then_inc(self.w1_loaded, 16)
        sp.dma_start(self.w2_stage[:, :, :], a["L0_ffn_fc2_w"].rearrange("e (f p) d -> e p f d", p=P)[0]) \
            .then_inc(self.w2_loaded, 16)


class Adapters:

    def __init__(self, sb, sem):
        nc_ = E * DH // P
        self.enc, self.dec = sb("ad_enc", [P, KD, E * DH], F32), sb("ad_dec", [P, nc_, D], F32)
        self.base = sb("ad_base", [P, KD, D], F32)
        self.down, self.up = sb("ad_down", [P, KD, E, DH], F32), sb("ad_up", [DH, E, D], F32)
        self.vec_rows, self.b_down_rows = sb("ad_vec_rows", [2 * E + nc_, P], F32), sb("ad_b_down_rows", [E, DH], F32)
        self.bias_rows = sb("ad_bias_rows", [E + 1, D], F32)
        self.index = sb("ad_index", [P, E], mybir.dt.int32)
        self.w_loaded, self.row_loaded, self.bias_loaded, self.late_loaded = \
            (sem("ad_" + n) for n in ("w_loaded", "row_loaded", "bias_loaded", "late_loaded"))

    def load(self, sp, a):
        n_dec = 2 * E
        row = lambda t: t.rearrange("(a n) -> a n", a=1)
        for k in range(KD):
            sp.dma_start(self.enc[:, :, :].rearrange("p k (n h) -> p k n h", n=E)[:, k, :, :],
                         a["L1_ffn_W_enc"].rearrange("n (k d) h -> k d n h", k=KD)[k]).then_inc(self.w_loaded, 16)
        sp.dma_start(self.dec[:, :, :], a["L1_ffn_W_dec"].rearrange("(c m) h d -> (m h) c d", m=2)) \
            .then_inc(self.w_loaded, 16)
        sp.dma_start(self.base[:, :, :], a["L1_ffn_W_base"].rearrange("(k d) e -> d k e", k=KD)).then_inc(self.w_loaded, 16)
        sp.dma_start(self.vec_rows[0:n_dec, :], a["L1_ffn_b_dec"].rearrange("n (k p) -> (n k) p", p=P)) \
            .then_inc(self.row_loaded, 16)
        sp.dma_start(self.vec_rows[n_dec:, :], a["L1_ffn_b_enc"].rearrange("(c m) h -> c (m h)", m=2)) \
            .then_inc(self.row_loaded, 16)
        sp.dma_start(self.b_down_rows[:, :], a["L1_ffn_b_down"]).then_inc(self.row_loaded, 16)
        sp.dma_start(self.bias_rows[E:E + 1, :], row(a["L1_ffn_b_base"])).then_inc(self.bias_loaded, 16)
        sp.dma_start(self.index[:, :], row(a["L1_ffn_connected_idx"]).to_broadcast([P, E])).then_inc(self.bias_loaded, 16)
        sp.dma_start(self.bias_rows[0:E, :], a["L1_ffn_b_up"]).then_inc(self.bias_loaded, 16)
        for k in range(KD):
            sp.dma_start(self.down[:, k, :, :], a["L1_ffn_W_down"].rearrange("n (k d) r -> k d n r", k=KD)[k]) \
                .then_inc(self.late_loaded, 16)
        sp.dma_start(self.up[:, :, :], a["L1_ffn_W_up"].rearrange("n r d -> r n d")).then_inc(self.late_loaded, 16)


def load_table(act, m, function):
    n = m.spare_used
    m.spare_used += 1
    act.activation(m.spare[:, n:n + 1], m.consts[:, 0:1], function)


class Chain:

    def __init__(self, eng, sem):
        self.eng, self.sem, self.count = eng, sem, 0

    def inc(self, instruction):
        self.count += 1
        instruction.then_inc(self.sem, 1)

    def wait(self):
        self.eng.wait_ge(self.sem, self.count)


def batch_statistics(dve, chain, m, b):
    for t in range(TPB * b, TPB * b + TPB):
        chain.inc(dve.bn_stats(m.bn[:, t, :], m.x[:, t, :]))
    chain.wait()
    for t in range(TPB * b, TPB * b + TPB):
        chain.inc(dve.bn_aggr(m.mv[:, t, :], m.bn[:, t, :]))


def norm_inputs(nc, m, tag, prefetch, x_dram=None, ctx_dram=None, uT32=None, experts=None):
    with ExitStack() as ctx:
        sb = lambda n, s, d: ctx.enter_context(nc.sbuf_tensor(f"{tag}_{n}", s, d))
        make = ctx.enter_context(cleared_semaphores(nc))
        sem = lambda n: make(f"{tag}_{n}")
        first = x_dram is not None
        col = {n: sb(n, [P, NT], F32) for n in ("veps", "sd", "r0", "t1", "t2", "t3", "r1", "v_u", "veps2", "sd2",
                                                "s0", "s1", "s2", "s3", "r2", "r12")}
        u = sb("u", [P, NT, D], F32)
        c = sb("c", [P, NT, D], F32) if first else None
        banks = [ctx.enter_context(nc.psum_tensor(f"{tag}_ps{i}", [P, BANK], F32)) for i in range(4)]
        x_loaded, c_loaded = ([sem(f"{n}_loaded{b}") for b in range(B)] for n in ("x", "c"))
        const_step, const_ready = sem("const_step"), sem("const_ready")
        dve_step, var_ready, sqrt_ready = sem("dve_step"), sem("var_ready"), sem("sqrt_ready")
        rstd_ready, u_dve_ready, u_pool_ready = sem("rstd_ready"), sem("u_dve_ready"), sem("u_pool_ready")
        wg_hi_ready, wg_ready = sem("wg_hi_ready"), sem("wg_ready")
        turned, hi_ready, lo_ready = sem("turned"), sem("hi_ready"), sem("lo_ready")
        f32_ready = sem("f32_ready")

        jobs = ([(c, m.cT_hi, m.cT_lo, g) for g in range(NT // 2)] if first else []) + \
               [(u, m.uT_hi, m.uT_lo, g) for g in range(NT // 2)]
        n_c = len(jobs) - NT // 2
        rstd = col["r12"] if experts is not None else col["r1"]

        def normalise(eng, t):
            return eng.tensor_scalar(u[:, t, :], m.x[:, t, :], m.mv[:, t, 0:1], rstd[:, t:t + 1], ALU.subtract, ALU.mult)

        with nc.Block() as block:
            @block.sync
            def _(sp):
                if first:
                    for b in range(B):
                        rows = slice(b * S, (b + 1) * S)
                        sp.dma_start(m.x[:, TPB * b:TPB * b + TPB, :],
                                     x_dram[rows, :].rearrange("(t p) d -> p t d", p=P)).then_inc(x_loaded[b], 16)
                prefetch(sp)

            @block.gpsimd
            def _(pool):
                if first:
                    make_constants(pool, m, const_step, const_ready)
                    pool.wait_ge(const_ready, 1)
                pool.wait_ge(rstd_ready, 1)
                for n, t in enumerate(range(3, NT, 4)):
                    ge(pool, u_pool_ready, n)
                    normalise(pool, t).then_inc(u_pool_ready, 1)

            @block.scalar
            def _(act):
                if first:
                    for b in range(B):
                        rows = slice(b * S, (b + 1) * S)
                        act.dma_start(c[:, TPB * b:TPB * b + TPB, :],
                                      ctx_dram[rows, :].rearrange("(t p) d -> p t d", p=P)).then_inc(c_loaded[b], 16)
                    act.wait_ge(const_ready, 1)
                    load_table(act, m, ACT.Sqrt)
                roots = [("sd", "veps")] + ([("sd2", "veps2")] if experts is not None else [])

                def root(i):
                    out, src = roots[i]
                    act.wait_ge(var_ready, i + 1)
                    act.activation(col[out][:, :], col[src][:, :], ACT.Sqrt).then_inc(sqrt_ready, 1)

                if not first:
                    for i in range(len(roots)):
                        root(i)
                for n, (_, hi, lo, g) in enumerate(jobs):
                    if first and n == n_c - 2:
                        root(0)
                    act.wait_ge(turned, n + 1)
                    act.activation(hi[:, :, 2 * P * g:2 * P * (g + 1)],
                                   banks[n % 4][:, :].rearrange("p (k t) -> p k t", k=KD), ACT.Copy) \
                        .then_inc(hi_ready, 1)
                    if uT32 is not None:
                        act.activation(uT32[:, :, 2 * P * g:2 * P * (g + 1)],
                                       banks[n % 4][:, :].rearrange("p (k t) -> p k t", k=KD), ACT.Copy) \
                            .then_inc(f32_ready, 1)

            @block.vector
            def _(dve):
                chain = Chain(dve, dve_step)

                def step(instruction):
                    chain.inc(instruction)
                    chain.wait()

                def inverse_root(veps, sd, names):
                    r0, t1, t2, t3, out = (col[n] for n in names)
                    step(dve.reciprocal(r0[:, :], col[sd][:, :]))
                    step(dve.tensor_tensor(t1[:, :], r0[:, :], r0[:, :], ALU.mult))
                    step(dve.tensor_tensor(t2[:, :], t1[:, :], col[veps][:, :], ALU.mult))
                    step(dve.tensor_scalar(t3[:, :], t2[:, :], -0.5, 1.5, ALU.mult, ALU.add))
                    step(dve.tensor_tensor(out[:, :], r0[:, :], t3[:, :], ALU.mult))

                def lo_of(n):
                    _, hi, lo, g = jobs[n]
                    dve.wait_ge(hi_ready, n + 1)
                    if uT32 is not None:
                        dve.wait_ge(f32_ready, n + 1)
                    cols = slice(2 * P * g, 2 * P * (g + 1))
                    dve.tensor_tensor(lo[:, :, cols], banks[n % 4][:, :].rearrange("p (k t) -> p k t", k=KD),
                                      as_f32(hi[:, :, cols]), ALU.subtract).then_inc(lo_ready, 1)

                if first:
                    for b in range(B):
                        dve.wait_ge(x_loaded[b], 16)
                        batch_statistics(dve, chain, m, b)
                        if b == 0:
                            lo_of(0)
                            lo_of(1)
                        elif b == 1:
                            lo_of(2)
                            lo_of(3)
                    chain.wait()
                dve.tensor_scalar(col["veps"][:, :], m.mv[:, :, 1], LN_EPS, None, ALU.add).then_inc(var_ready, 1)
                if first:
                    lo_of(4)
                    lo_of(5)
                dve.wait_ge(sqrt_ready, 1)
                dve.wait_ge(var_ready, 1)
                inverse_root("veps", "sd", ("r0", "t1", "t2", "t3", "r1"))
                if experts is not None:
                    step(dve.tensor_tensor(col["s0"][:, :], col["r1"][:, :], col["r1"][:, :], ALU.mult))
                    step(dve.tensor_tensor(col["v_u"][:, :], col["s0"][:, :], m.mv[:, :, 1], ALU.mult))
                    dve.tensor_scalar(col["veps2"][:, :], col["v_u"][:, :], LN_EPS, None, ALU.add).then_inc(var_ready, 1)
                    dve.wait_ge(sqrt_ready, 2)
                    dve.wait_ge(var_ready, 2)
                    inverse_root("veps2", "sd2", ("s1", "t1", "s2", "s3", "r2"))
                    step(dve.tensor_tensor(experts.root_u[:, :], col["veps2"][:, :], col["r2"][:, :], ALU.mult))
                    step(dve.tensor_tensor(col["r12"][:, :], col["r1"][:, :], col["r2"][:, :], ALU.mult))
                dve.tensor_copy(col["t1"][:, :], rstd[:, :]).then_inc(rstd_ready, 1)
                for t in range(6):
                    if t % 4 != 3:
                        normalise(dve, t).then_inc(u_dve_ready, 1)
                if experts is not None:
                    dve.wait_ge(experts.small_loaded, 32)
                    hi, lo = (experts.wg_halves[:, :, i, :] for i in range(2))
                    dve.tensor_copy(hi, experts.wg[:, :, :]).then_inc(wg_hi_ready, 1)
                    dve.wait_ge(wg_hi_ready, 1)
                    dve.tensor_tensor(lo, experts.wg[:, :, :], as_f32(hi), ALU.subtract).then_inc(wg_ready, 1)
                for n in range(6 if first else 0, len(jobs)):
                    lo_of(n)
                    for t in (2 * (n - n_c) + 6, 2 * (n - n_c) + 7):
                        if 6 <= t < NT and t % 4 != 3:
                            normalise(dve, t).then_inc(u_dve_ready, 1)

            @block.tensor
            def _(pe):
                if first:
                    pe.wait_ge(const_ready, 1)

                def logits_of(g):
                    pe.wait_ge(lo_ready, g + 1)
                    if g == 0:
                        pe.wait_ge(wg_ready, 1)
                    for t in (2 * g, 2 * g + 1):
                        cols = slice(P * t, P * t + P)
                        n = 0
                        for k in range(KD):
                            for u_half in (m.uT_hi, m.uT_lo):
                                pe.matmul(experts.logit_ps[:, 2 * E * t:2 * E * t + 2 * E], u_half[:, k, cols],
                                          experts.wg_halves[:, k, :, :], start=(n == 0), stop=(n == 3),
                                          skip_group_check=True)
                                n += 1

                for n, (src, _, _, g) in enumerate(jobs):
                    if n < n_c:
                        pe.wait_ge(c_loaded[g // 2], 16)
                    else:
                        pe.wait_ge(u_dve_ready, (2 * g + 2) - (g + 1) // 2)
                        ge(pe, u_pool_ready, (g + 1) // 2)
                    if n >= 4:
                        pe.wait_ge(lo_ready, n - 3)
                    for k in range(KD):
                        for j in range(2):
                            last = pe.transpose(banks[n % 4][:, (2 * k + j) * P:(2 * k + j + 1) * P],
                                                src[:, 2 * g + j, k * P:(k + 1) * P], m.ident[:, :])
                    last.then_inc(turned, 1)
                    if experts is not None and g >= 1:
                        logits_of(g - 1)
                if experts is not None:
                    logits_of(NT // 2 - 1)


def make_constants(pool, m, step, ready):
    pool.memset(m.ident[:, :], 0.0).then_inc(step, 1)
    pool.memset(m.masks[:, :, :], 0.0).then_inc(step, 1)
    pool.memset(m.consts[:, 0:1], 1.0).then_inc(step, 1)
    pool.memset(m.consts[:, 1:2], Q_SCALE).then_inc(step, 1)
    n = 4
    for tile, q_step, k_step, compare, fill in (
            (m.ident[:, :], 1, -1, ALU.not_equal, 1.0),
            (m.masks[:, LOW, :], -1, 1, ALU.is_ge, MASKED),
            (m.masks[:, UP, :], 1, -1, ALU.is_ge, MASKED)):
        pool.wait_ge(step, n)
        pool.affine_select(out=tile, in_=tile, compare_op=compare, fill=fill, base=0, pattern=[[k_step, P]],
                           channel_multiplier=q_step).then_inc(step, 1)
        n += 1
    pool.wait_ge(step, n)
    pool.memset(m.one[:, :], 1.0).then_inc(ready, 1)


def attention(nc, m, tag, weights, blocks_of, bo=None):
    biased = weights.biases is not None
    seen = [blocks_of(j) for j in range(TPB)]
    first_key = [s[0][0] for s in seen]
    width = [P * len(s) for s in seen]
    place = list(range(TPB))[::-1]
    turns = []
    for i in range(TPB):
        turns += [(i, (0, 1))] if 2 * width[place[i]] <= BANK else [(i, (0,)), (i, (1,))]
    t_of = [[q for q, (ii, _) in enumerate(turns) if ii == i] for i in range(TPB)]
    NTURN = len(turns)
    narrow_first = len(t_of[0]) < len(t_of[1])
    dve_norms = (0, TPB - 1) if narrow_first else (0,)
    pool_norms = [i for i in range(TPB) if i not in dve_norms]
    order = [("S", 0), ("Q", 0), ("S", 1), ("K", 0), ("PVB", 0)] + [("T", q) for q in t_of[0]] + \
            [("S", 2), ("S", 3)] + [("T", q) for q in t_of[1]] + \
            [("VT", 0), ("O", 0), ("O", 1), ("VR", 0), ("PVA", 0)] + [("T", q) for q in t_of[2] + t_of[3]]
    ring_jobs = [o for o in order if o[0] in ("Q", "K", "VT", "VR", "T", "O")]
    RING = 3
    assert len(ring_jobs) % RING == 0
    next_item, ends_before = ("Q", "K", "VT", "VR"), ("PVB", "O")

    with ExitStack() as ctx:
        sb = lambda n, s, d: ctx.enter_context(nc.sbuf_tensor(f"{tag}_{n}", s, d))
        make = ctx.enter_context(cleared_semaphores(nc))
        sem = lambda n: make(f"{tag}_{n}")
        w_stage, wo_stage, b_stage = weights.w, weights.wo, weights.b
        w_hi, w_lo = sb("w_hi", [P, 3, KD, P], F32R), sb("w_lo", [P, 3, KD, P], F32R)
        wo_hi, wo_lo = sb("wo_hi", [P, D], F32R), sb("wo_lo", [P, D], F32R)
        bqk, bvz = sb("bqk", [P, 2], F32), sb("bvz", [P, 1], F32)
        q_hi, q_lo = sb("q_hi", [P, 2, S], F32R), sb("q_lo", [P, 2, S], F32R)
        k_hi, k_lo = sb("k_hi", [P, 2, S], F32R), sb("k_lo", [P, 2, S], F32R)
        vT = sb("vT", [P, S], F32)
        v_hi, v_lo = sb("v_hi", [P, 2, TPB, 3, DH], F32R), sb("v_lo", [P, 2, TPB, 3, DH], F32R)
        probs = sb("probs", [P, TPB, 2, S], F32)
        negmax, sums, rsum = sb("negmax", [P, TPB, 2], F32), sb("sums", [P, TPB, 2], F32), sb("rsum", [P, TPB, 2], F32)
        pT_hi, pT_lo = (sb(n, [P, 2, 2, TPB, 2 * P], F32R) for n in ("pT_hi", "pT_lo"))
        z_hi, z_lo = sb("z_hi", [P, S], F32R), sb("z_lo", [P, S], F32R)
        o_sb = sb("o_sb", [P, 2, BANK], F32)
        s_ps = [ctx.enter_context(nc.psum_tensor(f"{tag}_s{i}", [P, 2, BANK], F32)) for i in range(2)]
        ring = [ctx.enter_context(nc.psum_tensor(f"{tag}_ring{i}", [P, BANK], F32)) for i in range(RING)]
        z_ps = ctx.enter_context(nc.psum_tensor(f"{tag}_z", [P, BANK], F32))

        w_loaded, wo_loaded, b_loaded = weights.w_loaded, weights.wo_loaded, weights.b_loaded
        bo_added, w_hi_ready = sem("bo_added"), sem("w_hi_ready")
        w_step, w_ready, wo_step, wo_ready = sem("w_step"), sem("w_ready"), sem("wo_step"), sem("wo_ready")
        dve_step, bqk_ready, bvz_ready = sem("dve_step"), sem("bqk_ready"), sem("bvz_ready")
        zeroed, o_read = sem("zeroed"), sem("o_read")
        s_done, q_done, k_done, vt_done, vr_done = sem("s_done"), sem("q_done"), sem("k_done"), sem("vt_done"), sem("vr_done")
        t_done, pva_done, pvb_done, o_done = sem("t_done"), sem("pva_done"), sem("pvb_done"), sem("o_done")
        max_ready, exp_ready, rsum_ready, norm_ready = sem("max_ready"), sem("exp_ready"), sem("rsum_ready"), sem("norm_ready")
        masked, dve_norm_ready = sem("masked"), sem("dve_norm_ready")
        q_hi_ready, k_hi_ready, vT_ready, v_hi_ready = sem("q_hi_ready"), sem("k_hi_ready"), sem("vT_ready"), sem("v_hi_ready")
        q_ready, k_ready, v_ready = sem("q_ready"), sem("k_ready"), sem("v_ready")
        pT_hi_ready, pT_ready, z_hi_ready, z_ready, x_added = \
            sem("pT_hi_ready"), sem("pT_ready"), sem("z_hi_ready"), sem("z_ready"), sem("x_added")

        def per_item(p, b, n, c):
            return p * (B * n) + (b * n + c)

        def ran(kind, p, b):
            if isinstance(p, int):
                it = B * p + b
                if it < 0:
                    return kind in next_item
                if it == 0:
                    return kind not in ends_before
                if it == B * NP - 1:
                    return kind not in next_item
                if it == B * NP:
                    return kind in ends_before
            return True

        def bank_of(kind, q):
            return ring[ring_jobs.index((kind, q)) % RING]

        def wait_bank_free(pe, kind, q, p, b):
            k, bb = ring_jobs.index((kind, q)), b
            while True:
                k -= RING
                if k < 0:
                    k, bb = k + len(ring_jobs), bb - 1
                if isinstance(p, int) and B * p + bb < -1:
                    return
                kk, qq = ring_jobs[k]
                if ran(kk, p, bb):
                    break
            sem, n, c = {"Q": (q_ready, 1, 2), "K": (k_ready, 1, 2), "VT": (vT_ready, 1, 2), "VR": (v_ready, 1, 2),
                         "T": (pT_ready, NTURN, qq + 1), "O": (o_read, 2, qq - 1)}[kk]
            pe.wait_ge(sem, per_item(p, bb, n, c))

        def turned_from(q):
            i, hs = turns[q]
            j = place[i]
            return bank_of("T", q)[:, 0:width[j] * len(hs)].rearrange(
                "p (h t n) -> p h t n", h=len(hs), n=P)

        def turned_into(half, q):
            i, hs = turns[q]
            j = place[i]
            k0, n = first_key[j], width[j] // P
            return half[:, j // 2, hs[0]:hs[-1] + 1, k0:k0 + n, P * (j % 2):P * (j % 2) + P]

        with nc.Block() as block:
            @block.sync
            def _(sp):
                with sp.Fori(1, NP) as p:
                    sp.wait_ge(w_ready, p * 3)
                    sp.wait_ge(wo_ready, p * 1)
                    if biased:
                        sp.wait_ge(bvz_ready, p * 1)
                    weights.load(sp, p)

            @block.gpsimd
            def _(pool):
                one, scale = (m.consts[:, i:i + 1] for i in range(2))

                def split_w(i, p):
                    done = {0: q_done, 1: k_done, 2: vt_done}[i]
                    if i == 0:
                        pool.wait_ge(w_loaded, p * (16 * weights.dmas) + 16 * weights.dmas)
                    ge(pool, done, per_item(p, 0, 1, 0))
                    w = w_stage[:, i, :, :].rearrange("p k n -> p (k n)")
                    hi, lo = (half[:, i, :, :].rearrange("p k n -> p (k n)") for half in (w_hi, w_lo))
                    steps = (p - 1) * 4 + (i + 1 if i else 0)
                    if i == 0:
                        pool.tensor_tensor(w, w, scale.to_broadcast([P, KD * P]), ALU.mult).then_inc(w_step, 1)
                        pool.wait_ge(w_step, steps + 1)
                        steps = steps + 1
                    pool.tensor_tensor(hi, w, one.to_broadcast([P, KD * P]), ALU.mult).then_inc(w_step, 1)
                    pool.wait_ge(w_step, steps + 1)
                    pool.tensor_tensor(lo, w, as_f32(hi), ALU.subtract).then_inc(w_ready, 1)

                def split_wo(p):
                    pool.wait_ge(wo_loaded, p * 16 + 16)
                    ge(pool, o_done, per_item(p, 0, 2, 0))
                    pool.tensor_tensor(wo_hi[:, :], wo_stage[:, :], one.to_broadcast([P, D]), ALU.mult).then_inc(wo_step, 1)
                    pool.wait_ge(wo_step, p * 1 + 1)
                    pool.tensor_tensor(wo_lo[:, :], wo_stage[:, :], as_f32(wo_hi[:, :]), ALU.subtract).then_inc(wo_ready, 1)

                def norm_of(i, p, b):
                    j = place[i]
                    pool.wait_ge(rsum_ready, per_item(p, b, TPB, i + 1))
                    for h in range(2):
                        tile = probs[:, j, h, 0:width[j]]
                        pool.tensor_tensor(tile, tile, rsum[:, j, h:h + 1].to_broadcast([P, width[j]]), ALU.mult) \
                            .then_inc(norm_ready, 1)

                def x_of(a, p, b):
                    pool.wait_ge(o_read, per_item(p, b, 2, a - 1))
                    ge(pool, x_added, per_item(p, b, 2, a - 3))
                    t0 = TPB * ((b - 1) % B) + 2 * a
                    rows = m.x[:, t0:t0 + 2, :].rearrange("p t d -> p (t d)")
                    pool.tensor_tensor(rows, rows, o_sb[:, a, :], ALU.add).then_inc(x_added, 1)

                def body(p):
                    for b in range(B):
                        if b == B - 2 and ran("Q", p, b + 1):
                            split_w(0, p + 1)
                            split_w(1, p + 1)
                        for i in pool_norms:
                            norm_of(i, p, b)
                        if b == B - 2 and ran("Q", p, b + 1):
                            split_w(2, p + 1)
                        if bo is not None and isinstance(p, int) and p == 0:
                            for t in range(TPB * b, TPB * b + TPB):
                                pool.tensor_tensor(m.x[:, t, :], m.x[:, t, :], bo[:, :], ALU.add).then_inc(bo_added, 1)
                            pool.wait_ge(bo_added, TPB * b + TPB)
                        if ran("O", p, b):
                            if b == 0:
                                split_wo(p)
                            x_of(0, p, b)
                            x_of(1, p, b)

                for half in (v_hi, v_lo):
                    for i in range(2):
                        pool.memset(as_f32(half[:, i, :, 1, :]), 0.0).then_inc(zeroed, 1)
                split_wo(0)
                body(0)
                with pool.Fori(1, NP - 1) as p:
                    body(p)
                body(NP - 1)
                x_of(0, NP, 0)
                x_of(1, NP, 0)

            @block.scalar
            def _(act):
                def copy_hi(dst, src, bias, done):
                    if bias is None:
                        act.activation(dst, src, ACT.Copy).then_inc(done, 1)
                    else:
                        act.activation(dst, src, ACT.Identity, bias=bias).then_inc(done, 1)

                def q_of(p, b):
                    act.wait_ge(q_done, per_item(p, b, 1, 2))
                    if biased and (b == B - 1 or b == -1):
                        act.wait_ge(bqk_ready, (p + (1 if b == B - 1 else 0)) * 1 + 1)
                    copy_hi(q_hi[:, (b + 1) % 2, :], bank_of("Q", 0)[:, :], bqk[:, 0:1] if biased else None, q_hi_ready)

                def k_of(p, b):
                    act.wait_ge(k_done, per_item(p, b, 1, 2))
                    copy_hi(k_hi[:, (b + 1) % 2, :], bank_of("K", 0)[:, :], bqk[:, 1:2] if biased else None, k_hi_ready)

                def vt_of(p, b):
                    act.wait_ge(vt_done, per_item(p, b, 1, 2))
                    act.activation(vT[:, :], bank_of("VT", 0)[:, :], ACT.Copy).then_inc(vT_ready, 1)

                def vr_of(p, b):
                    act.wait_ge(vr_done, per_item(p, b, 1, 2))
                    act.activation(v_hi[:, (b + 1) % 2, :, 0:3:2, :],
                                   bank_of("VR", 0)[:, :].rearrange("p (t h e) -> p t h e", t=TPB, h=2),
                                   ACT.Copy).then_inc(v_hi_ready, 1)

                def exp_of(i, p, b):
                    j = place[i]
                    act.wait_ge(max_ready, per_item(p, b, TPB, i + 1))
                    ge(act, t_done, per_item(p, b, NTURN, t_of[i][-1] + 1 - NTURN))
                    for h in range(2):
                        act.activation(probs[:, j, h, 0:width[j]], s_ps[i % 2][:, h, 0:width[j]], ACT.Exp,
                                       bias=negmax[:, j, h:h + 1], accum_out=sums[:, j, h:h + 1]) \
                            .then_inc(exp_ready, 1)

                def z_of(p, b):
                    act.wait_ge(pvb_done, per_item(p, b, 1, 0))
                    if biased and b == 1:
                        act.wait_ge(bvz_ready, p * 1 + 1)
                    copy_hi(z_hi[:, :], z_ps[:, :], bvz[:, 0:1] if biased else None, z_hi_ready)

                def turn_of(q, p, b):
                    act.wait_ge(t_done, per_item(p, b, NTURN, q + 1))
                    act.activation(turned_into(pT_hi, q), turned_from(q), ACT.Copy).then_inc(pT_hi_ready, 1)

                def o_of(a, p, b):
                    act.wait_ge(o_done, per_item(p, b, 2, a - 1))
                    ge(act, x_added, per_item(p, b, 2, a - 3))
                    act.activation(o_sb[:, a, :], bank_of("O", a)[:, :], ACT.Copy).then_inc(o_read, 1)

                def body(p):
                    for b in range(B):
                        on = lambda kind: ran(kind, p, b)
                        if on("Q"):
                            q_of(p, b)
                        exp_of(0, p, b)
                        if on("Q"):
                            k_of(p, b)
                        exp_of(1, p, b)
                        for q in t_of[0]:
                            turn_of(q, p, b)
                        if on("PVB"):
                            z_of(p, b)
                        for q in t_of[1]:
                            turn_of(q, p, b)
                        if on("VT") and not narrow_first:
                            vt_of(p, b)
                        exp_of(2, p, b)
                        if on("VT") and narrow_first:
                            vt_of(p, b)
                        exp_of(3, p, b)
                        if on("O"):
                            o_of(0, p, b)
                            o_of(1, p, b)
                        if on("VR"):
                            vr_of(p, b)
                        for q in t_of[2] + t_of[3]:
                            turn_of(q, p, b)

                load_table(act, m, ACT.Exp)
                q_of(0, -1), k_of(0, -1), vt_of(0, -1), vr_of(0, -1)
                body(0)
                with act.Fori(1, NP - 1) as p:
                    body(p)
                body(NP - 1)
                z_of(NP, 0)
                o_of(0, NP, 0)
                o_of(1, NP, 0)
                load_table(act, m, ACT.Sqrt)

            @block.vector
            def _(dve):
                chain = Chain(dve, dve_step)

                def statistics_of(b):
                    dve.wait_ge(x_added, B * 2 * (NP - 1) + 2 * b + 2)
                    batch_statistics(dve, chain, m, b)

                def bias_qk(p):
                    dve.wait_ge(b_loaded, p * 48 + 48)
                    ge(dve, k_ready, per_item(p, 0, 1, 0))
                    dve.tensor_scalar(bqk[:, 0:1], b_stage[:, 0:1], Q_SCALE, None, ALU.mult)
                    dve.tensor_copy(bqk[:, 1:2], b_stage[:, 1:2]).then_inc(bqk_ready, 1)

                def bias_v(p):
                    dve.wait_ge(b_loaded, p * 48 + 48)
                    ge(dve, z_ready, per_item(p, 0, 1, 0))
                    dve.tensor_copy(bvz[:, :], b_stage[:, 2:3]).then_inc(bvz_ready, 1)

                def sub_hi(dst, src, bias, hi, done):
                    if bias is None:
                        dve.tensor_tensor(dst, src, as_f32(hi), ALU.subtract).then_inc(done, 1)
                    else:
                        dve.scalar_tensor_tensor(dst, src, bias, as_f32(hi), ALU.add, ALU.subtract).then_inc(done, 1)

                def q_of(p, b):
                    dve.wait_ge(q_hi_ready, per_item(p, b, 1, 2))
                    sub_hi(q_lo[:, (b + 1) % 2, :], bank_of("Q", 0)[:, :], bqk[:, 0:1] if biased else None,
                           q_hi[:, (b + 1) % 2, :], q_ready)

                def k_of(p, b):
                    dve.wait_ge(k_hi_ready, per_item(p, b, 1, 2))
                    sub_hi(k_lo[:, (b + 1) % 2, :], bank_of("K", 0)[:, :], bqk[:, 1:2] if biased else None,
                           k_hi[:, (b + 1) % 2, :], k_ready)

                def vr_of(p, b):
                    dve.wait_ge(v_hi_ready, per_item(p, b, 1, 2))
                    sub_hi(v_lo[:, (b + 1) % 2, :, 0:3:2, :],
                           bank_of("VR", 0)[:, :].rearrange("p (t h e) -> p t h e", t=TPB, h=2), None,
                           v_hi[:, (b + 1) % 2, :, 0:3:2, :], v_ready)

                def max_of(i, p, b):
                    j = place[i]
                    dve.wait_ge(s_done, per_item(p, b, TPB, i + 1))
                    edges = [n for n, (_, kind) in enumerate(seen[j]) if kind is not None]
                    kinds = [seen[j][n][1] for n in edges]
                    tiles = s_ps[i % 2][:, :, 0:width[j]].rearrange("p h (t n) -> p h t n", n=P)
                    tiles = tiles[:, :, edges[0]:edges[-1] + 1:max(1, edges[-1] - edges[0]), :]
                    mask = m.masks[:, kinds[0]:kinds[-1] + 1, :].rearrange("p (a k) n -> p a k n", a=1) \
                        .to_broadcast([P, 2, len(kinds), P])
                    dve.tensor_tensor(tiles, tiles, mask, ALU.add).then_inc(masked, 1)
                    dve.wait_ge(masked, per_item(p, b, TPB, i + 1))
                    dve.tensor_reduce(negmax[:, j, :], s_ps[i % 2][:, :, 0:width[j]], AX.X, ALU.max,
                                      negate=True).then_inc(max_ready, 1)

                def rsum_of(i, p, b):
                    dve.wait_ge(exp_ready, per_item(p, b, 2 * TPB, 2 * i + 2))
                    dve.reciprocal(rsum[:, place[i], :], sums[:, place[i], :]).then_inc(rsum_ready, 1)

                def norm_of(i, p, b):
                    j = place[i]
                    dve.wait_ge(rsum_ready, per_item(p, b, TPB, i + 1))
                    for h in range(2):
                        tile = probs[:, j, h, 0:width[j]]
                        dve.tensor_scalar(tile, tile, rsum[:, j, h:h + 1], None, ALU.mult).then_inc(dve_norm_ready, 1)

                def z_of(p, b):
                    dve.wait_ge(z_hi_ready, per_item(p, b, 1, 0))
                    sub_hi(z_lo[:, :], z_ps[:, :], bvz[:, 0:1] if biased else None, z_hi[:, :], z_ready)

                def turn_of(q, p, b):
                    dve.wait_ge(pT_hi_ready, per_item(p, b, NTURN, q + 1))
                    dve.tensor_tensor(turned_into(pT_lo, q), turned_from(q), as_f32(turned_into(pT_hi, q)),
                                      ALU.subtract).then_inc(pT_ready, 1)

                def body(p):
                    for b in range(B):
                        on = lambda kind: ran(kind, p, b)
                        max_of(0, p, b)
                        if on("Q"):
                            q_of(p, b)
                        max_of(1, p, b)
                        rsum_of(0, p, b)
                        norm_of(0, p, b)
                        if on("Q"):
                            k_of(p, b)
                        rsum_of(1, p, b)
                        for q in t_of[0]:
                            turn_of(q, p, b)
                        if on("PVB"):
                            z_of(p, b)
                            if b == 0 and biased:
                                bias_v(p)
                        if narrow_first:
                            max_of(2, p, b)
                        for q in t_of[1]:
                            turn_of(q, p, b)
                        if not narrow_first:
                            max_of(2, p, b)
                        max_of(3, p, b)
                        rsum_of(2, p, b)
                        rsum_of(3, p, b)
                        if TPB - 1 in dve_norms:
                            norm_of(TPB - 1, p, b)
                        if b == B - 2 and biased and ran("Q", p, b + 1):
                            bias_qk(p + 1)
                        if on("VR"):
                            vr_of(p, b)
                        for q in t_of[2] + t_of[3]:
                            turn_of(q, p, b)

                if biased:
                    bias_qk(0)
                    bias_v(0)
                dve.wait_ge(w_loaded, 16 * weights.dmas)
                for i in range(3):
                    scale = Q_SCALE if i == 0 else 1.0
                    dve.tensor_scalar(w_hi[:, i, :, :], w_stage[:, i, :, :], scale, None, ALU.mult).then_inc(w_hi_ready, 1)
                    dve.wait_ge(w_hi_ready, i + 1)
                    dve.scalar_tensor_tensor(w_lo[:, i, :, :], w_stage[:, i, :, :], scale, as_f32(w_hi[:, i, :, :]),
                                             ALU.mult, ALU.subtract).then_inc(w_ready, 1)
                q_of(0, -1), k_of(0, -1), vr_of(0, -1)
                body(0)
                with dve.Fori(1, NP - 1) as p:
                    body(p)
                body(NP - 1)
                statistics_of(0)
                z_of(NP, 0)
                for b in range(1, B):
                    statistics_of(b)
                chain.wait()

            @block.tensor
            def _(pe):
                def project(kind, i, hi, lo, p, b):
                    wait_bank_free(pe, kind, 0, p, b)
                    cols = slice(S * ((b + 1) % B), S * ((b + 1) % B) + S)
                    out = bank_of(kind, 0)
                    n = 0
                    for k in range(KD):
                        for w, a in ((w_hi, hi), (w_hi, lo), (w_lo, hi)):
                            last = pe.matmul(out[:, :], w[:, i, k, :], a[:, k, cols], start=(n == 0), stop=(n == 5))
                            n += 1
                    return last

                def q_of(p, b):
                    pe.wait_ge(w_ready, (p + (1 if b == B - 1 else 0)) * 3 + 1)
                    project("Q", 0, m.uT_hi, m.uT_lo, p, b).then_inc(q_done, 1)

                def k_of(p, b):
                    pe.wait_ge(w_ready, (p + (1 if b == B - 1 else 0)) * 3 + 2)
                    project("K", 1, m.cT_hi, m.cT_lo, p, b).then_inc(k_done, 1)

                def vt_of(p, b):
                    pe.wait_ge(w_ready, (p + (1 if b == B - 1 else 0)) * 3 + 3)
                    project("VT", 2, m.cT_hi, m.cT_lo, p, b).then_inc(vt_done, 1)

                def vr_of(p, b):
                    wait_bank_free(pe, "VR", 0, p, b)
                    pe.wait_ge(vT_ready, per_item(p, b, 1, 2))
                    for t in range(TPB):
                        last = pe.transpose(bank_of("VR", 0)[:, P * t:P * t + P], vT[:, P * t:P * t + P], m.ident[:, :])
                    last.then_inc(vr_done, 1)

                def scores(i, p, b):
                    j = place[i]
                    if i == 0:
                        pe.wait_ge(q_ready, per_item(p, b, 1, 1))
                        pe.wait_ge(k_ready, per_item(p, b, 1, 1))
                    ge(pe, exp_ready, per_item(p, b, 2 * TPB, 2 * i - 2))
                    cols = slice(P * first_key[j], P * first_key[j] + width[j])
                    for n, (q, k) in enumerate(((q_hi, k_hi), (q_hi, k_lo), (q_lo, k_hi))):
                        for h in range(2):
                            rows = slice(DH * h, DH * h + DH)
                            last = pe.matmul(s_ps[i % 2][:, h, 0:width[j]], q[rows, b % 2, P * j:P * j + P],
                                             k[rows, b % 2, cols], start=(n == 0), stop=(n == 2))
                    last.then_inc(s_done, 1)

                def turn(q, p, b):
                    i, hs = turns[q]
                    j = place[i]
                    wait_bank_free(pe, "T", q, p, b)
                    if i in dve_norms:
                        pe.wait_ge(dve_norm_ready, per_item(p, b, 2 * len(dve_norms), 2 * dve_norms.index(i) + hs[-1] + 1))
                    else:
                        pe.wait_ge(norm_ready, per_item(p, b, 2 * len(pool_norms), 2 * pool_norms.index(i) + hs[-1] + 1))
                    n = 0
                    for h in hs:
                        for t in range(width[j] // P):
                            last = pe.transpose(bank_of("T", q)[:, P * n:P * n + P], probs[:, j, h, P * t:P * t + P],
                                                m.ident[:, :])
                            n += 1
                    last.then_inc(t_done, 1)

                def values(g, i, opens):
                    spans = []
                    for t in range(TPB):
                        js = [j for j in (2 * g, 2 * g + 1) if t in [x[0] for x in seen[j]]]
                        if js:
                            spans.append((t, js))
                    todo = [(h, t, js, w, a) for h in range(2) for t, js in spans
                            for w, a in ((v_hi, pT_hi), (v_hi, pT_lo), (v_lo, pT_hi))]
                    both = [x for x in todo if len(x[2]) == 2]
                    todo = both[:1] + [x for x in todo if len(x[2]) == 1] + both[1:]
                    for n, (h, t, js, w, a) in enumerate(todo):
                        c0, c1 = P * (js[0] % 2), P * (js[-1] % 2) + P
                        last = pe.matmul(z_ps[:, 2 * P * g + c0:2 * P * g + c1],
                                         w[:, i, t, h:h + 2, :], a[:, g, h, t, c0:c1],
                                         start=(opens and n == 0), stop=(n == len(todo) - 1),
                                         skip_group_check=True)
                    return last

                def pva(p, b):
                    pe.wait_ge(pT_ready, per_item(p, b, NTURN, t_of[1][-1] + 1))
                    pe.wait_ge(v_ready, per_item(p, b, 1, 1))
                    if isinstance(p, int) and p == 0:
                        pe.wait_ge(zeroed, 4)
                    ge(pe, z_ready, per_item(p, b, 1, 0))
                    values(place[0] // 2, b % 2, True).then_inc(pva_done, 1)

                def pvb(p, b):
                    pe.wait_ge(pT_ready, per_item(p, b, NTURN, 0))
                    values(place[2] // 2, (b - 1) % 2, False).then_inc(pvb_done, 1)

                def out_of(a, p, b):
                    wait_bank_free(pe, "O", a, p, b)
                    if a == 0:
                        pe.wait_ge(z_ready, per_item(p, b, 1, 0))
                        pe.wait_ge(wo_ready, p + (0 if b == 0 else 1))
                    out = bank_of("O", a)
                    n = 0
                    for t in range(2):
                        cols = slice(P * (2 * a + t), P * (2 * a + t) + P)
                        for z, w in ((z_hi, wo_hi), (z_hi, wo_lo), (z_lo, wo_hi)):
                            last = pe.matmul(out[:, D * t:D * t + D], z[:, cols], w[:, :], start=(n == 0),
                                             stop=(n == 5), skip_group_check=True)
                            n += 1
                    last.then_inc(o_done, 1)

                def body(p):
                    for b in range(B):
                        for kind, q in order:
                            if not ran(kind, p, b):
                                continue
                            if kind == "S":
                                scores(q, p, b)
                            elif kind == "PVB":
                                pvb(p, b)
                            elif kind == "PVA":
                                pva(p, b)
                            elif kind == "Q":
                                q_of(p, b)
                            elif kind == "K":
                                k_of(p, b)
                            elif kind == "VT":
                                vt_of(p, b)
                            elif kind == "VR":
                                vr_of(p, b)
                            elif kind == "T":
                                turn(q, p, b)
                            else:
                                out_of(q, p, b)

                q_of(0, -1), k_of(0, -1), vt_of(0, -1), vr_of(0, -1)
                body(0)
                with pe.Fori(1, NP - 1) as p:
                    body(p)
                body(NP - 1)
                pvb(NP, 0)
                out_of(0, NP, 0)
                out_of(1, NP, 0)



def gates(nc, m, g):
    with ExitStack() as ctx:
        sb = lambda n, s, d: ctx.enter_context(nc.sbuf_tensor(f"gate_{n}", s, d))
        make = ctx.enter_context(cleared_semaphores(nc))
        sem = lambda n: make(f"gate_{n}")
        logit = sb("logit", [P, NT, E], F32)
        names = ("eq", "cand", "first", "rest", "eq2", "cand2", "second", "g1", "g2")
        v = {n: sb(n, [P, NT, E], F32) for n in names}
        c = {n: sb(n, [P, NT], F32) for n in ("m1", "i1", "m2", "i2", "gap", "ex", "one_ex", "p1", "p2")}
        down = sb("down", [P, E], F32)
        rows_ps = ctx.enter_context(nc.psum_tensor("gate_rows", [P, BANK], F32))
        iota_ready, dve_step = sem("iota_ready"), sem("dve_step")
        rows_turned, rows_read = sem("rows_turned"), sem("rows_read")
        gap_ready, ex_ready, comb_ready = sem("gap_ready"), sem("ex_ready"), sem("comb_ready")

        with nc.Block() as block:
            @block.gpsimd
            def _(pool):
                pool.iota(down[:, :], pattern=[[-1, E]], base=E, channel_multiplier=0,
                          allow_small_or_imprecise_dtypes=True).then_inc(iota_ready, 1)

            @block.scalar
            def _(act):
                load_table(act, m, ACT.Exp)
                act.wait_ge(rows_turned, 1)
                act.activation(g.columns[:, :], rows_ps[:, 0:g.rows.shape[0]], ACT.Copy).then_inc(rows_read, 1)
                act.wait_ge(gap_ready, 1)
                act.activation(c["ex"][:, :], c["gap"][:, :], ACT.Exp).then_inc(ex_ready, 1)
                load_table(act, m, ACT.Gelu_apprx_tanh)

            @block.vector
            def _(dve):
                chain = Chain(dve, dve_step)

                def step(instruction):
                    chain.inc(instruction)
                    chain.wait()

                def over_experts(col):
                    return col[:, :].rearrange("p (t a) -> p t a", a=1).to_broadcast([P, NT, E])

                def over_tokens(row):
                    return row[:, :].rearrange("p (a e) -> p a e", a=1).to_broadcast([P, NT, E])

                dve.wait_ge(iota_ready, 1)
                halves = g.logit_ps[:, 0:NT * 2 * E].rearrange("p (t h e) -> p t h e", h=2, e=E)
                step(dve.tensor_tensor(v["g1"][:, :, :], halves[:, :, 0, :], over_experts(g.root_u), ALU.mult))
                step(dve.tensor_tensor(v["g2"][:, :, :], halves[:, :, 1, :], over_experts(g.root_u), ALU.mult))
                step(dve.tensor_tensor(logit[:, :, :], v["g1"][:, :, :], v["g2"][:, :, :], ALU.add))
                step(dve.tensor_reduce(c["m1"][:, :], logit[:, :, :], AX.X, ALU.max))
                step(dve.tensor_tensor(v["eq"][:, :, :], logit[:, :, :], over_experts(c["m1"]), ALU.is_equal))
                step(dve.tensor_tensor(v["cand"][:, :, :], v["eq"][:, :, :], over_tokens(down), ALU.mult))
                step(dve.tensor_reduce(c["i1"][:, :], v["cand"][:, :, :], AX.X, ALU.max))
                step(dve.tensor_tensor(v["first"][:, :, :], v["cand"][:, :, :], over_experts(c["i1"]), ALU.is_equal))
                step(dve.scalar_tensor_tensor(v["rest"][:, :, :], v["first"][:, :, :], -3.0e38, logit[:, :, :],
                                              ALU.mult, ALU.add))
                step(dve.tensor_reduce(c["m2"][:, :], v["rest"][:, :, :], AX.X, ALU.max))
                step(dve.tensor_tensor(v["eq2"][:, :, :], v["rest"][:, :, :], over_experts(c["m2"]), ALU.is_equal))
                step(dve.tensor_tensor(v["cand2"][:, :, :], v["eq2"][:, :, :], over_tokens(down), ALU.mult))
                step(dve.tensor_reduce(c["i2"][:, :], v["cand2"][:, :, :], AX.X, ALU.max))
                step(dve.tensor_tensor(v["second"][:, :, :], v["cand2"][:, :, :], over_experts(c["i2"]), ALU.is_equal))
                dve.tensor_tensor(c["gap"][:, :], c["m2"][:, :], c["m1"][:, :], ALU.subtract).then_inc(gap_ready, 1)
                dve.wait_ge(ex_ready, 1)
                step(dve.tensor_scalar(c["one_ex"][:, :], c["ex"][:, :], 1.0, None, ALU.add))
                step(dve.reciprocal(c["p1"][:, :], c["one_ex"][:, :]))
                step(dve.tensor_tensor(c["p2"][:, :], c["ex"][:, :], c["p1"][:, :], ALU.mult))
                step(dve.tensor_tensor(v["g1"][:, :, :], v["first"][:, :, :], over_experts(c["p1"]), ALU.mult))
                step(dve.tensor_tensor(v["g2"][:, :, :], v["second"][:, :, :], over_experts(c["p2"]), ALU.mult))
                step(dve.tensor_tensor(v["cand"][:, :, :], v["g1"][:, :, :], v["g2"][:, :, :], ALU.add))
                dve.tensor_tensor(g.comb[:, :, :], v["cand"][:, :, :], over_tokens(g.alpha), ALU.mult).then_inc(comb_ready, 1)
                dve.wait_ge(comb_ready, 1)
                dve.tensor_copy(g.comb_e[:, :, :].rearrange("p e t -> p t e"), g.comb[:, :, :])

            @block.tensor
            def _(pe):
                pe.wait_ge(g.rows_loaded, 48)
                nr = g.rows.shape[0]
                pe.transpose(rows_ps[:, 0:nr], g.rows[:, :], m.ident[0:nr, 0:nr]).then_inc(rows_turned, 1)


def experts(nc, m, g, tT, w1_dram, w2_dram, b2_dram):
    STEPS = B * NF
    RING = 4
    LASTB = (B - 1) * NF
    with ExitStack() as ctx:
        sb = lambda n, s, d: ctx.enter_context(nc.sbuf_tensor(f"ex_{n}", s, d))
        make = ctx.enter_context(cleared_semaphores(nc))
        sem = lambda n: make(f"ex_{n}")
        w1_stage, w2_stage = g.w1_stage, g.w2_stage
        w1_hi, w1_lo = sb("w1_hi", [P, KD, F], F32R), sb("w1_lo", [P, KD, F], F32R)
        w2_hi, w2_lo = sb("w2_hi", [P, NF, D], F32R), sb("w2_lo", [P, NF, D], F32R)
        lnw, lnb, b1 = sb("lnw", [P, KD], F32), sb("lnb", [P, KD], F32), sb("b1", [P, NF], F32)
        comb = sb("comb", [P, NT], F32)
        a_sb = sb("a", [P, RING, S], F32)
        a_hi, a_lo = sb("a_hi", [P, RING, S], F32R), sb("a_lo", [P, RING, S], F32R)
        h_ps = [ctx.enter_context(nc.psum_tensor(f"ex_h{i}", [P, BANK], F32)) for i in range(2)]
        y_ps = [ctx.enter_context(nc.psum_tensor(f"ex_y{i}", [P, TPB, D], F32)) for i in range(2)]
        scaled, gated_b2 = sb("scaled", [P, 2, S], F32), sb("gated_b2", [P, D], F32)

        w1_loaded, w2_loaded = g.w1_loaded, g.w2_loaded
        dve_step = sem("dve_step")
        small_ready, w1_hi_ready, w1_ready, w2_hi_ready, w2_ready = \
            sem("small_ready"), sem("w1_hi_ready"), sem("w1_ready"), sem("w2_hi_ready"), sem("w2_ready")
        b1_ready, comb_ready, bias_step, bias_added = sem("b1_ready"), sem("comb_ready"), sem("bias_step"), sem("bias_added")
        scaled_ready, t_hi_ready, t_ready = sem("scaled_ready"), sem("t_hi_ready"), sem("t_ready")
        h_done, a_ready, a_hi_ready, a_lo_ready, y_done, x_added = \
            sem("h_done"), sem("a_ready"), sem("a_hi_ready"), sem("a_lo_ready"), sem("y_done"), sem("x_added")

        def at(e, n, c):
            return e * n + c

        def is_last(e):
            return isinstance(e, int) and e == E - 1

        def is_first(e):
            return isinstance(e, int) and e == 0

        with nc.Block() as block:
            @block.sync
            def _(sp):
                w1_view = w1_dram.rearrange("e (k d) f -> e d k f", k=KD)
                w2_view = w2_dram.rearrange("e (f p) d -> e p f d", p=P)

                b2_view = b2_dram.rearrange("(e a) d -> e a d", a=1)

                with sp.Fori(1, E) as e:
                    sp.wait_ge(w1_ready, at(e, NF, 0))
                    sp.dma_start(w1_stage[:, :, :], w1_view[e]).then_inc(w1_loaded, 16)
                    sp.wait_ge(w2_ready, at(e, NF, 0))
                    sp.dma_start(w2_stage[:, :, :], w2_view[e]).then_inc(w2_loaded, 16)
                    sp.wait_ge(bias_added, at(e, NT, 0))
                    sp.dma_start(g.b2_row[:, :], b2_view[e].to_broadcast([P, D])).then_inc(g.b2_loaded, 16)

            @block.gpsimd
            def _(pool):
                def split_w2(e, f):
                    if f == 0:
                        pool.wait_ge(w2_loaded, at(e, 16, 16))
                    if not is_first(e):
                        pool.wait_ge(y_done, at(e, STEPS, LASTB - STEPS + f + 1))
                    one = m.one[:, 0:1].to_broadcast([P, D])
                    pool.tensor_tensor(w2_hi[:, f, :], w2_stage[:, f, :], one, ALU.mult).then_inc(w2_hi_ready, 1)
                    pool.wait_ge(w2_hi_ready, at(e, NF, f + 1))
                    pool.tensor_tensor(w2_lo[:, f, :], w2_stage[:, f, :], as_f32(w2_hi[:, f, :]),
                                       ALU.subtract).then_inc(w2_ready, 1)

                def add_b2(e):
                    pool.wait_ge(g.b2_loaded, at(e, 16, 16))
                    pool.wait_ge(comb_ready, at(e, 1, 1))
                    for t in range(NT):
                        if not is_first(e) and t % TPB == 0:
                            pool.wait_ge(x_added, at(e, NT, t + TPB - NT))
                        if not (is_first(e) and t == 0):
                            pool.wait_ge(bias_added, at(e, NT, t))
                        pool.tensor_tensor(gated_b2[:, :], g.b2_row[:, :], comb[:, t:t + 1].to_broadcast([P, D]), ALU.mult) \
                            .then_inc(bias_step, 1)
                        pool.wait_ge(bias_step, at(e, NT, t + 1))
                        pool.tensor_tensor(m.x[:, t, :], m.x[:, t, :], gated_b2[:, :], ALU.add).then_inc(bias_added, 1)

                for f in range(NF):
                    split_w2(0, f)
                add_b2(0)
                with pool.Fori(1, E) as e:
                    for f in range(NF):
                        split_w2(e, f)
                    add_b2(e)

            @block.scalar
            def _(act):
                def body(e):
                    for s in range(STEPS):
                        if s == 0:
                            act.wait_ge(b1_ready, at(e, 1, 1))
                        act.wait_ge(h_done, at(e, STEPS, s + 1))
                        if not (is_first(e) and s < RING):
                            act.wait_ge(a_lo_ready, at(e, STEPS, s - RING + 1))
                        act.activation(a_sb[:, s % RING, :], h_ps[s % 2][:, :], ACT.Gelu_apprx_tanh,
                                       bias=b1[:, s % NF:s % NF + 1]).then_inc(a_ready, 1)

                body(0)
                with act.Fori(1, E - 1) as e:
                    body(e)
                body(E - 1)
                load_table(act, m, ACT.Sqrt)

            @block.vector
            def _(dve):
                chain = Chain(dve, dve_step)

                def statistics_of(b):
                    dve.wait_ge(x_added, (E - 1) * NT + TPB * (b + 1))
                    batch_statistics(dve, chain, m, b)

                def small(e):
                    dve.tensor_scalar(lnw[:, :], g.lnw[:, bass.ds(e * KD, KD)], 1.0, None, ALU.mult).then_inc(small_ready, 1)
                    dve.tensor_scalar(lnb[:, :], g.lnb[:, bass.ds(e * KD, KD)], 1.0, None, ALU.mult).then_inc(small_ready, 1)

                def split_w1(e, f):
                    if f == 0:
                        dve.wait_ge(w1_loaded, at(e, 16, 16))
                    if not is_first(e):
                        dve.wait_ge(h_done, at(e, STEPS, LASTB - STEPS + f + 1))
                    cols = slice(P * f, P * f + P)
                    dve.tensor_copy(w1_hi[:, :, cols], w1_stage[:, :, cols]).then_inc(w1_hi_ready, 1)
                    dve.wait_ge(w1_hi_ready, at(e, NF, f + 1))
                    dve.tensor_tensor(w1_lo[:, :, cols], w1_stage[:, :, cols], as_f32(w1_hi[:, :, cols]),
                                      ALU.subtract).then_inc(w1_ready, 1)

                def scale_t(e, b, k):
                    n = KD * b + k
                    cols = slice(S * b, S * b + S)
                    if k == 0:
                        dve.wait_ge(small_ready, at(e, 2, 2))
                        if not is_first(e):
                            dve.wait_ge(h_done, at(e, STEPS, (b + 1) * NF - STEPS))
                    dve.tensor_scalar(scaled[:, k, :], tT[:, k, cols], lnw[:, k:k + 1], lnb[:, k:k + 1],
                                      ALU.mult, ALU.add).then_inc(scaled_ready, 1)
                    dve.wait_ge(scaled_ready, at(e, KD * B, n + 1))
                    dve.tensor_copy(m.uT_hi[:, k, cols], scaled[:, k, :]).then_inc(t_hi_ready, 1)
                    dve.wait_ge(t_hi_ready, at(e, KD * B, n + 1))
                    dve.tensor_tensor(m.uT_lo[:, k, cols], scaled[:, k, :], as_f32(m.uT_hi[:, k, cols]),
                                      ALU.subtract).then_inc(t_ready, 1)

                def scale_at(e, s):
                    if is_first(e) and 0 <= s < 2 * KD:
                        scale_t(0, 1 + s // KD, s % KD)
                    elif s in (4, 6):
                        scale_t(e, B - 1, (s - 4) // 2)
                    elif s > NF and s % NF in (2, 4) and not is_last(e):
                        scale_t(e + 1, s // NF - 1, (s % NF - 2) // 2)

                def bias(e):
                    if not is_first(e):
                        dve.wait_ge(a_ready, at(e, STEPS, 0))
                    dve.tensor_scalar(b1[:, :], g.fc1b[:, bass.ds(e * NF, NF)], 1.0, None, ALU.mult).then_inc(b1_ready, 1)

                def halves(e, s):
                    dve.wait_ge(a_ready, at(e, STEPS, s + 1))
                    dve.tensor_copy(a_hi[:, s % RING, :], a_sb[:, s % RING, :]).then_inc(a_hi_ready, 1)
                    dve.wait_ge(a_hi_ready, at(e, STEPS, s + 1))
                    dve.tensor_tensor(a_lo[:, s % RING, :], a_sb[:, s % RING, :], as_f32(a_hi[:, s % RING, :]),
                                      ALU.subtract).then_inc(a_lo_ready, 1)

                def add_y(e, b):
                    dve.wait_ge(y_done, at(e, STEPS, (b + 1) * NF))
                    dve.wait_ge(comb_ready, at(e, 1, 1 if b >= 0 else 0))
                    dve.wait_ge(bias_added, at(e, NT, TPB * (b + 1)))
                    for t in range(TPB):
                        tile = m.x[:, TPB * (b % B) + t, :]
                        dve.scalar_tensor_tensor(tile, y_ps[b % 2][:, t, :], comb[:, TPB * (b % B) + t:TPB * (b % B) + t + 1],
                                                 tile, ALU.mult, ALU.add).then_inc(x_added, 1)

                def body(e):
                    for s in range(STEPS):
                        halves(e, s)
                        scale_at(e, s)
                        if s >= LASTB and not is_last(e):
                            split_w1(e + 1, s - LASTB)
                        if s % NF == 1 and not (is_first(e) and s == 1):
                            add_y(e, s // NF - 1)
                        if is_last(e) and s % NF == 4 and s > NF:
                            statistics_of(s // NF - 1)
                        if s == 1:
                            if not is_first(e):
                                dve.wait_ge(x_added, at(e, NT, 0))
                            dve.tensor_scalar(comb[:, :], g.comb_e[:, bass.ds(e, 1), :].rearrange("p a t -> p (a t)"),
                                              1.0, None, ALU.mult).then_inc(comb_ready, 1)
                        if s == NF and not is_last(e):
                            dve.wait_ge(t_ready, at(e, KD * B, KD * B))
                            small(e + 1)
                    if not is_last(e):
                        bias(e + 1)

                small(0)
                scale_t(0, 0, 0)
                scale_t(0, 0, 1)
                bias(0)
                for f in range(NF):
                    split_w1(0, f)
                body(0)
                with dve.Fori(1, E - 1) as e:
                    body(e)
                body(E - 1)
                add_y(E, -1)
                statistics_of(B - 1)
                chain.wait()

            @block.tensor
            def _(pe):
                def hidden(e, s):
                    b, f = s // NF, s % NF
                    if b == 0:
                        pe.wait_ge(w1_ready, at(e, NF, f + 1))
                    if f == 0:
                        pe.wait_ge(t_ready, at(e, KD * B, KD * (b + 1)))
                    if not (is_first(e) and s < 2):
                        pe.wait_ge(a_ready, at(e, STEPS, s - 1))
                    cols = slice(S * b, S * b + S)
                    n = 0
                    for k in range(KD):
                        for w, t in ((w1_hi, m.uT_hi), (w1_hi, m.uT_lo), (w1_lo, m.uT_hi)):
                            last = pe.matmul(h_ps[s % 2][:, :], w[:, k, P * f:P * f + P], t[:, k, cols],
                                             start=(n == 0), stop=(n == 5))
                            n += 1
                    last.then_inc(h_done, 1)

                def output(e, s):
                    b, f = s // NF, s % NF
                    pe.wait_ge(a_lo_ready, at(e, STEPS, s + 1))
                    if b == 0:
                        pe.wait_ge(w2_ready, at(e, NF, f + 1))
                    if f == 0 and not (is_first(e) and b < 2):
                        pe.wait_ge(x_added, at(e, NT, TPB * (b - 1)))
                    for t in range(TPB):
                        cols = slice(P * t, P * t + P)
                        for n, (a, w) in enumerate(((a_hi, w2_hi), (a_hi, w2_lo), (a_lo, w2_hi))):
                            last = pe.matmul(y_ps[b % 2][:, t, :], a[:, s % RING, cols], w[:, f, :],
                                             start=(f == 0 and n == 0 and t % 2 == 0),
                                             stop=(f == NF - 1 and n == 2), skip_group_check=True)
                    last.then_inc(y_done, 1)

                def body(e):
                    for s in range(STEPS):
                        if s + 2 < STEPS:
                            hidden(e, s + 2)
                        elif not is_last(e):
                            hidden(e + 1, s + 2 - STEPS)
                        output(e, s)

                hidden(0, 0)
                hidden(0, 1)
                body(0)
                with pe.Fori(1, E - 1) as e:
                    body(e)
                body(E - 1)


def adapters(nc, m, uT, w, out_dram):
    N, HD = E, DH
    NC = N * HD // P
    with ExitStack() as ctx:
        sb = lambda n, s, d: ctx.enter_context(nc.sbuf_tensor(f"ad_{n}", s, d))
        make = ctx.enter_context(cleared_semaphores(nc))
        sem = lambda n: make(f"ad_{n}")
        raw = {"base": w.base, "enc": w.enc, "dec": w.dec}
        down, up = w.down, w.up
        hi = {n: sb(n + "_hi", list(t.shape), F32R) for n, t in raw.items()}
        lo = {n: sb(n + "_lo", list(t.shape), F32R) for n, t in raw.items()}
        vec_rows, b_down_rows = w.vec_rows, w.b_down_rows
        vec = sb("vec", [P, 2 * N + NC], F32)
        b_dec, b_enc = vec[:, 0:2 * N], vec[:, 2 * N:2 * N + NC]
        b_down = sb("b_down", [HD, N], F32)
        index = w.index
        bias_hi, bias_lo = sb("bias_hi", [N + 1, D], F32R), sb("bias_lo", [N + 1, D], F32R)
        pick_row = sb("pick_row", [P, N + 1], F32)
        pick = sb("pick", [N + 1, P], F32R)
        index_f, falling, rising = sb("index_f", [P, N], F32), sb("falling", [P, N], F32), sb("rising", [P, N], F32)
        h32 = sb("h32", [P, 2, S], F32)
        h_hi, h_lo = sb("h_hi", [P, NC, S], F32R), sb("h_lo", [P, NC, S], F32R)
        diff, square = sb("diff", [P, 2, S], F32), sb("square", [P, S], F32)
        loss = sb("loss", [P, 2 * N], F32)
        names = ("sum8", "eq", "cand", "best", "pick", "chosen")
        v = {n: sb("v_" + n, [P, N], F32) for n in names}
        c = {n: sb("c_" + n, [P, 1], F32) for n in ("low", "first", "adapter", "negative", "wrapped", "least", "most")}
        sel_down, sel_up = sb("sel_down", [P, KD, HD], F32), sb("sel_up", [HD, D], F32)
        sd_hi, sd_lo = sb("sd_hi", [P, KD, HD], F32R), sb("sd_lo", [P, KD, HD], F32R)
        su_hi, su_lo = sb("su_hi", [HD, D], F32R), sb("su_lo", [HD, D], F32R)
        term, sel_bd, bd_terms = sb("term", [HD, D], F32), sb("sel_bd", [HD, 1], F32), sb("bd_terms", [HD, N], F32)
        mid, mid_hi, mid_lo = sb("mid", [HD, S], F32), sb("mid_hi", [HD, S], F32R), sb("mid_lo", [HD, S], F32R)
        e_ps = [ctx.enter_context(nc.psum_tensor(f"ad_e{i}", [P, BANK], F32)) for i in range(2)]
        r_ps = [ctx.enter_context(nc.psum_tensor(f"ad_r{i}", [P, BANK], F32)) for i in range(4)]
        o_ps = ctx.enter_context(nc.psum_tensor("ad_o", [P, BANK], F32))
        s_ps = ctx.enter_context(nc.psum_tensor("ad_s", [P, BANK], F32))

        w_loaded, row_loaded, bias_loaded, late_loaded = w.w_loaded, w.row_loaded, w.bias_loaded, w.late_loaded
        iota_ready = sem("iota_ready")
        w_hi_ready, w_ready, rows_turned, vec_ready = sem("w_hi_ready"), sem("w_ready"), sem("rows_turned"), sem("vec_ready")
        enc_done, h32_ready, h_hi_ready, h_ready = sem("enc_done"), sem("h32_ready"), sem("h_hi_ready"), sem("h_ready")
        dec_done, diff_ready, loss_ready, loss_summed = sem("dec_done"), sem("diff_ready"), sem("loss_ready"), sem("loss_summed")
        dve_step, pool_step, chosen_ready, picked = sem("dve_step"), sem("pool_step"), sem("chosen_ready"), sem("picked")
        up_picked = sem("up_picked")
        up_summed, bias_step, bias_ready = sem("up_summed"), sem("bias_step"), sem("bias_ready")
        pick_turned, pick_ready = sem("pick_turned"), sem("pick_ready")
        stored, down_done, mid_ready, mid_split, out_done, x_added = \
            sem("stored"), sem("down_done"), sem("mid_ready"), sem("mid_split"), sem("out_done"), sem("x_added")

        jobs = [(ch, dh, e) for ch in range(NC) for dh in range(KD) for e in range(2)]
        NJ = len(jobs)

        def out_bank(i):
            return r_ps[i][:, :]

        with nc.Block() as block:
            @block.sync
            def _(sp):
                for b in range(B):
                    sp.wait_ge(x_added, 2 * b + 2)
                    sp.dma_start(out_dram[b * S:(b + 1) * S, :].rearrange("(t p) d -> p t d", p=P),
                                 m.x[:, TPB * b:TPB * b + TPB, :]).then_inc(stored, 16)
                sp.wait_ge(stored, 16 * B)

            @block.gpsimd
            def _(pool):
                pool.iota(falling[:, :], pattern=[[-1, N]], base=N, channel_multiplier=0,
                          allow_small_or_imprecise_dtypes=True).then_inc(iota_ready, 1)
                pool.wait_ge(iota_ready, 1)
                pool.iota(rising[:, :], pattern=[[1, N]], base=0, channel_multiplier=0,
                          allow_small_or_imprecise_dtypes=True).then_inc(iota_ready, 1)
                chain = Chain(pool, pool_step)
                pool.wait_ge(iota_ready, 2)
                for b in range(B + 1):
                    if b < B:
                        for ch in range(NC):
                            pool.wait_ge(h32_ready, NC * b + ch + 1)
                            pool.wait_ge(h_hi_ready, NC * b + ch + 1)
                            ge(pool, dec_done, NJ * b)
                            pool.tensor_tensor(h_lo[:, ch, :], h32[:, ch % 2, :], as_f32(h_hi[:, ch, :]),
                                               ALU.subtract).then_inc(h_ready, 1)
                            pool.wait_ge(h_ready, NC * b + ch + 1)
                    if 1 <= b < B:
                        pool.wait_ge(chosen_ready, b)
                        ge(pool, up_picked, b - 1)
                        if b == 1:
                            pool.wait_ge(late_loaded, 48)
                        for n in range(N):
                            pick_n = pick_row[0:HD, n:n + 1].to_broadcast([HD, D])
                            if n == 0:
                                chain.inc(pool.tensor_tensor(sel_up[:, :], up[:, n, :], pick_n, ALU.mult))
                                chain.wait()
                                continue
                            chain.inc(pool.tensor_tensor(term[:, :], up[:, n, :], pick_n, ALU.mult))
                            chain.wait()
                            last = pool.tensor_tensor(sel_up[:, :], sel_up[:, :], term[:, :], ALU.add)
                            if n < N - 1:
                                chain.inc(last)
                                chain.wait()
                            else:
                                last.then_inc(up_summed, 1)
                        pool.wait_ge(up_summed, b)

            @block.scalar
            def _(act):
                def pick_of(b):
                    act.wait_ge(pick_turned, b + 1)
                    ge(act, out_done, 2 * b)
                    act.activation(pick[:, :], s_ps[0:N + 1, 128:256], ACT.Copy).then_inc(pick_ready, 1)

                def middle(b):
                    act.wait_ge(down_done, b + 1)
                    act.wait_ge(picked, b + 1)
                    act.activation(mid[:, :], o_ps[0:HD, :], ACT.Relu, bias=sel_bd[:, 0:1]).then_inc(mid_ready, 1)
                    act.activation(mid_hi[:, :], o_ps[0:HD, :], ACT.Relu, bias=sel_bd[:, 0:1]).then_inc(mid_ready, 1)

                act.wait_ge(vec_ready, 2)
                for b in range(B + 1):
                    if b < B:
                        for ch in range(NC):
                            n = NC * b + ch
                            act.wait_ge(enc_done, n + 1)
                            ge(act, h_ready, n - 1)
                            act.activation(h32[:, ch % 2, :], e_ps[ch % 2][:, :], ACT.Relu, bias=b_enc[:, ch:ch + 1]) \
                                .then_inc(h32_ready, 1)
                            act.activation(h_hi[:, ch, :], e_ps[ch % 2][:, :], ACT.Relu, bias=b_enc[:, ch:ch + 1]) \
                                .then_inc(h_hi_ready, 1)
                        if b >= 1:
                            pick_of(b - 1)
                        for q in range(NJ):
                            ch, dh, e = jobs[q]
                            col = (2 * ch + e) * KD + dh
                            act.wait_ge(diff_ready, NJ * b + q + 1)
                            ge(act, loss_summed, b)
                            ge(act, loss_ready, NJ * b + q)
                            act.activation(square[:, :], diff[:, q % 2, :], ACT.Square,
                                           accum_out=loss[:, col:col + 1]).then_inc(loss_ready, 1)
                    else:
                        pick_of(B - 1)
                    if b >= 1:
                        middle(b - 1)

            @block.vector
            def _(dve):
                chain = Chain(dve, dve_step)

                def step(instruction):
                    chain.inc(instruction)
                    chain.wait()

                dve.wait_ge(w_loaded, 64)
                for i, n in enumerate(("enc", "dec", "base")):
                    dve.tensor_copy(hi[n][:, :, :], raw[n][:, :, :]).then_inc(w_hi_ready, 1)
                    dve.wait_ge(w_hi_ready, i + 1)
                    dve.tensor_tensor(lo[n][:, :, :], raw[n][:, :, :], as_f32(hi[n][:, :, :]),
                                      ALU.subtract).then_inc(w_ready, 1)
                dve.wait_ge(rows_turned, 1)
                dve.tensor_copy(vec[:, :], s_ps[:, 0:2 * N + NC]).then_inc(vec_ready, 1)
                dve.tensor_copy(b_down[:, :], s_ps[0:HD, 64:64 + N]).then_inc(vec_ready, 1)
                dve.wait_ge(vec_ready, 2)
                dve.wait_ge(bias_loaded, 48)
                dve.tensor_copy(bias_hi[:, :], w.bias_rows[:, :]).then_inc(bias_step, 1)
                dve.wait_ge(bias_step, 1)
                dve.tensor_tensor(bias_lo[:, :], w.bias_rows[:, :], as_f32(bias_hi[:, :]), ALU.subtract) \
                    .then_inc(bias_ready, 1)
                step(dve.tensor_scalar(pick_row[:, N:N + 1], m.one[:, 0:1], 1.0, None, ALU.mult))
                dve.wait_ge(iota_ready, 2)
                step(dve.tensor_copy(index_f[:, :], index[:, :]))

                def choose(b):
                    dve.wait_ge(loss_summed, b + 1)
                    step(dve.tensor_reduce(v["sum8"][:, :], s_ps[:, 0:2 * N].rearrange("p (n k) -> p n k", k=KD), AX.X, ALU.add))
                    step(dve.tensor_reduce(c["low"][:, :], v["sum8"][:, :], AX.X, ALU.min))
                    step(dve.tensor_scalar(v["eq"][:, :], v["sum8"][:, :], c["low"][:, 0:1], None, ALU.is_equal))
                    step(dve.tensor_tensor(v["cand"][:, :], v["eq"][:, :], falling[:, :], ALU.mult))
                    step(dve.tensor_reduce(c["first"][:, :], v["cand"][:, :], AX.X, ALU.max))
                    step(dve.tensor_scalar(v["best"][:, :], falling[:, :], c["first"][:, 0:1], None, ALU.is_equal))
                    step(dve.tensor_tensor(v["pick"][:, :], v["best"][:, :], index_f[:, :], ALU.mult))
                    step(dve.tensor_reduce(c["adapter"][:, :], v["pick"][:, :], AX.X, ALU.add))
                    step(dve.tensor_scalar(c["negative"][:, :], c["adapter"][:, :], 0.0, float(N), ALU.is_lt, ALU.mult))
                    step(dve.tensor_tensor(c["wrapped"][:, :], c["adapter"][:, :], c["negative"][:, :], ALU.add))
                    step(dve.tensor_scalar(c["most"][:, :], c["wrapped"][:, :], 0.0, float(N - 1), ALU.max, ALU.min))
                    ge(dve, up_summed, b)
                    ge(dve, pick_turned, b)
                    dve.tensor_scalar(pick_row[:, 0:N], rising[:, :], c["most"][:, 0:1], None, ALU.is_equal) \
                        .then_inc(chosen_ready, 1)
                    dve.wait_ge(chosen_ready, b + 1)
                    chain.inc(dve.tensor_tensor(bd_terms[:, :], b_down[:, :], pick_row[0:HD, 0:N], ALU.mult))

                def add_down(n):
                    if n == 0:
                        chain.inc(dve.tensor_scalar(sel_down[:, :, :], down[:, :, 0, :], pick_row[:, 0:1], None, ALU.mult))
                        return
                    chain.wait()
                    chain.inc(dve.scalar_tensor_tensor(sel_down[:, :, :], down[:, :, n, :], pick_row[:, n:n + 1],
                                                       sel_down[:, :, :], ALU.mult, ALU.add))

                def add_up(n):
                    if n == 0:
                        dve.wait_ge(up_summed, B - 1)
                        chain.inc(dve.tensor_scalar(sel_up[:, :], up[:, 0, :], pick_row[0:HD, 0:1], None, ALU.mult))
                        return
                    chain.wait()
                    chain.inc(dve.scalar_tensor_tensor(sel_up[:, :], up[:, n, :], pick_row[0:HD, n:n + 1],
                                                       sel_up[:, :], ALU.mult, ALU.add))

                def halves_down(b):
                    chain.wait()
                    ge(dve, down_done, b)
                    ge(dve, mid_ready, 2 * b)
                    chain.inc(dve.tensor_reduce(sel_bd[:, :], bd_terms[:, :], AX.X, ALU.add))
                    chain.inc(dve.tensor_copy(sd_hi[:, :, :], sel_down[:, :, :]))
                    chain.wait()
                    dve.tensor_tensor(sd_lo[:, :, :], sel_down[:, :, :], as_f32(sd_hi[:, :, :]), ALU.subtract) \
                        .then_inc(picked, 1)

                def halves_up(b):
                    ge(dve, out_done, 2 * b)
                    if b < B - 1:
                        dve.wait_ge(up_summed, b + 1)
                    else:
                        chain.wait()
                    chain.inc(dve.tensor_copy(su_hi[:, :], sel_up[:, :]))
                    chain.wait()
                    dve.tensor_tensor(su_lo[:, :], sel_up[:, :], as_f32(su_hi[:, :]), ALU.subtract).then_inc(up_picked, 1)

                EARLY = 3
                for b in range(B + 1):
                    if b >= 1:
                        choose(b - 1)
                        if b == 1:
                            dve.wait_ge(late_loaded, 48)
                        for n in range(EARLY):
                            add_down(n)
                    for q in range(NJ):
                        if b < B:
                            ch, dh, e = jobs[q]
                            col = (2 * ch + e) * KD + dh
                            dve.wait_ge(dec_done, NJ * b + q + 1)
                            ge(dve, loss_ready, NJ * b + q - 1)
                            dve.scalar_tensor_tensor(diff[:, q % 2, :], r_ps[q % 4][:, :], b_dec[:, col:col + 1],
                                                     uT[:, dh, S * b:S * b + S], ALU.add, ALU.subtract) \
                                .then_inc(diff_ready, 1)
                        if b >= 1:
                            if q % 2 == 1 and q // 2 < N - EARLY:
                                add_down(EARLY + q // 2)
                            if q == 2 * (N - EARLY) + 1:
                                halves_down(b - 1)
                                if b == B:
                                    for n in range(N):
                                        add_up(n)
                            if q == NJ - 1:
                                halves_up(b - 1)
                    if b >= 1:
                        dve.wait_ge(mid_ready, 2 * b)
                        dve.tensor_tensor(mid_lo[:, :], mid[:, :], as_f32(mid_hi[:, :]), ALU.subtract).then_inc(mid_split, 1)
                        for i in range(2):
                            dve.wait_ge(out_done, 2 * (b - 1) + i + 1)
                            t = TPB * (b - 1) + 2 * i
                            rows = m.x[:, t:t + 2, :]
                            dve.tensor_tensor(rows, rows, out_bank(i).rearrange("p (t d) -> p t d", t=2),
                                              ALU.add).then_inc(x_added, 1)

            @block.tensor
            def _(pe):
                pe.wait_ge(row_loaded, 48)
                nr = 2 * N + NC
                pe.transpose(s_ps[:, 0:nr], vec_rows[:, :], m.ident[0:nr, 0:nr])
                pe.transpose(s_ps[0:HD, 64:64 + N], b_down_rows[:, :], m.ident[0:N, 0:N]).then_inc(rows_turned, 1)

                def three(out, w_hi, w_lo, b_hi, b_lo, first, last_, **more):
                    pe.matmul(out, w_hi, b_hi, start=first, stop=False, **more)
                    pe.matmul(out, w_hi, b_lo, start=False, stop=False, **more)
                    return pe.matmul(out, w_lo, b_hi, start=False, stop=last_, **more)

                def sum_losses(b):
                    pe.wait_ge(loss_ready, NJ * (b + 1))
                    pe.wait_ge(vec_ready, 2)
                    ge(pe, chosen_ready, b)
                    pe.matmul(s_ps[:, 0:2 * N], m.one[:, :], loss[:, :], start=True, stop=True).then_inc(loss_summed, 1)

                def turn_pick(b):
                    pe.wait_ge(chosen_ready, b + 1)
                    pe.transpose(s_ps[0:N + 1, 128:256], pick_row[:, :], m.ident[:, :]).then_inc(pick_turned, 1)

                for b in range(B + 1):
                    if b < B:
                        cols = slice(S * b, S * b + S)
                        for ch in range(NC):
                            if b == 0 and ch == 0:
                                pe.wait_ge(w_ready, 1)
                            ge(pe, h_hi_ready, NC * b + ch - 1)
                            for k in range(KD):
                                f = slice(P * ch, P * ch + P)
                                last = three(e_ps[ch % 2][:, :], hi["enc"][:, k, f], lo["enc"][:, k, f],
                                             m.uT_hi[:, k, cols], m.uT_lo[:, k, cols], k == 0, k == KD - 1)
                            last.then_inc(enc_done, 1)
                            if b >= 1 and ch == 0:
                                sum_losses(b - 1)
                        for q in range(0, NJ, 2):
                            ch, dh, _ = jobs[q]
                            if b >= 1 and q == 2:
                                turn_pick(b - 1)
                            if b == 0 and q == 0:
                                pe.wait_ge(w_ready, 2)
                            pe.wait_ge(h_ready, NC * b + ch + 1)
                            ge(pe, diff_ready, NJ * b + q - 2)
                            if b >= 2 and q == 0:
                                pe.wait_ge(x_added, 2 * (b - 1))
                            d = slice(P * dh, P * dh + P)
                            for n, (half, h) in enumerate(((hi, h_hi), (hi, h_lo), (lo, h_hi))):
                                for e in range(2):
                                    rows = slice(HD * e, HD * e + HD)
                                    last = pe.matmul(r_ps[(q + e) % 4][:, :], half["dec"][rows, ch, d], h[rows, ch, :],
                                                     start=(n == 0), stop=(n == 2))
                                    if n == 2:
                                        last.then_inc(dec_done, 1)
                    else:
                        sum_losses(B - 1)
                    if b >= 1:
                        cols = slice(S * (b - 1), S * b)
                        if b == 1:
                            pe.wait_ge(w_ready, 3)
                        for i in range(2):
                            pe.wait_ge(diff_ready, NJ * min(b + 1, B) - 2 + i)
                            if b == B:
                                pe.wait_ge(x_added, 2 * (B - 1))
                            for j in range(2):
                                t = slice(S * (b - 1) + P * (2 * i + j), S * (b - 1) + P * (2 * i + j) + P)
                                for k in range(KD):
                                    three(out_bank(i)[:, D * j:D * j + D], m.uT_hi[:, k, t], m.uT_lo[:, k, t],
                                          hi["base"][:, k, :], lo["base"][:, k, :], j == 0 and k == 0, False,
                                          skip_group_check=True)
                            if i == 0 and b == B:
                                turn_pick(B - 1)
                            if i == 0:
                                pe.wait_ge(picked, b)
                                ge(pe, mid_ready, 2 * (b - 1))
                                for k in range(KD):
                                    last = three(o_ps[0:HD, :], sd_hi[:, k, :], sd_lo[:, k, :],
                                                 m.uT_hi[:, k, cols], m.uT_lo[:, k, cols], k == 0, k == KD - 1)
                                last.then_inc(down_done, 1)
                        for i in range(2):
                            if i == 0:
                                pe.wait_ge(pick_ready, b)
                                if b == 1:
                                    pe.wait_ge(bias_ready, 1)
                            for j in range(2):
                                for half in (bias_hi, bias_lo):
                                    pe.matmul(out_bank(i)[:, D * j:D * j + D], pick[:, :], half[:, :], start=False,
                                              stop=False, skip_group_check=True)
                        for i in range(2):
                            if i == 0:
                                pe.wait_ge(mid_split, b)
                                pe.wait_ge(up_picked, b)
                            for j in range(2):
                                t = slice(P * (2 * i + j), P * (2 * i + j) + P)
                                last = three(out_bank(i)[:, D * j:D * j + D], mid_hi[:, t], mid_lo[:, t],
                                             su_hi[:, :], su_lo[:, :], False, True, skip_group_check=True)
                            last.then_inc(out_done, 1)


def causal(j):
    return [(t, UP if t == j else None) for t in range(j + 1)]


def banded(j):
    return [(t, {-1: LOW, 0: None, 1: UP}[t - j]) for t in range(max(0, j - 1), min(TPB, j + 2))]


def program(nc, a, out):
    x_dram = a["x"].rearrange("b s d -> (b s) d")
    ctx_dram = a["ctx_1024"].rearrange("b s d -> (b s) d")
    out_dram = out.rearrange("b s d -> (b s) d")
    with ExitStack() as ctx:
        sb = lambda n, s, d: ctx.enter_context(nc.sbuf_tensor(n, s, d))
        m = Shared(sb)

        def head_major(w):
            view = w.rearrange("(p h) (k d) e -> p h d k e", h=2, k=KD)
            return lambda dst, p: [(dst[:, :, DH * h:DH * h + DH], view[p, h]) for h in range(2)]

        def column_major(w):
            view = w.rearrange("(k d) (p n) -> p d k n", k=KD, n=P)
            return lambda dst, p: [(dst, view[p])]

        def head_bias(w):
            view = w.rearrange("(p h) (e a) -> p (h e) a", h=2, a=1)
            return lambda p: view[p]

        wo0 = a["L0_xattn_W_O"].rearrange("(p h) e d -> p (h e) d", h=2)
        wo1 = a["L1_xattn_Wo"].rearrange("(p n) d -> p n d", n=P)
        with ExitStack() as inner:
            inner_sb = lambda n, shape, dtype: inner.enter_context(nc.sbuf_tensor(n, shape, dtype))
            sem = inner.enter_context(cleared_semaphores(nc))
            weights = PairWeights(inner_sb, sem, "att0", head_major(a["L0_xattn_W_Q"]), head_major(a["L0_xattn_W_K"]),
                                  head_major(a["L0_xattn_W_V"]), lambda p: wo0[p],
                                  [head_bias(a["L0_xattn_" + n]) for n in ("b_Q", "b_K", "b_V")])
            bo, bo_loaded = inner_sb("bo", [P, D], F32), sem("bo_loaded")

            def prefetch(sp):
                weights.load(sp, 0)
                sp.dma_start(bo[:, :], a["L0_xattn_b_O"].rearrange("(a n) -> a n", a=1).to_broadcast([P, D])) \
                    .then_inc(bo_loaded, 16)
                sp.wait_ge(bo_loaded, 16)

            norm_inputs(nc, m, "in0", prefetch, x_dram, ctx_dram)
            attention(nc, m, "att0", weights, causal, bo)
        with ExitStack() as inner:
            g = Experts(lambda n, shape, dtype: inner.enter_context(nc.sbuf_tensor(n, shape, dtype)),
                        lambda n, shape, dtype: inner.enter_context(nc.psum_tensor(n, shape, dtype)),
                        inner.enter_context(cleared_semaphores(nc)))
            tT = inner.enter_context(nc.sbuf_tensor("tT", [P, KD, TOK], F32))
            norm_inputs(nc, m, "in_e", lambda sp: g.load(sp, a), uT32=tT, experts=g)
            gates(nc, m, g)
            experts(nc, m, g, tT, a["L0_ffn_fc1_w"], a["L0_ffn_fc2_w"], a["L0_ffn_fc2_b"])
        with ExitStack() as inner:
            weights = PairWeights(lambda n, shape, dtype: inner.enter_context(nc.sbuf_tensor(n, shape, dtype)),
                                  inner.enter_context(cleared_semaphores(nc)), "att1", column_major(a["L1_xattn_Wq"]),
                                  column_major(a["L1_xattn_Wk"]), column_major(a["L1_xattn_Wv"]), lambda p: wo1[p])
            norm_inputs(nc, m, "in1", lambda sp: weights.load(sp, 0))
            attention(nc, m, "att1", weights, banded)
        with ExitStack() as inner:
            uT32 = inner.enter_context(nc.sbuf_tensor("uT32", [P, KD, TOK], F32))
            w = Adapters(lambda n, shape, dtype: inner.enter_context(nc.sbuf_tensor(n, shape, dtype)),
                         inner.enter_context(cleared_semaphores(nc)))
            norm_inputs(nc, m, "in2", lambda sp: w.load(sp, a), uT32=uT32)
            adapters(nc, m, uT32, w, out_dram)


def kernel(**inputs):
    import numpy as _np
    import concourse.bacc as _bacc
    from concourse import mybir as _mybir
    from concourse.bass_utils import run_bass_kernel_spmd as _run

    nc = _bacc.Bacc("TRN2", target_bir_lowering=False, num_devices=1)
    arrays, args = {}, {}
    for name in inputs:
        array = _np.ascontiguousarray(inputs[name])
        arrays[f"in_{name}"] = array
        args[name] = nc.dram_tensor(f"in_{name}", array.shape, _mybir.dt.from_np(array.dtype),
                                    kind="ExternalInput").ap()
    out = nc.dram_tensor("out_0", (4, 512, 256), _mybir.dt.float32, kind="ExternalOutput").ap()
    program(nc, args, out)
    result = _run(nc, [arrays], core_ids=[0])
    return result.results[0]["out_0"]
```
